# Optimizing a Trainium2 kernel written in Bass

```python
import numpy as np
import jax
import jax.numpy as jnp

def _softmax(x, axis=-1):
    return jax.nn.softmax(x, axis=axis)

def _gelu(x):
    return jax.nn.gelu(x, approximate=True)

def _silu(x):
    return jax.nn.silu(x)

def _sigmoid(x):
    return jax.nn.sigmoid(x)

def _layernorm(x, axis=-1, eps=1e-05):
    m = jnp.mean(x, axis=axis, keepdims=True)
    v = jnp.var(x, axis=axis, keepdims=True)
    return (x - m) / jnp.sqrt(v + eps)

def _scatter_add(tgt, idx, src, axis=0):
    return tgt.at[idx].add(src)

def _segment_sum(src, seg, n):
    return jax.ops.segment_sum(src, seg, n)
kernel_name = 'mk_decoder_postln_d1_seqx_r8_bce781'

def setup_inputs(seed: int=0):
    np.random.seed(seed)
    _w = jnp.asarray

    def _rec_inputs():
        import jax
        import jax.numpy as jnp
        _rk = jax.random.key(seed)
        x = -7.109e-05 + 0.9999 * jax.random.normal(jax.random.fold_in(_rk, 1), (2, 512, 128), jnp.float32)
        _lenS = 512 - jax.random.randint(jax.random.fold_in(_rk, 7), (2,), 0, max(1, 512 // 4) + 1, jnp.int32)
        _lenS2 = 154 - jax.random.randint(jax.random.fold_in(_rk, 8), (2,), 0, max(1, 154 // 4) + 1, jnp.int32)
        _ctx_768P = jax.random.normal(jax.random.fold_in(_rk, 11), (2, 16, 96), jnp.float32)
        _ctx_768c = jax.random.dirichlet(jax.random.fold_in(_rk, 511), 0.3 * jnp.ones((16,), jnp.float32), (2, 154))
        _ctx_768t = jnp.einsum('bsk,bkd->bsd', _ctx_768c, _ctx_768P)
        _ctx_768t = _ctx_768t * jax.lax.rsqrt(jnp.mean(jnp.square(_ctx_768t)) + 1e-12) * 0.953939
        ctx_768 = 0.000486113 + 1.00014 * (_ctx_768t + 0.3 * jax.random.normal(jax.random.fold_in(_rk, 611), (2, 154, 96), jnp.float32))
        return (x, ctx_768)
    x, ctx_768 = _rec_inputs()

    def _L0_attn_setup():
        import jax, jax.numpy as jnp
        import numpy as np
        import math
        N_EMBD = 128
        N_HEAD = 16
        HEAD_DIM = N_EMBD // N_HEAD // 2
        DEPTH = 1
        LAMBDA_INIT = 0.8 - 0.6 * math.exp(-0.3 * (DEPTH - 1))
        EPS = 1e-05
        key = jax.random.key(seed)
        ks = jax.random.split(key, 8)
        B, T, C = (4, 128, N_EMBD)
        x = jax.random.normal(ks[0], (B, T, C), dtype=jnp.float32)
        w_attn = jax.random.normal(ks[1], (C, 3 * C), dtype=jnp.float32) * (1.0 / math.sqrt(C))
        w_proj = jax.random.normal(ks[2], (C, C), dtype=jnp.float32) * (1.0 / math.sqrt(C))
        lambda_q1 = jax.random.normal(ks[3], (HEAD_DIM,), dtype=jnp.float32) * 0.1
        lambda_q2 = jax.random.normal(ks[4], (HEAD_DIM,), dtype=jnp.float32) * 0.1
        lambda_k1 = jax.random.normal(ks[5], (HEAD_DIM,), dtype=jnp.float32) * 0.1
        lambda_k2 = jax.random.normal(ks[6], (HEAD_DIM,), dtype=jnp.float32) * 0.1
        gamma = jnp.ones((2 * HEAD_DIM,), dtype=jnp.float32)
        return {'x': x, 'w_attn': w_attn, 'w_proj': w_proj, 'lambda_q1': lambda_q1, 'lambda_q2': lambda_q2, 'lambda_k1': lambda_k1, 'lambda_k2': lambda_k2, 'gamma': gamma}
    _L0_attn_all = _L0_attn_setup()
    _L0_attn_in = {k: v for k, v in _L0_attn_all.items() if k in ('w_attn', 'w_proj', 'lambda_q1', 'lambda_q2', 'lambda_k1', 'lambda_k2', 'gamma')}
    del _L0_attn_all

    def _L0_xattn_setup():
        import jax, jax.numpy as jnp
        import numpy as np
        HEADS = 16
        DIM_HEAD = 64
        key = jax.random.key(seed)
        ks = jax.random.split(key, 8)
        B, S, D = (16, 512, 128)
        K, DE = (77, 96)
        inner = HEADS * DIM_HEAD
        hidden_states = jax.random.normal(ks[0], (B, S, D), dtype=jnp.float32)
        encoder_hidden_states = jax.random.normal(ks[1], (B, K, DE), dtype=jnp.float32)
        sc_q = 1.0 / np.sqrt(D)
        sc_kv = 1.0 / np.sqrt(DE)
        sc_o = 1.0 / np.sqrt(inner)
        Wq = jax.random.normal(ks[2], (D, inner), dtype=jnp.float32) * sc_q
        Wk = jax.random.normal(ks[3], (DE, inner), dtype=jnp.float32) * sc_kv
        Wv = jax.random.normal(ks[4], (DE, inner), dtype=jnp.float32) * sc_kv
        Wo = jax.random.normal(ks[5], (inner, D), dtype=jnp.float32) * sc_o
        bo = jax.random.normal(ks[6], (D,), dtype=jnp.float32) * 0.01
        return {'hidden_states': hidden_states, 'encoder_hidden_states': encoder_hidden_states, 'Wq': Wq, 'Wk': Wk, 'Wv': Wv, 'Wo': Wo, 'bo': bo}
    _L0_xattn_all = _L0_xattn_setup()
    _L0_xattn_in = {k: v for k, v in _L0_xattn_all.items() if k in ('Wq', 'Wk', 'Wv', 'Wo', 'bo')}
    del _L0_xattn_all

    def _L0_ffn_setup():
        import jax, jax.numpy as jnp
        import numpy as np
        E, K = (8, 2)
        B, S, H, F = (2, 256, 128, 512)
        EPS = 1e-12

        def _expert_ffn(xf, Wi_e, bi_e, Wg_e, bg_e, Wo_e, bo_e, g_e, b_e):
            h = jax.nn.gelu(xf @ Wi_e + bi_e, approximate=False) * jax.nn.sigmoid(xf @ Wg_e + bg_e)
            r = xf + (h @ Wo_e + bo_e)
            mu = jnp.mean(r, axis=-1, keepdims=True)
            var = jnp.mean(jnp.square(r - mu), axis=-1, keepdims=True)
            return (r - mu) * jax.lax.rsqrt(var + EPS) * g_e + b_e
        key = jax.random.key(seed)
        ks = jax.random.split(key, 8)
        s = 0.02
        return {'x': jax.random.normal(ks[0], (B, S, H), jnp.float32), 'Wr': jax.random.normal(ks[1], (H, E), jnp.float32) * s, 'br': jnp.zeros((E,), jnp.float32), 'Wi': jax.random.normal(ks[2], (E, H, F), jnp.float32) * s, 'bi': jnp.zeros((E, F), jnp.float32), 'Wg': jax.random.normal(ks[3], (E, H, F), jnp.float32) * s, 'bg': jnp.zeros((E, F), jnp.float32), 'Wo': jax.random.normal(ks[4], (E, F, H), jnp.float32) * s, 'bo': jnp.zeros((E, H), jnp.float32), 'gamma': jnp.ones((E, H), jnp.float32), 'beta': jnp.zeros((E, H), jnp.float32)}
    _L0_ffn_all = _L0_ffn_setup()
    _L0_ffn_in = {k: v for k, v in _L0_ffn_all.items() if k in ('Wr', 'br', 'Wi', 'bi', 'Wg', 'bg', 'Wo', 'bo', 'gamma', 'beta')}
    del _L0_ffn_all
    return {'x': x, 'ctx_768': ctx_768, 'L0_attn_w_attn': _L0_attn_in['w_attn'], 'L0_attn_w_proj': _L0_attn_in['w_proj'], 'L0_attn_lambda_q1': _L0_attn_in['lambda_q1'], 'L0_attn_lambda_q2': _L0_attn_in['lambda_q2'], 'L0_attn_lambda_k1': _L0_attn_in['lambda_k1'], 'L0_attn_lambda_k2': _L0_attn_in['lambda_k2'], 'L0_attn_gamma': _L0_attn_in['gamma'], 'L0_xattn_Wq': _L0_xattn_in['Wq'], 'L0_xattn_Wk': _L0_xattn_in['Wk'], 'L0_xattn_Wv': _L0_xattn_in['Wv'], 'L0_xattn_Wo': _L0_xattn_in['Wo'], 'L0_xattn_bo': _L0_xattn_in['bo'], 'L0_ffn_Wr': _L0_ffn_in['Wr'], 'L0_ffn_br': _L0_ffn_in['br'], 'L0_ffn_Wi': _L0_ffn_in['Wi'], 'L0_ffn_bi': _L0_ffn_in['bi'], 'L0_ffn_Wg': _L0_ffn_in['Wg'], 'L0_ffn_bg': _L0_ffn_in['bg'], 'L0_ffn_Wo': _L0_ffn_in['Wo'], 'L0_ffn_bo': _L0_ffn_in['bo'], 'L0_ffn_gamma': _L0_ffn_in['gamma'], 'L0_ffn_beta': _L0_ffn_in['beta']}

def reference(x, ctx_768, L0_attn_w_attn, L0_attn_w_proj, L0_attn_lambda_q1, L0_attn_lambda_q2, L0_attn_lambda_k1, L0_attn_lambda_k2, L0_attn_gamma, L0_xattn_Wq, L0_xattn_Wk, L0_xattn_Wv, L0_xattn_Wo, L0_xattn_bo, L0_ffn_Wr, L0_ffn_br, L0_ffn_Wi, L0_ffn_bi, L0_ffn_Wg, L0_ffn_bg, L0_ffn_Wo, L0_ffn_bo, L0_ffn_gamma, L0_ffn_beta):
    import jax
    import jax.numpy as jnp

    def _L0_attn_ref(x, w_attn, w_proj, lambda_q1, lambda_q2, lambda_k1, lambda_k2, gamma):
        import jax, jax.numpy as jnp
        import numpy as np
        import math
        N_EMBD = 128
        N_HEAD = 16
        HEAD_DIM = N_EMBD // N_HEAD // 2
        DEPTH = 1
        LAMBDA_INIT = 0.8 - 0.6 * math.exp(-0.3 * (DEPTH - 1))
        EPS = 1e-05
        B, T, C = x.shape
        H, hd = (N_HEAD, HEAD_DIM)
        qkv = x @ w_attn
        q, k, v = jnp.split(qkv, 3, axis=-1)
        q = q.reshape(B, T, 2 * H, hd).transpose(0, 2, 1, 3)
        k = k.reshape(B, T, 2 * H, hd).transpose(0, 2, 1, 3)
        v = v.reshape(B, T, H, 2 * hd).transpose(0, 2, 1, 3)
        q = q * hd ** (-0.5)
        att = jnp.einsum('bhtd,bhsd->bhts', q, k) * (1.0 / math.sqrt(hd))
        causal = jnp.tril(jnp.ones((T, T), dtype=bool))
        att = jnp.where(causal, att, -jnp.inf)
        att = jax.nn.softmax(att, axis=-1)
        lam1 = jnp.exp(jnp.sum(lambda_q1 * lambda_k1))
        lam2 = jnp.exp(jnp.sum(lambda_q2 * lambda_k2))
        lambda_full = lam1 - lam2 + LAMBDA_INIT
        att = att.reshape(B, H, 2, T, T)
        att = att[:, :, 0] - lambda_full * att[:, :, 1]
        out = jnp.einsum('bhts,bhsd->bhtd', att, v)
        rms = jax.lax.rsqrt(jnp.mean(out * out, axis=-1, keepdims=True) + EPS)
        out = out * rms * gamma
        out = (1.0 - LAMBDA_INIT) * out
        out = out.transpose(0, 2, 1, 3).reshape(B, T, C)
        return out @ w_proj

    def _L0_xattn_ref(hidden_states, encoder_hidden_states, Wq, Wk, Wv, Wo, bo):
        import jax, jax.numpy as jnp
        import numpy as np
        HEADS = 16
        DIM_HEAD = 64
        B, S, D = hidden_states.shape
        K = encoder_hidden_states.shape[1]
        H, Dh = (HEADS, DIM_HEAD)
        scale = 1.0 / np.sqrt(Dh)
        q = hidden_states @ Wq
        k = encoder_hidden_states @ Wk
        v = encoder_hidden_states @ Wv
        q = q.reshape(B, S, H, Dh).transpose(0, 2, 1, 3)
        k = k.reshape(B, K, H, Dh).transpose(0, 2, 1, 3)
        v = v.reshape(B, K, H, Dh).transpose(0, 2, 1, 3)
        scores = jnp.einsum('bhsd,bhkd->bhsk', q, k) * scale
        probs = jax.nn.softmax(scores, axis=-1)
        out = jnp.einsum('bhsk,bhkd->bhsd', probs, v)
        out = out.transpose(0, 2, 1, 3).reshape(B, S, H * Dh)
        out = out @ Wo + bo
        return out

    def _L0_ffn_ref(x, Wr, br, Wi, bi, Wg, bg, Wo, bo, gamma, beta):
        import jax, jax.numpy as jnp
        import numpy as np
        E, K = (8, 2)
        B, S, H, F = (2, 256, 128, 512)
        EPS = 1e-12

        def _expert_ffn(xf, Wi_e, bi_e, Wg_e, bg_e, Wo_e, bo_e, g_e, b_e):
            h = jax.nn.gelu(xf @ Wi_e + bi_e, approximate=False) * jax.nn.sigmoid(xf @ Wg_e + bg_e)
            r = xf + (h @ Wo_e + bo_e)
            mu = jnp.mean(r, axis=-1, keepdims=True)
            var = jnp.mean(jnp.square(r - mu), axis=-1, keepdims=True)
            return (r - mu) * jax.lax.rsqrt(var + EPS) * g_e + b_e
        b, s, h = x.shape
        T = b * s
        xf = x.reshape(T, h)
        probs = jax.nn.softmax(xf @ Wr + br, axis=-1)
        topw, topi = jax.lax.top_k(probs, K)
        topw = topw / jnp.sum(topw, axis=-1, keepdims=True)
        c = jnp.zeros((T, E), x.dtype).at[jnp.arange(T)[:, None], topi].set(topw)
        y = jax.vmap(_expert_ffn, in_axes=(None, 0, 0, 0, 0, 0, 0, 0, 0))(xf, Wi, bi, Wg, bg, Wo, bo, gamma, beta)
        out = jnp.einsum('te,eth->th', c, y)
        return out.reshape(b, s, h)
    x = _layernorm(x + _L0_attn_ref(x, L0_attn_w_attn, L0_attn_w_proj, L0_attn_lambda_q1, L0_attn_lambda_q2, L0_attn_lambda_k1, L0_attn_lambda_k2, L0_attn_gamma), axis=-1)
    x = _layernorm(x + _L0_xattn_ref(x, ctx_768, L0_xattn_Wq, L0_xattn_Wk, L0_xattn_Wv, L0_xattn_Wo, L0_xattn_bo), axis=-1)
    x = _layernorm(x + _L0_ffn_ref(x, L0_ffn_Wr, L0_ffn_br, L0_ffn_Wi, L0_ffn_bi, L0_ffn_Wg, L0_ffn_bg, L0_ffn_Wo, L0_ffn_bo, L0_ffn_gamma, L0_ffn_beta), axis=-1)
    return x

_drawn_inputs = setup_inputs


def setup_inputs(seed=0):
    import zlib

    import numpy as np

    out = dict(_drawn_inputs(seed))
    spreads = {'L0_attn_gamma': (1.0, 0.2),
     'L0_ffn_br': (0.0, 0.1),
     'L0_ffn_bi': (0.0, 0.8),
     'L0_ffn_bg': (0.0, 0.8),
     'L0_ffn_bo': (0.0, 0.333),
     'L0_ffn_gamma': (1.0, 0.2),
     'L0_ffn_beta': (0.0, 0.1)}
    factors = {'L0_attn_lambda_q1': 8.0,
     'L0_attn_lambda_q2': 8.0,
     'L0_attn_lambda_k1': 8.0,
     'L0_attn_lambda_k2': 8.0,
     'L0_xattn_bo': 4.53,
     'L0_ffn_Wi': 5.972,
     'L0_ffn_Wg': 8.0,
     'L0_ffn_Wo': 5.362}
    for name, (base, spread) in spreads.items():
        noise = np.random.default_rng([zlib.crc32(name.encode()), seed]).standard_normal(out[name].shape)
        drawn = base * np.exp(spread * noise) if base else spread * noise
        out[name] = jnp.asarray(drawn.astype(out[name].dtype))
    for name, factor in factors.items():
        out[name] = (out[name] * factor).astype(out[name].dtype)
    return out
```

```python
from contextlib import ExitStack

import numpy as np

import concourse.bass as bass
from concourse import mybir

F32 = mybir.dt.float32
F32R = mybir.dt.float32r
BF16 = mybir.dt.bfloat16
I32 = mybir.dt.int32
ALU = mybir.AluOpType
ACT = mybir.ActivationFunctionType
AX = mybir.AxisListType

P = 128
NB, TB, D = 2, 512, 128
T = NB * TB
QT, NT = TB // P, T // P
HD = 4
SH = D // HD
GH = 4
NG = SH // GH
STEPS = NB * NG
COMBOS = 8
Q_PARTS = [0, 0, 1, 1, 0, 2]
K_PARTS = [0, 1, 0, 1, 2, 0]
SCORE_ROWS = len(Q_PARTS) * HD
SHIFT_ROWS = 2
LAMBDA_INIT = 0.2
RMS_EPS, LN_EPS, EXPERT_EPS = 1e-5, 1e-5, 1e-12
XH, XD, KC, DE = 16, 64, 154, 96
XCOLS = XH * KC
XT = -(-XCOLS // P)
XPAD = XT * P
HPC = 3
XCH = -(-XH // HPC)
FOLD_HEADS = [slice(2 * HPC * (c // 2) + c % 2, min(2 * HPC * (c // 2 + 1), XH), 2) for c in range(XCH)]
HPO = 7
XOB = -(-XH // HPO)
NE, F = 8, 512
FT = F // P

MAX_PARTS = [[(3, 0)], [(2, 0), (0, 3 * P)], [(1, 0)]]
EXP_PARTS = [[(j, j, 1, j * P) for j in range(QT)], [(0, 1, 3, 0), (2, 3, 1, 3 * P)], [(1, 2, 2, 0)]]
EXP_WIDTH = [TB, TB, TB // 2]
UNITS = 3 * GH
HEAD_COLS = sum(EXP_WIDTH)
VALUE_BLOCKS = sorted((j, t, k, TB * part + col) for part, blocks in enumerate(EXP_PARTS) for j, t, k, col in blocks)


def segments(k):
    return [h for h in range(XH) if h * KC < (k + 1) * P and (h + 1) * KC > k * P]


def decoder_layer(nc, A, out):
    ctx = ExitStack()
    with ctx:
        def sb(name, shape, dt=F32):
            return ctx.enter_context(nc.sbuf_tensor(name, shape, dt))

        def sem(name):
            return ctx.enter_context(nc.semaphore(name))

        def cut(region, start, *dims):
            n = int(np.prod(dims))
            v = region[:, start:start + n]
            if len(dims) == 1:
                return v
            names = "abcd"[:len(dims)]
            sizes = {a: d for a, d in zip(names, dims)}
            return v.rearrange(f"p ({' '.join(names)}) -> p {' '.join(names)}", **sizes)

        ident = sb("ident", [P, P])
        identb = sb("identb", [P, P], BF16)
        maskb = sb("maskb", [P, P], BF16)
        x_tok = sb("x_tok", [P, NT, D])
        w_proj = sb("w_proj", [P, D])
        scaled_proj = sb("scaled_proj", [P, D])
        gamma_col = sb("gamma_col", [P, 1])
        lambdas = sb("lambdas", [P, 4, HD])
        lam = sb("lam", [P, 8])
        small = sb("small", [P, 6, NT * XH])

        early = sb("early", [P, 5504])
        xT = cut(early, 0, T)
        parts = cut(early, T, 3 * T).bitcast(BF16).rearrange("p (o i t) -> p o i t", o=2, i=3)
        rest = cut(early, 4 * T, 2, TB)
        w_attn = cut(early, 5 * T, 3 * D)
        vblock = cut(early, 0, NB, XT, 130)
        w_raw1 = cut(early, 0, 2, F)
        xres = cut(early, 1024, 2, TB)
        weighted = cut(early, 2048, NT, D)
        acc = cut(early, 3072, NT, D)

        stacks = sb("stacks", [P, 2, 4, TB], BF16)
        indicator = stacks[0:32, :, :, :].rearrange("p a b c -> p (a b c)")[:, 0:XPAD]
        probs = sb("probs", [P, 10240])
        pr = [cut(probs, 5120 * n, GH, HEAD_COLS) for n in range(2)]
        xprobs = cut(probs, 0, XT, TB)
        squares = cut(probs, 0, TB)
        hidden = [cut(probs, 2048 * n, FT, TB) for n in range(2)]
        gelu = cut(probs, 4096, FT, TB)
        gate = cut(probs, 6144, FT, TB)
        res = [cut(probs, 8192 + 1024 * n, NT, D) for n in range(2)]

        v_now = sb("v_now", [P, 2, QT, 2, 32])
        v_all = sb("v_all", [P, STEPS, QT, 16])
        w_raw0 = v_all[:, :, :, :].rearrange("p a b c -> p (a b c)").rearrange("p (a b) -> p a b", a=2)
        head_out = sb("head_out", [P, STEPS * QT * GH * 9])
        ho = head_out[:, :].rearrange("p (s i g d) -> p s i g d", s=STEPS, i=QT, g=GH)
        x2 = cut(head_out, 0, NT, D)
        x2T = cut(head_out, 1024, T)
        out_t = [sb(f"out_t{n}", [P, TB]) for n in range(2)]
        neg_max = sb("neg_max", [P, 2, GH, QT])
        neg_maxb = sb("neg_maxb", [P, 2, 2, GH, QT], BF16)
        max_rows = sb("max_rows", [32, 2, P], BF16)
        wqT = sb("wqT", [P, XH // 2, D])
        attn = wqT
        kT = sb("kT", [P, XH // 2, NB * KC])
        xattn = kT[:, :, :].rearrange("p a b -> p (a b)")[:, 0:2048].rearrange("p (n c) -> p n c", n=2)
        x2d = kT[:, :, :].rearrange("p a b -> p (a b)")[:, 0:NT * D].rearrange("p (n d) -> p n d", n=NT)
        ctx_pad = sb("ctx_pad", [DE + 1, NB, 2 * P + KC])
        wkv = sb("wkv", [P, XH * XD + XH * (XD + 1)])
        wk = wkv[0:DE, 0:XH * XD]
        wv = wkv[0:DE + 1, XH * XD:].rearrange("p (h d) -> p h d", h=XH)
        xattnT = wkv[:, 0:2048].rearrange("p (n k t) -> p n k t", n=2, k=XH // 2)
        wo = sb("wo", [P, XH // 2, D])
        bo_bc = sb("bo_bc", [P, D])
        x1 = sb("x1", [P, NT, D])
        ones_b = x1[:, 0:2, :].rearrange("p a b -> p (a b)").bitcast(BF16)
        fold = sb("fold", [P, 2, NB, XPAD], F32R)

        def fold_heads(part, b, c):
            v = fold[:, part, b, 0:XCOLS].rearrange("p (h s) -> p h s", h=XH)[:, FOLD_HEADS[c], :]
            return v, v.shape[1]

        x1T = sb("x1T", [P, 2, T], F32R)
        x2Tr = sb("x2Tr", [P, 2, T], F32R)
        w_split0 = sb("w_split0", [P, 2, 2, F], F32R)
        w_split1 = fold[:, 0, 0, 0:2048].rearrange("p (s m f) -> p s m f", s=2, m=2)
        w_raw, w_split = [w_raw0, w_raw1], [w_split0[:, :, :, :], w_split1]
        wo_e = sb("wo_e", [P, 2, FT, D])
        rows_e = sb("rows_e", [P, 2, 2, D])
        bi = sb("bi", [P, NE, FT])
        bg = sb("bg", [P, NE, FT])
        bgh = sb("bgh", [P, NE, FT])
        gamma_beta = sb("gamma_beta", [2 * NE, D])
        wr = sb("wr", [P, NE])
        br_bc = sb("br_bc", [P, NE])
        gatew = sb("gatew", [P, 8, NT, NE])
        ranks = sb("ranks", [P, NE])
        coef = sb("coef", [P, NT, 2 * NE])
        coefT = [out_t[n][0:2 * NE, :] for n in range(2)]
        xneg = sb("xneg", [P, 2, XH])
        xnegb = sb("xnegb", [P, 2, 2, XH], BF16)
        xneg_rows = sb("xneg_rows", [32, NB, TB], BF16)
        xmax_free = sb("xrec", [P, 2, XH])

        bank = [ctx.enter_context(nc.psum_tensor(f"bank{n}", [P, TB], F32)) for n in range(8)]
        q_scratch = nc.dram_tensor("q_scratch", [NB * SH * COMBOS * HD, TB], BF16, kind="Internal").ap()
        k_scratch = nc.dram_tensor("k_scratch", [NB * SH * COMBOS * HD, TB], BF16, kind="Internal").ap()

        S = {n: sem(n) for n in (
            "loaded_x", "loaded_attn", "loaded_const", "loaded_cross", "loaded_gate", "loaded_rows",
            "ones_ready", "pads_ready", "qk_ready", "v_ready", "v_copied", "high_ready", "parts_ready", "written",
            "kt_ready", "kt_copied", "fold_ready", "fold_high", "fold_low",
            "max_ready", "max_taken", "neg_high", "neg_low", "rows_ready", "rows_copied",
            "st_ready", "exp_done", "masked", "v_staged", "pv_done", "ot_copied", "otr_done", "head_taken",
            "vb_ready", "vb_copied", "attn_ready", "attnT_ready", "attnT_copied", "proj_ready",
            "x1_ready", "x1T_ready", "x1T_high", "x1T_low", "dve_step", "lam_exp", "lam_in",
            "ind_loaded", "xmax_ready", "xmax_taken", "xneg_done", "xrows_ready", "xrows_copied",
            "xst_ready", "xexp_done", "xpv_ready", "xnorm_done", "xtr_ready", "xtr_copied", "xproj_ready",
            "x2_ready", "x2T_ready", "x2T_high", "x2T_low", "x2T_copied",
            "wraw_free", "split_done", "up_ready", "gelu_done", "tanh_done", "hidden_done", "down_ready",
            "down_taken", "logits_ready", "gate_exp_in", "gate_exp", "xres_ready", "weighted_ready", "acc_done",
            "applied", "coef_ready", "coefT_ready", "coefT_copied", "corr_ready", "stored", "bgh_ready", "rows2_ready")}
        stack_loaded = [sem(f"stack_loaded{n}") for n in range(4)]
        shift_loaded = [sem(f"shift_loaded{n}") for n in range(4)]
        w_loaded = [sem(f"w_loaded{n}") for n in range(2)]

        block = ctx.enter_context(nc.Block())

        def has(i, n):
            return not isinstance(i, int) or 0 <= n < STEPS

        def bodies(eng, body, first=2):
            for i in range(-2, first):
                body(i, i, 0)
            with eng.Fori(0, 3) as turn:
                for c in range(first, first + 4):
                    body(turn * 4 + c, c, turn)
            for i in range(first + 12, STEPS + 2):
                body(i, i, 0)

        def at_least(eng, semaphore, i, count):
            if isinstance(i, int) and count <= 0:
                return
            eng.wait_ge(semaphore, count)

        def turn_of(q, c, lag):
            return q + (c + lag) // 4

        @block.sync
        def _(sp):
            sp.dma_start(xT, A["xT"]).then_inc(S["loaded_x"], 16)
            sp.dma_start(w_attn, A["w_attn"]).then_inc(S["loaded_x"], 16)
            sp.dma_start(ident[:, :], A["ident"]).then_inc(S["loaded_const"], 16)
            sp.dma_start(identb[:, :], A["identb"]).then_inc(S["loaded_const"], 16)
            sp.dma_start(maskb[:, :], A["maskb"]).then_inc(S["loaded_const"], 16)
            sp.wait_ge(S["pads_ready"], 2)
            for b in range(NB):
                sp.dma_start(ctx_pad[0:DE, b, P:P + KC], A["ctxT"][:, b, :]).then_inc(S["loaded_cross"], 16)
            sp.dma_start(wk, A["wk"]).then_inc(S["loaded_cross"], 16)
            sp.dma_start(wv[0:DE, :, 0:XD], A["wv"].rearrange("p (h d) -> p h d", h=XH)).then_inc(S["loaded_cross"], 16)
            sp.dma_start(wqT[:, :, :], A["wqT"].rearrange("(a p) d -> p a d", p=P)).then_inc(S["loaded_cross"], 16)

            qs = q_scratch.rearrange("(b h c d) t -> b c h d t", b=NB, h=SH, c=COMBOS)
            ks = k_scratch.rearrange("(b h c d) t -> b c h d t", b=NB, h=SH, c=COMBOS)
            sp.wait_ge(S["ones_ready"], 1)
            for b in range(NB):
                for c in (6, 7):
                    sp.dma_start(qs[b, c], ones_b).then_inc(S["written"], 16)
                    sp.dma_start(ks[b, c], ones_b).then_inc(S["written"], 16)
            for b in range(NB):
                sp.wait_ge(S["parts_ready"], 4 * (b + 1))
                sp.wait_ge(S["high_ready"], 2 * (b + 1))
                for c in range(len(Q_PARTS)):
                    sp.dma_start(qs[b, c], parts[:, 0, Q_PARTS[c], b * TB:(b + 1) * TB]).then_inc(S["written"], 16)
                    sp.dma_start(ks[b, c], parts[:, 1, K_PARTS[c], b * TB:(b + 1) * TB]).then_inc(S["written"], 16)
            sp.wait_ge(S["written"], 16 * 2 * NB * COMBOS)

            rows = GH * COMBOS * HD

            def load_stacks(i, c, lag):
                b = (c + lag) % 4
                first = (i + lag) * rows
                sp.dma_start(stacks[:, 0, b, :], q_scratch[bass.ds(first, rows), :]).then_inc(stack_loaded[b], 16)
                sp.dma_start(stacks[:, 1, b, :], k_scratch[bass.ds(first, rows), :]).then_inc(stack_loaded[b], 16)

            def body(i, c, q):
                if isinstance(i, int) and i == -2:
                    load_stacks(i, c, 2)
                if has(i, i + 3):
                    at_least(sp, S["st_ready"], i, UNITS * i)
                    load_stacks(i, c, 3)
                if has(i, i + 1):
                    sp.wait_ge(S["rows_copied"], i + 2)
                    b = (c + 1) % 4
                    for part in range(SHIFT_ROWS):
                        row = SCORE_ROWS + part
                        sp.dma_start(stacks[row:P:32, 0, b, :].rearrange("p (i t) -> p i t", i=QT),
                                     max_rows[16 * part:16 * part + 16, (c + 1) % 2, :]).then_inc(shift_loaded[b], 16)

            bodies(sp, body, first=1)

            sp.wait_ge(S["st_ready"], UNITS * STEPS)
            sp.dma_start(indicator, A["indicator"]).then_inc(S["ind_loaded"], 16)

            def load_expert(e):
                n = e % 2
                sp.dma_start(w_raw[n][:, 0, :], A["Wi"][e]).then_inc(w_loaded[n], 16)
                sp.dma_start(w_raw[n][:, 1, :], A["Wg"][e]).then_inc(w_loaded[n], 16)
                sp.dma_start(wo_e[:, n, :, :], A["Wo_e"][e].rearrange("(k p) d -> p k d", p=P)).then_inc(w_loaded[n], 16)
                sp.dma_start(rows_e[:, n, 0, :], A["gamma_e"][e:e + 1, :].partition_broadcast(P)).then_inc(w_loaded[n], 16)
                sp.dma_start(rows_e[:, n, 1, :], A["bo_e"][e:e + 1, :].partition_broadcast(P)).then_inc(w_loaded[n], 16)

            sp.wait_ge(S["v_staged"], QT * STEPS)
            load_expert(0)
            sp.wait_ge(S["xpv_ready"], NT * XOB)
            load_expert(1)
            for e in range(2, NE):
                sp.wait_ge(S["split_done"], 4 * (e - 1))
                sp.wait_ge(S["down_ready"], 2 * (e - 1))
                sp.wait_ge(S["xres_ready"], 2 * (e - 1))
                sp.wait_ge(S["weighted_ready"], e - 1)
                load_expert(e)
            sp.wait_ge(S["stored"], 16)

        @block.scalar
        def _(act):
            act.dma_start(x_tok[:, :, :], A["x"].rearrange("(n p) d -> p n d", p=P)).then_inc(S["loaded_attn"], 16)
            act.dma_start(w_proj[:, :], A["w_proj"]).then_inc(S["loaded_attn"], 16)
            act.dma_start(gamma_col[:, :], A["gamma_col"]).then_inc(S["loaded_attn"], 16)
            for n, name in enumerate(("lambda_q1", "lambda_k1", "lambda_q2", "lambda_k2")):
                act.dma_start(lambdas[:, n, :], A[name].partition_broadcast(P)).then_inc(S["loaded_attn"], 16)
            act.dma_start(wo[:, :, :], A["wo"].rearrange("(k p) d -> p k d", p=P)).then_inc(S["loaded_attn"], 16)
            act.dma_start(bo_bc[:, :], A["bo"].partition_broadcast(P)).then_inc(S["loaded_attn"], 16)
            act.dma_start(bi[:, :, :], A["bi"]).then_inc(S["loaded_gate"], 16)
            act.dma_start(bg[:, :, :], A["bg"]).then_inc(S["loaded_gate"], 16)
            act.dma_start(gamma_beta[0:NE, :], A["gamma_e"]).then_inc(S["loaded_gate"], 16)
            act.dma_start(gamma_beta[NE:2 * NE, :], A["beta_e"]).then_inc(S["loaded_gate"], 16)
            act.dma_start(wr[:, :], A["wr"]).then_inc(S["loaded_gate"], 16)
            act.dma_start(br_bc[:, :], A["br"].partition_broadcast(P)).then_inc(S["loaded_gate"], 16)
            act.dma_start(ranks[:, :], A["ranks"].partition_broadcast(P)).then_inc(S["loaded_gate"], 16)

            for b in range(NB):
                for o in range(2):
                    act.wait_ge(S["qk_ready"], 2 * b + o + 1)
                    nc.scalar.activation(parts[:, o, 0, b * TB:(b + 1) * TB], bank[2 * b + o][:, :], ACT.Copy,
                                         scale=[0.25, 1.0][o]).then_inc(S["high_ready"], 1)
            for b in range(NB):
                act.wait_ge(S["v_ready"], b + 1)
                nc.scalar.copy(v_all[:, b * NG:(b + 1) * NG, :, :].rearrange("p g j d -> p j g d"),
                               bank[4 + b][:, :].rearrange("p (j g d) -> p j g d", j=QT, g=NG)).then_inc(S["v_copied"], 1)
            act.wait_ge(S["lam_in"], 1)
            nc.scalar.activation(lam[:, 2:4], lam[:, 0:2], ACT.Exp).then_inc(S["lam_exp"], 1)
            for n in range(XH // 2):
                act.wait_ge(S["kt_ready"], n + 1)
                nc.scalar.copy(kT[:, n, :], bank[6 + n % 2][:, 0:NB * KC]).then_inc(S["kt_copied"], 1)
            for n in range(NB * XCH):
                b, c = divmod(n, XCH)
                to, w = fold_heads(0, b, c)
                act.wait_ge(S["fold_ready"], n + 1)
                nc.scalar.activation(to, bank[6 + n % 2][:, 0:w * KC].rearrange("p (h s) -> p h s", h=w), ACT.Copy,
                                     scale=0.125).then_inc(S["fold_high"], 1)

            def take_out(i, c):
                act.wait_ge(S["pv_done"], i - 1)
                if not has(i, i):
                    act.wait_ge(S["otr_done"], i - 3)
                nc.scalar.copy(out_t[c % 2][:, :], bank[6][:, :]).then_inc(S["ot_copied"], 1)

            def body(i, c, q):
                if has(i, i):
                    at_least(act, S["pv_done"], i, i - 1)
                    for u in range(UNITS):
                        act.wait_ge(S["st_ready"], UNITS * i + u + 1)
                        h, part = divmod(u, 3)
                        w = EXP_WIDTH[part]
                        nc.scalar.activation(pr[c % 2][:, h, TB * part:TB * part + w], bank[3 + part][:, 0:w],
                                             ACT.Exp).then_inc(S["exp_done"], 1)
                        if u == 1 and has(i, i - 2):
                            take_out(i, c)
                elif has(i, i - 2):
                    take_out(i, c)

            bodies(act, body)

            for n in range(NB * 7):
                b, g = divmod(n, 7)
                w = min(3, XT - 3 * g)
                act.wait_ge(S["vb_ready"], n + 1)
                nc.scalar.copy(vblock[:, b, 3 * g:3 * g + w, :],
                               bank[n % 2][:, 0:130 * w].rearrange("p (k c) -> p k c", k=w)).then_inc(S["vb_copied"], 1)
            for b in range(NB):
                act.wait_ge(S["attnT_ready"], b + 1)
                nc.scalar.copy(out_t[b][:, :], bank[2 + b][:, :]).then_inc(S["attnT_copied"], 1)
            for b in range(NB):
                act.wait_ge(S["x1T_ready"], b + 1)
                nc.scalar.copy(x1T[:, 0, b * TB:(b + 1) * TB], bank[6 + b][:, :]).then_inc(S["x1T_high"], 1)

            for b in range(NB):
                if b == 0:
                    for n in range(NT):
                        act.wait_ge(S["xrows_ready"], n + 1)
                        nc.scalar.copy(xneg_rows[:, n // QT, (n % QT) * P:(n % QT + 1) * P],
                                       bank[6 + n % 2][0:32, 0:64].bitcast(BF16)).then_inc(S["xrows_copied"], 1)
                if b:
                    act.wait_ge(S["xpv_ready"], QT * XOB * b)
                for k in range(XT):
                    act.wait_ge(S["xst_ready"], XT * b + k + 1)
                    nc.scalar.activation(xprobs[:, k, :], bank[(XT * b + k) % 3][:, :], ACT.Exp).then_inc(S["xexp_done"], 1)
                for t in range(QT):
                    n = QT * b + t
                    for half in range(2):
                        act.wait_ge(S["xtr_ready"], 2 * n + half + 1)
                        nc.scalar.copy(xattnT[:, n % 2, 4 * half:4 * half + 4, :],
                                       bank[6 + half][:, :].rearrange("p (k t) -> p k t", k=4)).then_inc(S["xtr_copied"], 1)
                act.wait_ge(S["x2T_ready"], b + 1)
                nc.scalar.copy(x2T[:, b * TB:(b + 1) * TB], bank[6 + b][:, :]).then_inc(S["x2T_copied"], 1)
                nc.scalar.copy(x2Tr[:, 0, b * TB:(b + 1) * TB], bank[6 + b][:, :]).then_inc(S["x2T_high"], 1)
            act.wait_ge(S["gate_exp_in"], 1)
            nc.scalar.activation(gatew[:, 1, :, :], gatew[:, 0, :, :], ACT.Exp).then_inc(S["gate_exp"], 1)

            act.wait_ge(S["bgh_ready"], 1)
            act.wait_ge(S["loaded_gate"], 16 * 7)

            def activations(e, half):
                for f in range(FT):
                    n = (2 * e + half) * FT + f
                    if n >= FT:
                        act.wait_ge(S["hidden_done"], n - FT + 1)
                    act.wait_ge(S["up_ready"], 2 * n + 1)
                    nc.scalar.activation(gelu[:, f, :], bank[2 * (f % 2)][:, :], ACT.Gelu,
                                         bias=bi[:, e, f:f + 1]).then_inc(S["gelu_done"], 1)
                    act.wait_ge(S["up_ready"], 2 * n + 2)
                    nc.scalar.activation(gate[:, f, :], bank[2 * (f % 2) + 1][:, :], ACT.Tanh,
                                         bias=bgh[:, e, f:f + 1], scale=0.5).then_inc(S["tanh_done"], 1)

            for e in range(NE):
                activations(e, 0)
                activations(e, 1)
            act.wait_ge(S["coefT_ready"], 1)
            nc.scalar.copy(coefT[0], bank[6][0:2 * NE, :]).then_inc(S["coefT_copied"], 1)
            nc.scalar.copy(coefT[1], bank[7][0:2 * NE, :]).then_inc(S["coefT_copied"], 1)
            act.wait_ge(S["acc_done"], 2 * NE + 1)
            act.dma_start(out.rearrange("(n p) d -> p n d", p=P), weighted).then_inc(S["stored"], 16)

        @block.gpsimd
        def _(pool):
            nc.gpsimd.memset(ones_b, 1.0).then_inc(S["ones_ready"], 1)
            pool.wait_ge(S["ones_ready"], 1)
            pads = [(ctx_pad[0:DE, :, :], 0.0), (wv[0:DE, :, XD:XD + 1], 0.0), (ctx_pad[DE:DE + 1, :, :], 0.0),
                    (wv[DE:DE + 1, :, :], 0.0), (ctx_pad[DE:DE + 1, :, P:P + KC], 1.0),
                    (wv[DE:DE + 1, :, XD:XD + 1], 1.0), (v_now[:, :, :, :, :], 0.0), (v_now[:, :, :, :, 8:9], 1.0)]
            for n, (region, value) in enumerate(pads):
                nc.gpsimd.memset(region, value).then_inc(S["pads_ready"], 1)
                pool.wait_ge(S["pads_ready"], n + 1)
            pool.wait_ge(S["v_copied"], NB)

            def body(i, c, q):
                if not has(i, i):
                    return
                at_least(pool, S["pv_done"], i, i - 1)
                for h in range(GH):
                    pool.wait_ge(S["exp_done"], UNITS * i + 3 * h + 1)
                    nc.gpsimd.tensor_copy(v_now[:, c % 2, h, :, 0:8],
                                          v_all[:, bass.ds(i, 1), h, :].rearrange("p s (h d) -> p (s h) d", h=2)
                                          ).then_inc(S["v_staged"], 1)
                    blocks = pr[c % 2][:, h, 0:TB].rearrange("p (j t) -> p j t", j=QT)
                    nc.gpsimd.affine_select(out=blocks, in_=blocks, compare_op=ALU.is_ge, fill=0.0, base=0,
                                            pattern=[[0, QT], [1, P]], channel_multiplier=-1).then_inc(S["masked"], 1)

            bodies(pool, body)

            def split(e):
                n = e % 2
                pool.wait_ge(w_loaded[n], 16 * 5 * (e // 2 + 1))
                if e >= 2:
                    pool.wait_ge(S["up_ready"], 4 * FT * (e - 1))
                for m in range(2):
                    nc.gpsimd.tensor_copy(w_split[n][:, 0, m, :], w_raw[n][:, m, :]).then_inc(S["split_done"], 1)
                pool.wait_ge(S["split_done"], 4 * e + 2)
                for m in range(2):
                    nc.gpsimd.tensor_tensor(w_split[n][:, 1, m, :], w_raw[n][:, m, :],
                                            w_split[n][:, 0, m, :].bitcast(F32), ALU.subtract).then_inc(S["split_done"], 1)

            def residual(e, half):
                n = 2 * e + half
                if half == 0:
                    nc.gpsimd.tensor_tensor(rows_e[:, e % 2, 1, :], rows_e[:, e % 2, 1, :], rows_e[:, e % 2, 1, :],
                                            ALU.add).then_inc(S["rows2_ready"], 1)
                    pool.wait_ge(S["rows2_ready"], e + 1)
                if n >= 2:
                    pool.wait_ge(S["down_taken"], n - 1)
                nc.gpsimd.tensor_tensor(xres[:, half, :].rearrange("p (n d) -> p n d", n=QT),
                                        x2d[:, half * QT:(half + 1) * QT, :],
                                        rows_e[:, e % 2, 1:2, :].broadcast_to([P, QT, D]),
                                        ALU.add).then_inc(S["xres_ready"], 1)

            def accumulate(e):
                pool.wait_ge(S["weighted_ready"], e + 1)
                for half in range(2):
                    own = slice(half * QT, (half + 1) * QT)
                    if e:
                        pool.wait_ge(S["acc_done"], 2 * e - 1 + half)
                    nc.gpsimd.tensor_tensor(acc[:, own, :], x2[:, own, :] if e == 0 else acc[:, own, :],
                                            weighted[:, own, :], ALU.add).then_inc(S["acc_done"], 1)

            split(0)
            pool.wait_ge(S["xst_ready"], NB * XT)
            pool.wait_ge(S["xpv_ready"], NT * XOB)
            pool.wait_ge(S["applied"], 1)
            residual(0, 0)
            residual(0, 1)
            split(1)
            for e in range(1, NE):
                residual(e, 0)
                residual(e, 1)
                accumulate(e - 1)
                if e + 1 < NE:
                    split(e + 1)
            accumulate(NE - 1)

        @block.vector
        def _(dve):
            count = [0]

            def link(ins):
                count[0] += 1
                ins.then_inc(S["dve_step"], 1)
                dve.wait_ge(S["dve_step"], count[0])

            def rsqrt(y, v, tmp):
                link(nc.vector.tensor_scalar(tmp.bitcast(I32), v.bitcast(I32), 1, None, ALU.logical_shift_right))
                link(nc.vector.tensor_scalar(y.bitcast(I32), tmp.bitcast(I32), -1.0, float(0x5F3759DF),
                                             ALU.mult, ALU.add))
                for _ in range(3):
                    link(nc.vector.tensor_tensor(tmp, y, y, ALU.mult))
                    link(nc.vector.scalar_tensor_tensor(out=tmp, in0=tmp, scalar=-0.5, in1=v, op0=ALU.mult, op1=ALU.mult))
                    link(nc.vector.scalar_tensor_tensor(out=y, in0=tmp, scalar=1.5, in1=y, op0=ALU.add, op1=ALU.mult))

            def statistics(src, tiles, mv, stats):
                for t in range(tiles):
                    ins = nc.vector.bn_stats(stats[:, t, :], src[:, t, :])
                    if t == tiles - 1:
                        link(ins)
                for t in range(tiles):
                    ins = nc.vector.bn_aggr(mv[:, t, :], stats[:, t, :])
                    if t == tiles - 1:
                        link(ins)

            def layer_norm(dst, src, tiles):
                stats = small[:, 0, 0:6 * tiles].rearrange("p (n c) -> p n c", c=6)
                mv = small[:, 1, 0:2 * tiles].rearrange("p (n c) -> p n c", c=2)
                v, y, tmp = small[:, 2, 0:tiles], small[:, 3, 0:tiles], small[:, 4, 0:tiles]
                statistics(src, tiles, mv, stats)
                link(nc.vector.tensor_scalar(v, mv[:, :, 1], LN_EPS, None, ALU.add))
                rsqrt(y, v, tmp)
                for t in range(tiles):
                    ins = nc.vector.tensor_scalar(dst[:, t, :], src[:, t, :], mv[:, t, 0:1], y[:, t:t + 1],
                                                  ALU.subtract, ALU.mult)
                return ins

            for b in range(NB):
                for o in range(2):
                    own = slice(b * TB, (b + 1) * TB)
                    n = 2 * b + o
                    dve.wait_ge(S["high_ready"], n + 1)
                    link(nc.vector.scalar_tensor_tensor(out=rest[:, o, :], in0=bank[n][:, :], scalar=[0.25, 1.0][o],
                                                        in1=parts[:, o, 0, own], op0=ALU.mult, op1=ALU.subtract))
                    nc.vector.tensor_copy(parts[:, o, 1, own], rest[:, o, :]).then_inc(S["parts_ready"], 1)
                    dve.wait_ge(S["parts_ready"], 2 * n + 1)
                    nc.vector.tensor_tensor(parts[:, o, 2, own], rest[:, o, :], parts[:, o, 1, own],
                                            ALU.subtract).then_inc(S["parts_ready"], 1)
            dve.wait_ge(S["loaded_attn"], 16 * 9)
            lv = lambdas[:, :, :].rearrange("p (a two) d -> p a two d", two=2)
            link(nc.vector.tensor_tensor(small[:, 0, 0:8].rearrange("p (a d) -> p a d", a=2), lv[:, :, 0, :],
                                         lv[:, :, 1, :], ALU.mult))
            nc.vector.tensor_reduce(lam[:, 0:2], small[:, 0, 0:8].rearrange("p (a d) -> p a d", a=2), AX.X,
                                    ALU.add).then_inc(S["lam_in"], 1)
            link(nc.vector.tensor_scalar(scaled_proj[:, :], w_proj[:, :], gamma_col[:, 0:1], 1.0 - LAMBDA_INIT,
                                         ALU.mult, ALU.mult))
            dve.wait_ge(S["lam_exp"], 1)
            link(nc.vector.tensor_tensor(lam[:, 4:5], lam[:, 3:4], lam[:, 2:3], ALU.subtract))
            link(nc.vector.tensor_scalar(lam[:, 5:6], lam[:, 4:5], -LAMBDA_INIT, None, ALU.add))
            for n in range(NB * XCH):
                b, c = divmod(n, XCH)
                high, w = fold_heads(0, b, c)
                dve.wait_ge(S["fold_high"], n + 1)
                nc.vector.scalar_tensor_tensor(out=fold_heads(1, b, c)[0],
                                               in0=bank[6 + n % 2][:, 0:w * KC].rearrange("p (h s) -> p h s", h=w),
                                               scalar=0.125, in1=high.bitcast(F32), op0=ALU.mult,
                                               op1=ALU.subtract).then_inc(S["fold_low"], 1)
            nc.vector.memset(fold[:, :, :, XCOLS:XPAD].bitcast(F32), 0.0).then_inc(S["fold_low"], 1)

            def body(i, c, q):
                if has(i, i + 2):
                    at_least(dve, S["rows_ready"], i, i + 1)
                m = neg_max[:, c % 2, :, :]
                for u in range(UNITS):
                    h, part = divmod(u, 3)
                    if has(i, i + 2):
                        dve.wait_ge(S["max_ready"], UNITS * (i + 2) + u + 1)
                        for qt, col in MAX_PARTS[part]:
                            ins = nc.vector.tensor_reduce(m[:, h, qt:qt + 1], bank[part][:, col:col + (qt + 1) * P],
                                                          AX.X, ALU.max, negate=True)
                        ins.then_inc(S["max_taken"], 1)
                    if u == 2 and has(i, i + 1):
                        dve.wait_ge(S["rows_ready"], i + 2)
                        if has(i, i - 1):
                            dve.wait_ge(shift_loaded[(c - 1) % 4], 16 * SHIFT_ROWS * (turn_of(q, c, -1) + 1))
                        nc.vector.tensor_copy(max_rows[:, (c + 1) % 2, :],
                                              bank[7][0:32, 0:64].bitcast(BF16)).then_inc(S["rows_copied"], 1)
                    if u == 8 and has(i, i - 2):
                        dve.wait_ge(S["otr_done"], i - 1)
                        nc.vector.tensor_copy(
                            ho[:, bass.ds(i - 2, 1), :, :, :].rearrange("p s i g d -> p (s i) g d"),
                            bank[7][:, :].rearrange("p (i g d) -> p i g d", i=QT, g=GH)[:, :, :, 0:9]
                        ).then_inc(S["head_taken"], 1)
                if has(i, i + 2):
                    dve.wait_ge(S["max_taken"], UNITS * (i + 3))
                    nc.vector.tensor_copy(neg_maxb[:, c % 2, 0, :, :], m).then_inc(S["neg_high"], 1)
                    dve.wait_ge(S["neg_high"], i + 3)
                    nc.vector.tensor_tensor(neg_maxb[:, c % 2, 1, :, :], m, neg_maxb[:, c % 2, 0, :, :],
                                            ALU.subtract).then_inc(S["neg_low"], 1)

            bodies(dve, body)

            dve.wait_ge(S["head_taken"], STEPS)
            for b in range(NB):
                own = slice(b * NG, (b + 1) * NG)
                sums = small[:, 0, :].rearrange("p (s i g) -> p s i g", s=NG, i=QT)
                link(nc.vector.reciprocal(sums, ho[:, own, :, :, 8]))
                odd = small[:, 0, :].rearrange("p (n two) -> p n two", two=2)[:, :, 1:2]
                link(nc.vector.tensor_scalar(odd, odd, lam[:, 5:6], None, ALU.mult))
                heads = head_out[:, b * NG * QT * GH * 9:(b + 1) * NG * QT * GH * 9].rearrange("p (n d) -> p n d", d=9)
                link(nc.vector.tensor_tensor(heads[:, :, 0:8], heads[:, :, 0:8],
                                             small[:, 0, :].unsqueeze(2).broadcast_to([P, NG * QT * GH, 8]), ALU.mult))
                for g in range(NG):
                    pair = ho[:, b * NG + g, :, :, :].rearrange("p i (h two) d -> p i h two d", two=2)
                    ins = nc.vector.tensor_tensor(
                        attn[:, b * QT:(b + 1) * QT, 16 * g:16 * g + 16].rearrange("p i (h d) -> p i h d", h=2),
                        pair[:, :, :, 0, 0:8], pair[:, :, :, 1, 0:8], ALU.add)
                link(ins)
                o = attn[:, b * QT:(b + 1) * QT, :].rearrange("p i c -> p (i c)")
                link(nc.vector.tensor_tensor(squares, o, o, ALU.mult))
                n = QT * D // 8
                ms, v, y, tmp = (small[:, s, 0:n] for s in (1, 2, 3, 4))
                link(nc.vector.tensor_reduce(ms, squares.rearrange("p (n d) -> p n d", d=8), AX.X, ALU.add))
                link(nc.vector.tensor_scalar(v, ms, 0.125, RMS_EPS, ALU.mult, ALU.add))
                rsqrt(y, v, tmp)
                o8 = o.rearrange("p (n d) -> p n d", d=8)
                nc.vector.tensor_tensor(o8, o8, y.unsqueeze(2).broadcast_to([P, n, 8]), ALU.mult).then_inc(S["attn_ready"], 1)
            for b in range(NB):
                own = slice(b * QT, (b + 1) * QT)
                dve.wait_ge(S["proj_ready"], b + 1)
                link(nc.vector.tensor_tensor(x1[:, own, :], bank[4 + b][:, :].rearrange("p (n d) -> p n d", n=QT),
                                             x_tok[:, own, :], ALU.add))
                layer_norm(x1[:, own, :], x1[:, own, :], QT).then_inc(S["x1_ready"], 1)
            for b in range(NB):
                dve.wait_ge(S["x1T_high"], b + 1)
                nc.vector.tensor_tensor(x1T[:, 1, b * TB:(b + 1) * TB], bank[6 + b][:, :],
                                        x1T[:, 0, b * TB:(b + 1) * TB].bitcast(F32),
                                        ALU.subtract).then_inc(S["x1T_low"], 1)
            dve.wait_ge(S["x1_ready"], NB)
            for t in range(NT):
                ins = nc.vector.tensor_tensor(x1[:, t, :], x1[:, t, :], bo_bc[:, :], ALU.add)
            link(ins)

            for n in range(NT):
                if n >= 2:
                    dve.wait_ge(S["xrows_ready"], n - 1)
                for c in range(XCH):
                    w = min(HPC, XH - HPC * c)
                    dve.wait_ge(S["xmax_ready"], XCH * n + c + 1)
                    nc.vector.tensor_reduce(xneg[:, n % 2, HPC * c:HPC * c + w],
                                            bank[(XCH * n + c) % 4][:, 0:w * KC].rearrange("p (h s) -> p h s", s=KC),
                                            AX.X, ALU.max, negate=True).then_inc(S["xmax_taken"], 1)
                dve.wait_ge(S["xmax_taken"], XCH * (n + 1))
                link(nc.vector.tensor_copy(xnegb[:, n % 2, 0, :], xneg[:, n % 2, :]))
                nc.vector.tensor_tensor(xnegb[:, n % 2, 1, :], xneg[:, n % 2, :], xnegb[:, n % 2, 0, :],
                                        ALU.subtract).then_inc(S["xneg_done"], 1)

            rec = xmax_free
            for b in range(NB):
                for t in range(QT):
                    n = QT * b + t
                    if n >= 2:
                        dve.wait_ge(S["xtr_ready"], 2 * (n - 1))
                    for c in range(XOB):
                        w = min(HPO, XH - HPO * c)
                        own = slice(HPO * c, HPO * c + w)
                        dve.wait_ge(S["xpv_ready"], XOB * n + c + 1)
                        o = bank[3 + c][:, 0:65 * w].rearrange("p (h d) -> p h d", h=w)
                        link(nc.vector.reciprocal(rec[:, n % 2, own], o[:, :, 64]))
                        nc.vector.tensor_tensor(xattn[:, n % 2, :].rearrange("p (h d) -> p h d", h=XH)[:, own, :],
                                                o[:, :, 0:64],
                                                rec[:, n % 2, own].unsqueeze(2).broadcast_to([P, w, 64]),
                                                ALU.mult).then_inc(S["xnorm_done"], 1)
                own = slice(b * QT, (b + 1) * QT)
                dve.wait_ge(S["xproj_ready"], QT * (b + 1))
                link(nc.vector.tensor_tensor(x2[:, own, :], bank[[2, 1][b]][:, :].rearrange("p (n d) -> p n d", n=QT),
                                             x1[:, own, :], ALU.add))
                layer_norm(x2[:, own, :], x2[:, own, :], QT).then_inc(S["x2_ready"], 1)
                dve.wait_ge(S["x2T_high"], b + 1)
                nc.vector.tensor_tensor(x2Tr[:, 1, b * TB:(b + 1) * TB], bank[6 + b][:, :],
                                        x2Tr[:, 0, b * TB:(b + 1) * TB].bitcast(F32),
                                        ALU.subtract).then_inc(S["x2T_low"], 1)
            dve.wait_ge(S["xtr_ready"], 2 * NT)
            dve.wait_ge(S["x2_ready"], NB)
            nc.vector.tensor_scalar(x2d, x2, 2.0, None, ALU.mult).then_inc(S["applied"], 1)
            dve.wait_ge(S["loaded_gate"], 16 * 7)
            nc.vector.tensor_scalar(bgh[:, :, :], bg[:, :, :], 0.5, None, ALU.mult).then_inc(S["bgh_ready"], 1)

            G = [gatew[:, s, :, :] for s in range(8)]
            row = small[:, 5, :].rearrange("p (s n) -> p s n", s=NT * XH // NT)

            def over(v):
                return v.unsqueeze(2).broadcast_to([P, NT, NE])

            dve.wait_ge(S["logits_ready"], 1)
            link(nc.vector.tensor_tensor(G[2], bank[5][:, 0:NT * NE].rearrange("p (n e) -> p n e", n=NT),
                                         br_bc[:, :].unsqueeze(1).broadcast_to([P, NT, NE]), ALU.add))
            link(nc.vector.tensor_reduce(row[:, 0, :], G[2], AX.X, ALU.max))
            nc.vector.tensor_tensor(G[0], G[2], over(row[:, 0, :]), ALU.subtract).then_inc(S["gate_exp_in"], 1)
            dve.wait_ge(S["gate_exp"], 1)
            link(nc.vector.tensor_reduce(row[:, 1, :], G[1], AX.X, ALU.add))
            link(nc.vector.reciprocal(row[:, 2, :], row[:, 1, :]))
            link(nc.vector.tensor_tensor(G[2], G[1], over(row[:, 2, :]), ALU.mult))

            def pick(probabilities, at, chosen, tmp):
                link(nc.vector.tensor_reduce(row[:, at, :], probabilities, AX.X, ALU.max))
                link(nc.vector.tensor_tensor(tmp, probabilities, over(row[:, at, :]), ALU.is_equal))
                link(nc.vector.tensor_tensor(tmp, tmp, ranks[:, :].unsqueeze(1).broadcast_to([P, NT, NE]), ALU.mult))
                link(nc.vector.tensor_reduce(row[:, 5, :], tmp, AX.X, ALU.max))
                link(nc.vector.tensor_tensor(chosen, tmp, over(row[:, 5, :]), ALU.is_equal))

            pick(G[2], 3, G[3], G[4])
            link(nc.vector.scalar_tensor_tensor(out=G[5], in0=G[3], scalar=-2.0, in1=G[2], op0=ALU.mult, op1=ALU.add))
            pick(G[5], 4, G[6], G[4])
            link(nc.vector.tensor_tensor(row[:, 6, :], row[:, 3, :], row[:, 4, :], ALU.add))
            link(nc.vector.reciprocal(row[:, 7, :], row[:, 6, :]))
            link(nc.vector.tensor_tensor(G[3], G[3], G[6], ALU.add))
            link(nc.vector.tensor_tensor(G[3], G[3], G[2], ALU.mult))
            link(nc.vector.tensor_tensor(coef[:, :, NE:2 * NE], G[3], over(row[:, 7, :]), ALU.mult))

            stats = small[:, 0, 0:6 * NT].rearrange("p (n c) -> p n c", c=6)
            mv = small[:, 1, 0:2 * NT].rearrange("p (n c) -> p n c", c=2)
            v, y, tmp = small[:, 2, 0:NT], small[:, 3, 0:NT], small[:, 4, 0:NT]

            def gated(e, half, f):
                n = (2 * e + half) * FT + f
                if f == 0 and e:
                    dve.wait_ge(S["down_ready"], 2 * e - 1 + half)
                dve.wait_ge(S["tanh_done"], n + 1)
                nc.vector.scalar_tensor_tensor(out=hidden[half][:, f, :], in0=gate[:, f, :], scalar=1.0,
                                               in1=gelu[:, f, :], op0=ALU.add, op1=ALU.mult).then_inc(S["hidden_done"], 1)

            def take(e, half):
                n = 2 * e + half
                own = slice(half * QT, (half + 1) * QT)
                r = res[e % 2]
                dve.wait_ge(S["down_ready"], n + 1)
                dve.wait_ge(S["xres_ready"], n + 1)
                nc.vector.tensor_tensor(r[:, own, :], bank[4 + half][:, :].rearrange("p (n d) -> p n d", n=QT),
                                        xres[:, half, :].rearrange("p (n d) -> p n d", n=QT),
                                        ALU.add).then_inc(S["down_taken"], 1)
                dve.wait_ge(S["down_taken"], n + 1)
                statistics(r[:, own, :], QT, mv[:, own, :], stats[:, own, :])

            def root():
                link(nc.vector.tensor_scalar(v, mv[:, :, 1], 4 * EXPERT_EPS, None, ALU.add))
                rsqrt(y, v, tmp)

            def apply(e):
                link(nc.vector.tensor_tensor(row[:, 0, :], y, coef[:, :, NE + e], ALU.mult))
                link(nc.vector.scalar_tensor_tensor(out=coef[:, :, e], in0=mv[:, :, 0], scalar=-1.0, in1=row[:, 0, :],
                                                    op0=ALU.mult, op1=ALU.mult))
                if e:
                    dve.wait_ge(S["acc_done"], 2 * e)
                for t in range(NT):
                    ins = nc.vector.scalar_tensor_tensor(out=weighted[:, t, :], in0=res[e % 2][:, t, :],
                                                         scalar=row[:, 0, t:t + 1], in1=rows_e[:, e % 2, 0, :],
                                                         op0=ALU.mult, op1=ALU.mult)
                ins.then_inc(S["weighted_ready"], 1)

            for e in range(NE):
                gated(e, 0, 0)
                gated(e, 0, 1)
                if e:
                    take(e - 1, 1)
                gated(e, 0, 2)
                gated(e, 0, 3)
                if e:
                    root()
                gated(e, 1, 0)
                if e:
                    apply(e - 1)
                gated(e, 1, 1)
                gated(e, 1, 2)
                take(e, 0)
                gated(e, 1, 3)
            take(NE - 1, 1)
            root()
            apply(NE - 1)
            dve.wait_ge(S["weighted_ready"], NE)
            dve.wait_ge(S["dve_step"], count[0])
            nc.vector.tensor_copy(small[:, 5, 120:121], coef[:, 0, 0:1]).then_inc(S["coef_ready"], 1)
            dve.wait_ge(S["corr_ready"], 1)
            dve.wait_ge(S["acc_done"], 2 * NE)
            for half in range(2):
                own = slice(half * QT, (half + 1) * QT)
                link(nc.vector.tensor_tensor(weighted[:, own, :], bank[4 + half][:, :].rearrange("p (n d) -> p n d", n=QT),
                                             acc[:, own, :], ALU.add))
            layer_norm(weighted, weighted, NT).then_inc(S["acc_done"], 1)


        @block.tensor
        def _(pe):
            pe.wait_ge(S["loaded_x"], 32)
            for b in range(NB):
                for o in range(2):
                    nc.tensor.matmul(bank[2 * b + o][:, :], w_attn[:, o * D:(o + 1) * D], xT[:, b * TB:(b + 1) * TB],
                                     start=True, stop=True).then_inc(S["qk_ready"], 1)
            for b in range(NB):
                for j in range(QT):
                    n = b * QT + j
                    ins = nc.tensor.matmul(bank[4 + b][:, j * D:(j + 1) * D], xT[:, n * P:(n + 1) * P],
                                           w_attn[:, 2 * D:3 * D], start=True, stop=True)
                ins.then_inc(S["v_ready"], 1)
            pe.wait_ge(S["loaded_cross"], 16 * 5)
            pe.wait_ge(S["pads_ready"], 6)
            for n in range(XH // 2):
                if n >= 2:
                    pe.wait_ge(S["kt_copied"], n - 1)
                nc.tensor.matmul(bank[6 + n % 2][:, 0:NB * KC], wk[:, n * P:(n + 1) * P],
                                 ctx_pad[0:DE, :, P:P + KC], start=True, stop=True).then_inc(S["kt_ready"], 1)
            pe.wait_ge(S["kt_copied"], XH // 2)
            for n in range(NB * XCH):
                b, c = divmod(n, XCH)
                if n >= 2:
                    pe.wait_ge(S["fold_low"], n - 1)
                for m, h in enumerate(range(XH)[FOLD_HEADS[c]]):
                    at = (h % 2) * XD
                    ins = nc.tensor.matmul(bank[6 + n % 2][:, m * KC:(m + 1) * KC],
                                           wqT[at:at + XD, h // 2, :], kT[at:at + XD, h // 2, b * KC:(b + 1) * KC],
                                           start=True, stop=True)
                ins.then_inc(S["fold_ready"], 1)
            pe.wait_ge(S["loaded_const"], 16 * 3)
            pe.wait_ge(S["parts_ready"], 8)
            pe.wait_ge(S["v_copied"], NB)
            pe.wait_ge(S["fold_low"], NB * XCH)
            pe.wait_ge(S["pads_ready"], 8)

            def max_unit(i, c, q, u):
                b = (c + 2) % 4
                if u == 0:
                    pe.wait_ge(stack_loaded[b], 32 * (turn_of(q, c, 2) + 1))
                h, part = divmod(u, 3)
                own = slice(32 * h, 32 * h + SCORE_ROWS)
                at_least(pe, S["max_taken"], i, UNITS * (i + 2) + u - 2)
                for n, (qt, col) in enumerate(MAX_PARTS[part]):
                    nc.tensor.matmul(bank[part][:, col:col + (qt + 1) * P], stacks[own, 0, b, qt * P:(qt + 1) * P],
                                     stacks[own, 1, b, 0:(qt + 1) * P], start=(n == 0), stop=False,
                                     skip_group_check=True)
                for qt, col in MAX_PARTS[part]:
                    ins = nc.tensor.matmul(bank[part][:, col + qt * P:col + (qt + 1) * P], identb[:, :], maskb[:, :],
                                           start=False, stop=True, skip_group_check=True)
                ins.then_inc(S["max_ready"], 1)

            def score_unit(i, c, q, u):
                b = c % 4
                if u == 0:
                    pe.wait_ge(shift_loaded[b], 16 * SHIFT_ROWS * (turn_of(q, c, 0) + 1))
                h, part = divmod(u, 3)
                own = slice(32 * h, 32 * h + SCORE_ROWS + SHIFT_ROWS)
                at_least(pe, S["exp_done"], i, UNITS * i + u - 2)
                for n, (j, t, k, col) in enumerate(EXP_PARTS[part]):
                    ins = nc.tensor.matmul(bank[3 + part][:, col:col + k * P], stacks[own, 1, b, j * P:(j + 1) * P],
                                           stacks[own, 0, b, t * P:(t + k) * P], start=(n == 0), stop=True,
                                           skip_group_check=True)
                ins.then_inc(S["st_ready"], 1)

            def value_block(i, c, n):
                j, t, k, col = VALUE_BLOCKS[n]
                p = (c - 1) % 2
                if n == 0:
                    pe.wait_ge(S["masked"], GH * i)
                    pe.wait_ge(S["exp_done"], UNITS * i)
                    pe.wait_ge(S["v_staged"], QT * i)
                    at_least(pe, S["ot_copied"], i, i - 1)
                for h in range(GH):
                    ins = nc.tensor.matmul(bank[6][32 * h:32 * h + 32, t * P:(t + k) * P], v_now[:, p, j, h // 2, :],
                                           pr[p][:, h, col:col + k * P], start=(n == 0),
                                           stop=(n == len(VALUE_BLOCKS) - 1),
                                           skip_group_check=True)
                if n == len(VALUE_BLOCKS) - 1:
                    ins.then_inc(S["pv_done"], 1)

            def body(i, c, q):
                for u in range(UNITS):
                    if has(i, i + 2):
                        max_unit(i, c, q, u)
                    if u == 1 and has(i, i + 1):
                        pe.wait_ge(S["neg_low"], i + 2)
                        at_least(pe, S["head_taken"], i, i - 2)
                        nc.tensor.transpose(bank[7][0:32, 0:64].bitcast(BF16),
                                            neg_maxb[:, (c + 1) % 2, :, :, :].rearrange("p a h i -> p (a h i)"),
                                            identb[:, :]).then_inc(S["rows_ready"], 1)
                    if has(i, i):
                        score_unit(i, c, q, u)
                    if has(i, i - 1) and u >= UNITS - len(VALUE_BLOCKS):
                        value_block(i, c, u - UNITS + len(VALUE_BLOCKS))
                    if u == 6 and has(i, i - 2):
                        pe.wait_ge(S["ot_copied"], i - 1)
                        if has(i, i + 1):
                            pe.wait_ge(S["rows_copied"], i + 2)
                        else:
                            pe.wait_ge(S["head_taken"], i - 2)
                            pe.wait_ge(S["rows_copied"], STEPS)
                        for t in range(QT):
                            ins = nc.tensor.transpose(bank[7][:, t * P:(t + 1) * P], out_t[c % 2][:, t * P:(t + 1) * P],
                                                      ident[:, :])
                        ins.then_inc(S["otr_done"], 1)

            bodies(pe, body)

            for n in range(NB * 7):
                b, g = divmod(n, 7)
                if n >= 2:
                    pe.wait_ge(S["vb_copied"], n - 1)
                to = bank[n % 2]
                for m, k in enumerate(range(3 * g, min(3 * g + 3, XT))):
                    for s in range(2):
                        h = segments(k)[0] + s
                        at = max(P + k * P - KC * h, 0)
                        h = min(h, XH - 1)
                        ins = nc.tensor.matmul(to[:, 130 * m + 65 * s:130 * m + 65 * s + 65],
                                               ctx_pad[:, b, at:at + P],
                                               wv[:, h, :], start=True, stop=True)
                ins.then_inc(S["vb_ready"], 1)
            for b in range(NB):
                pe.wait_ge(S["attn_ready"], b + 1)
                for t in range(QT):
                    ins = nc.tensor.transpose(bank[2 + b][:, t * P:(t + 1) * P], attn[:, b * QT + t, :], ident[:, :])
                ins.then_inc(S["attnT_ready"], 1)
                pe.wait_ge(S["attnT_copied"], b + 1)
                for t in range(QT):
                    ins = nc.tensor.matmul(bank[4 + b][:, t * D:(t + 1) * D], out_t[b][:, t * P:(t + 1) * P],
                                           scaled_proj[:, :], start=True, stop=True)
                ins.then_inc(S["proj_ready"], 1)
            pe.wait_ge(S["head_taken"], STEPS)
            for b in range(NB):
                pe.wait_ge(S["x1_ready"], b + 1)
                for t in range(QT):
                    ins = nc.tensor.transpose(bank[6 + b][:, t * P:(t + 1) * P], x1[:, b * QT + t, :], ident[:, :])
                ins.then_inc(S["x1T_ready"], 1)

            pe.wait_ge(S["vb_copied"], NB * 7)
            pe.wait_ge(S["x1T_high"], NB)

            def max_tile_rows(n):
                pe.wait_ge(S["xneg_done"], n + 1)
                if n < 2:
                    pe.wait_ge(S["x1T_low"], NB)
                else:
                    pe.wait_ge(S["xrows_copied"], n - 1)
                nc.tensor.transpose(bank[6 + n % 2][0:32, 0:64].bitcast(BF16),
                                    xnegb[:, n % 2, :, :].rearrange("p a h -> p (a h)"),
                                    identb[:, :]).then_inc(S["xrows_ready"], 1)

            for n in range(NT):
                for c in range(XCH):
                    m = XCH * n + c
                    w = min(HPC, XH - HPC * c) * KC
                    if m >= 4:
                        pe.wait_ge(S["xmax_taken"], m - 3)
                    nc.tensor.matmul(bank[m % 4][:, 0:w], x1T[:, 0, n * P:(n + 1) * P],
                                     fold[:, 0, n // QT, HPC * KC * c:HPC * KC * c + w],
                                     start=True, stop=True).then_inc(S["xmax_ready"], 1)
                    if c == 2 and n:
                        max_tile_rows(n - 1)
            max_tile_rows(NT - 1)

            pe.wait_ge(S["ind_loaded"], 16)
            pe.wait_ge(S["xmax_taken"], NT * XCH)

            def cross_transposes(n):
                if n == 0:
                    pe.wait_ge(S["xrows_copied"], NT)
                for half in range(2):
                    pe.wait_ge(S["xnorm_done"], XOB * (n + 1))
                    if n:
                        pe.wait_ge(S["xtr_copied"], 2 * n - 1 + half)
                    if n == QT:
                        pe.wait_ge(S["x2T_low"], 1)
                    for k in range(4):
                        ins = nc.tensor.transpose(bank[6 + half][:, k * P:(k + 1) * P],
                                                  xattn[:, n % 2, (4 * half + k) * P:(4 * half + k + 1) * P], ident[:, :])
                    ins.then_inc(S["xtr_ready"], 1)

            def cross_projection(n):
                pe.wait_ge(S["xtr_copied"], 2 * n + 2)
                to = bank[[2, 1][n // QT]]
                for k in range(XH // 2):
                    ins = nc.tensor.matmul(to[:, (n % QT) * D:(n % QT + 1) * D], xattnT[:, n % 2, k, :], wo[:, k, :],
                                           start=(k == 0), stop=(k == XH // 2 - 1))
                ins.then_inc(S["xproj_ready"], 1)

            for b in range(NB):
                for k in range(XT):
                    m = XT * b + k
                    if m >= 3:
                        pe.wait_ge(S["xexp_done"], m - 2)
                    if b and k < 3:
                        pe.wait_ge(S["x2_ready"], b)
                    if k == 0:
                        pe.wait_ge(S["xrows_copied"], QT * (b + 1))
                        pe.wait_ge(S["x1T_low"], b + 1)
                    to = bank[m % 3][:, :]
                    cols = slice(k * P, (k + 1) * P)
                    tok = slice(b * TB, (b + 1) * TB)
                    nc.tensor.matmul(to, fold[:, 0, b, cols], x1T[:, 0, tok], start=True, stop=False)
                    nc.tensor.matmul(to, fold[:, 0, b, cols], x1T[:, 1, tok], start=False, stop=False)
                    nc.tensor.matmul(to, fold[:, 1, b, cols], x1T[:, 0, tok], start=False, stop=False)
                    nc.tensor.matmul(to, indicator[:, cols], xneg_rows[:, b, :], start=False,
                                     stop=True).then_inc(S["xst_ready"], 1)
                for t in range(QT):
                    n = QT * b + t
                    started, done = [], [max(k for k in range(XT) for h in segments(k) if h // HPO == c)
                                         for c in range(XOB)]
                    for k in range(XT):
                        pe.wait_ge(S["xexp_done"], XT * b + k + 1)
                        for s, h in enumerate(segments(k)):
                            c = h // HPO
                            if c not in started and n:
                                pe.wait_ge(S["xnorm_done"], XOB * (n - 1) + c + 1)
                            last = k == done[c] and (s == len(segments(k)) - 1 or segments(k)[s + 1] // HPO != c)
                            ins = nc.tensor.matmul(bank[3 + c][:, 65 * (h % HPO):65 * (h % HPO) + 65],
                                                   xprobs[:, k, t * P:(t + 1) * P], vblock[:, b, k, 65 * s:65 * s + 65],
                                                   start=c not in started, stop=last, skip_group_check=True)
                            started.append(c)
                            if last:
                                ins.then_inc(S["xpv_ready"], 1)
                    if t:
                        cross_projection(n - 1)
                    cross_transposes(n)
                cross_projection(QT * b + QT - 1)
                pe.wait_ge(S["x2_ready"], b + 1)
                for t in range(QT):
                    ins = nc.tensor.transpose(bank[6 + b][:, t * P:(t + 1) * P], x2[:, QT * b + t, :], ident[:, :])
                ins.then_inc(S["x2T_ready"], 1)

            pe.wait_ge(S["x2T_copied"], NB)
            pe.wait_ge(S["loaded_gate"], 16 * 7)
            pe.wait_ge(S["xnorm_done"], NT * XOB)
            for n in range(NT):
                ins = nc.tensor.matmul(bank[5][:, n * NE:(n + 1) * NE], x2T[:, n * P:(n + 1) * P], wr[:, :],
                                       start=True, stop=True)
            ins.then_inc(S["logits_ready"], 1)
            pe.wait_ge(S["x2T_low"], NB)

            def up(e, half):
                tok = slice(half * TB, (half + 1) * TB)
                if half == 0:
                    pe.wait_ge(S["split_done"], 4 * (e + 1))
                for f in range(FT):
                    cols = slice(f * P, (f + 1) * P)
                    n = (2 * e + half) * FT + f
                    for m in range(2):
                        to = bank[2 * (f % 2) + m][:, :]
                        if n >= 2:
                            pe.wait_ge([S["gelu_done"], S["tanh_done"]][m], n - 1)
                        w = w_split[e % 2]
                        nc.tensor.matmul(to, w[:, 0, m, cols], x2Tr[:, 0, tok], start=True, stop=False)
                        nc.tensor.matmul(to, w[:, 0, m, cols], x2Tr[:, 1, tok], start=False, stop=False)
                        nc.tensor.matmul(to, w[:, 1, m, cols], x2Tr[:, 0, tok], start=False,
                                         stop=True).then_inc(S["up_ready"], 1)

            def down(e, half):
                n = 2 * e + half
                if n >= 2:
                    pe.wait_ge(S["down_taken"], n - 1)
                else:
                    pe.wait_ge(S["gate_exp_in"], 1)
                pe.wait_ge(w_loaded[e % 2], 16 * 5 * (e // 2 + 1))
                pe.wait_ge(S["hidden_done"], FT * (n + 1))
                for t in range(QT):
                    for f in range(FT):
                        ins = nc.tensor.matmul(bank[4 + half][:, t * D:(t + 1) * D], hidden[half][:, f, t * P:(t + 1) * P],
                                               wo_e[:, e % 2, f, :], start=(f == 0), stop=(f == FT - 1))
                ins.then_inc(S["down_ready"], 1)

            for e in range(NE):
                up(e, 0)
                if e:
                    down(e - 1, 1)
                up(e, 1)
                down(e, 0)
            down(NE - 1, 1)
            pe.wait_ge(S["coef_ready"], 1)
            for n in range(NT):
                ins = nc.tensor.transpose(bank[6 + n // QT][0:2 * NE, (n % QT) * P:(n % QT + 1) * P], coef[:, n, :],
                                          ident[:, :])
            ins.then_inc(S["coefT_ready"], 1)
            pe.wait_ge(S["coefT_copied"], 2)
            pe.wait_ge(S["down_taken"], 2 * NE)
            for n in range(NT):
                ins = nc.tensor.matmul(bank[4 + n // QT][:, (n % QT) * D:(n % QT + 1) * D], coefT[n // QT][:, (n % QT) * P:(n % QT + 1) * P],
                                       gamma_beta[:, :], start=True, stop=True)
            ins.then_inc(S["corr_ready"], 1)


def kernel(**inputs):
    import concourse.bacc as bacc
    from concourse.bass_utils import run_bass_kernel_spmd
    import ml_dtypes

    a = {k: np.asarray(v) for k, v in inputs.items()}
    pre, xa, ff = "L0_attn_", "L0_xattn_", "L0_ffn_"
    x = a["x"].reshape(T, D)
    row = np.arange(XPAD)
    head = np.arange(XH)[:, None]
    hot = ((row // KC == head) & (row < XCOLS))
    layout = {
        "x": x, "xT": x.T,
        "ctxT": a["ctx_768"].transpose(2, 0, 1),
        "w_attn": a[pre + "w_attn"], "w_proj": a[pre + "w_proj"],
        "gamma_col": np.tile(a[pre + "gamma"], D // (2 * HD))[:, None],
        "wk": a[xa + "Wk"], "wv": a[xa + "Wv"], "wqT": a[xa + "Wq"].T, "wo": a[xa + "Wo"], "bo": a[xa + "bo"][None],
        "wr": a[ff + "Wr"], "br": a[ff + "br"][None], "Wi": a[ff + "Wi"], "Wg": a[ff + "Wg"], "Wo_e": a[ff + "Wo"],
        "bi": a[ff + "bi"].reshape(NE, FT, P).transpose(2, 0, 1), "bg": a[ff + "bg"].reshape(NE, FT, P).transpose(2, 0, 1),
        "bo_e": a[ff + "bo"], "gamma_e": a[ff + "gamma"], "beta_e": a[ff + "beta"],
        "ident": np.eye(P, dtype=np.float32), "identb": np.eye(P).astype(ml_dtypes.bfloat16),
        "maskb": np.triu(np.full((P, P), -3e38), 1).astype(ml_dtypes.bfloat16),
        "indicator": np.concatenate([hot, hot]).astype(ml_dtypes.bfloat16),
        "ranks": np.arange(NE, 0, -1, dtype=np.float32)[None],
    }
    for n in ("q1", "k1", "q2", "k2"):
        layout[f"lambda_{n}"] = a[f"{pre}lambda_{n}"][None]
    nc = bacc.Bacc("TRN2", target_bir_lowering=False, num_devices=1)
    arrays, aps = {}, {}
    for name, v in layout.items():
        v = np.ascontiguousarray(v)
        arrays[f"in_{name}"] = v
        aps[name] = nc.dram_tensor(f"in_{name}", v.shape, mybir.dt.from_np(v.dtype), kind="ExternalInput").ap()
    out = nc.dram_tensor("out_x", [T, D], F32, kind="ExternalOutput").ap()
    decoder_layer(nc, aps, out)
    r = run_bass_kernel_spmd(nc, [arrays], core_ids=[0])
    return r.results[0]["out_x"].reshape(NB, TB, D)
```

```python
from contextlib import ExitStack

import numpy as np

import concourse.bass as bass
from concourse import mybir

F32 = mybir.dt.float32
F32R = mybir.dt.float32r
BF16 = mybir.dt.bfloat16
I32 = mybir.dt.int32
ALU = mybir.AluOpType
ACT = mybir.ActivationFunctionType
AX = mybir.AxisListType

P = 128
NB, TB, D = 2, 512, 128
T = NB * TB
QT, NT = TB // P, T // P
HD = 4
SH = D // HD
GH = 4
NG = SH // GH
STEPS = NB * NG
COMBOS = 8
Q_ROWS = [(0, 1, 3, 0), (3, 1, 2, 1), (5, 1, 1, 2)]
K_ROWS = [(0, 3, 2, 0), (5, 1, 1, 0), (1, 3, 2, 1), (2, 1, 1, 2)]
SHIFT_ROW, SHIFT_ROWS = 6, 2
HEAD_ROWS = HD * COMBOS
LAMBDA_INIT = 0.2
RMS_EPS, LN_EPS, EXPERT_EPS = 1e-5, 1e-5, 1e-12
XH, XD, KC, DE = 16, 64, 154, 96
XCOLS = XH * KC
XT = -(-XCOLS // P)
XPAD = XT * P
HPC = 3
XCH = -(-XH // HPC)
FOLD_HEADS = [slice(2 * HPC * (c // 2) + c % 2, min(2 * HPC * (c // 2 + 1), XH), 2) for c in range(XCH)]
HPO = 7
XOB = -(-XH // HPO)
SECOND_MAX = [[XCH * QT + m for m in range(1, XCH * QT) if m * XT // (XCH * QT) == k] for k in range(XT)]
MAX_RING, SCORE_RING = [0, 1, 5], [2, 3, 4]
NE, F = 8, 512
FT = F // P

MAX_PARTS = [[(3, 0)], [(2, 0), (0, 3 * P)], [(1, 0)]]
EXP_PARTS = [[(j, j, 1, j * P) for j in range(QT)], [(0, 1, 3, 0), (2, 3, 1, 3 * P)], [(1, 2, 2, 0)]]
EXP_WIDTH = [TB, TB, TB // 2]
UNITS = 3 * GH
HEAD_COLS = sum(EXP_WIDTH)
VALUE_BLOCKS = sorted((j, t, k, TB * part + col) for part, blocks in enumerate(EXP_PARTS) for j, t, k, col in blocks)
VALUE_AT = [2, 3, 5, 6, 8, 9, 10]


def segments(k):
    return [h for h in range(XH) if h * KC < (k + 1) * P and (h + 1) * KC > k * P]


OUTPUT_RUNS = []
for _k in range(XT):
    _banks = [h // HPO for h in segments(_k)]
    OUTPUT_RUNS.append([(_banks.index(c), _banks.count(c), c) for c in sorted(set(_banks))])


def decoder_layer(nc, A, out):
    ctx = ExitStack()
    with ctx:
        def sb(name, shape, dt=F32):
            return ctx.enter_context(nc.sbuf_tensor(name, shape, dt))

        def sem(name):
            return ctx.enter_context(nc.semaphore(name))

        def cut(region, start, *dims):
            n = int(np.prod(dims))
            v = region[:, start:start + n]
            if len(dims) == 1:
                return v
            names = "abcd"[:len(dims)]
            sizes = {a: d for a, d in zip(names, dims)}
            return v.rearrange(f"p ({' '.join(names)}) -> p {' '.join(names)}", **sizes)

        columns = sb("columns", [P, 2 * P + 2 * NE * FT + NE + 1])
        ident = cut(columns, 0, P)
        w_proj = cut(columns, P, D)
        bi = cut(columns, 2 * P, NE, FT)
        bg = cut(columns, 2 * P + NE * FT, NE, FT)
        wr = cut(columns, 2 * P + 2 * NE * FT, NE)
        gamma_col = cut(columns, 2 * P + 2 * NE * FT + NE, 1)
        rows_bc = sb("rows_bc", [P, 4 * HD + 2 * NE + D])
        lambdas = cut(rows_bc, 0, 2, 2, HD)
        br_bc = cut(rows_bc, 4 * HD, NE)
        ranks = cut(rows_bc, 4 * HD + NE, NE)
        bo_bc = cut(rows_bc, 4 * HD + 2 * NE, D)
        identb = sb("identb", [P, P], BF16)
        maskb = sb("maskb", [P, P], BF16)
        x_tok = sb("x_tok", [P, NT, D])
        scaled_proj = sb("scaled_proj", [P, D])
        lam = sb("lam", [P, 8])
        small = sb("small", [P, 6, NT * XH])

        early = sb("early", [P, 5504])
        xT = cut(early, 0, T)
        parts = cut(early, T, 3 * T).bitcast(BF16).rearrange("p (o i t) -> p o i t", o=2, i=3)
        rest = cut(early, 4 * T, 2, TB)
        w_attn = cut(early, 5 * T, 3 * D)
        vblock = cut(early, 0, NB, XT, 130)
        w_raw1 = cut(early, 0, 2, F)
        xres = cut(early, 1024, 2, TB)
        weighted = cut(early, 2048, NT, D)
        acc = cut(early, 3072, NT, D)

        stacks = sb("stacks", [P, 4, 2, TB], BF16)
        indicator = stacks[0:32, :, :, :].rearrange("p a b c -> p (a b c)")[:, 0:XPAD]
        probs = sb("probs", [P, 10240])
        pr = [cut(probs, 5120 * n, GH, HEAD_COLS) for n in range(2)]
        zeros_b = cut(probs, 0, TB // 2).bitcast(BF16)
        xprobs = cut(probs, 0, XT, TB)
        squares = cut(probs, 0, T)
        hidden = [cut(probs, 2048 * n, FT, TB) for n in range(2)]
        gelu = cut(probs, 4096, FT, TB)
        gate = cut(probs, 6144, FT, TB)
        res = [cut(probs, 8192 + 1024 * n, NT, D) for n in range(2)]

        v_now = sb("v_now", [P, 2, QT, 2, 32])
        v_all = sb("v_all", [P, STEPS, QT, 16])
        w_raw0 = v_all[:, :, :, :].rearrange("p a b c -> p (a b c)").rearrange("p (a b) -> p a b", a=2)
        x2_both = sb("x2_both", [P, 2 * T])
        head_inv = sb("head_inv", [P, QT, GH])
        head_val = sb("head_val", [P, 2, QT, GH, 8])
        k_alone = x2_both[:, :].bitcast(BF16).rearrange("p (n g t) -> p n g t", n=2, g=GH)
        x2 = cut(x2_both, 0, NT, D)
        x2T = cut(x2_both, 1024, T)
        out_t = [sb(f"out_t{n}", [P, TB]) for n in range(2)]
        neg_max = sb("neg_max", [P, 2, GH, QT])
        neg_maxb = sb("neg_maxb", [P, 2, 2, GH, QT], BF16)
        max_rows = sb("max_rows", [32, 2, P], BF16)
        wqT = sb("wqT", [P, XH // 2, D])
        attn = wqT[:, :, :].rearrange("p a b -> p (a b)").rearrange("p (s i c) -> p s i c", s=STEPS, i=QT)
        kT = sb("kT", [P, XH // 2, NB * KC])
        xattn = kT[:, :, :].rearrange("p a b -> p (a b)")[:, 0:2048].rearrange("p (n c) -> p n c", n=2)
        x2d = kT[:, :, :].rearrange("p a b -> p (a b)")[:, 0:NT * D].rearrange("p (n d) -> p n d", n=NT)
        attn_rms = kT[:, :, :].rearrange("p a b -> p (a b)")[:, 0:T].rearrange("p (n c) -> p n c", n=NT)
        ctx_pad = sb("ctx_pad", [DE + 1, NB, 2 * P + KC])
        wkv = sb("wkv", [P, XH * XD + XH * (XD + 1)])
        wk = wkv[0:DE, 0:XH * XD]
        wv = wkv[0:DE + 1, XH * XD:].rearrange("p (h d) -> p h d", h=XH)
        xattnT = wkv[:, 0:2048].rearrange("p (n k t) -> p n k t", n=2, k=XH // 2)
        wo = sb("wo", [P, XH // 2, D])
        x1 = sb("x1", [P, NT, D])
        ones_b = x1[:, 0:2, :].rearrange("p a b -> p (a b)").bitcast(BF16)
        fold = sb("fold", [P, 2, NB, XPAD], F32R)

        def fold_heads(part, b, c):
            v = fold[:, part, b, 0:XCOLS].rearrange("p (h s) -> p h s", h=XH)[:, FOLD_HEADS[c], :]
            return v, v.shape[1]

        x1T = sb("x1T", [P, 2, T], F32R)
        x2Tr = sb("x2Tr", [P, 2, T], F32R)
        w_split0 = sb("w_split0", [P, 2, 2, F], F32R)
        w_split1 = fold[:, 0, 0, 0:2048].rearrange("p (s m f) -> p s m f", s=2, m=2)
        w_raw, w_split = [w_raw0, w_raw1], [w_split0[:, :, :, :], w_split1]
        wo_e = sb("wo_e", [P, 2, FT, D])
        rows_e = sb("rows_e", [P, 2, 2, D])
        bgh = sb("bgh", [P, NE, FT])
        gamma_beta = sb("gamma_beta", [2 * NE, D])
        gatew = sb("gatew", [P, 8, NT, NE])
        coef = sb("coef", [P, NT, 2 * NE])
        coefT = [out_t[n][0:2 * NE, :] for n in range(2)]
        xneg = sb("xneg", [P, 2, XH])
        xnegb = sb("xnegb", [P, 2, 2, XH], BF16)
        xneg_rows = sb("xneg_rows", [32, NB, TB], BF16)
        xmax_free = sb("xrec", [P, 2, XH])

        bank = [ctx.enter_context(nc.psum_tensor(f"bank{n}", [P, TB], F32)) for n in range(8)]
        scratch = nc.dram_tensor("scratch", [NB * D * COMBOS, 2, TB], BF16, kind="Internal").ap()

        S = {n: sem(n) for n in ("zeroed", "head_inv_done", "head_scaled", "head_done", "consts_ready", "wo_loaded0", "wo_loaded1",
            "rows_loaded0", "rows_loaded1", "written0", "written1", "loaded_x1", "loaded_tok", "loaded_wv",
            "loaded_x", "loaded_attn", "loaded_const", "loaded_cross", "loaded_gate", "loaded_rows",
            "ones_ready", "pads_ready", "qk_ready", "v_ready", "v_copied", "high_ready", "parts_ready", "written",
            "kt_ready", "kt_copied", "fold_ready", "fold_high", "fold_low",
            "max_ready", "max_taken", "neg_high", "neg_low", "rows_ready", "rows_copied",
            "st_ready", "exp_done", "masked", "v_staged", "pv_done", "ot_copied", "otr_done", "head_taken",
            "vb_ready", "vb_copied", "attn_ready", "attnT_ready", "attnT_copied", "proj_ready",
            "x1_ready", "x1T_ready", "x1T_high", "x1T_low", "dve_step", "lam_exp", "lam_in",
            "ind_loaded", "xmax_ready", "xmax_taken", "xneg_done", "xrows_ready", "xrows_copied",
            "xst_ready", "xexp_done", "xpv_ready", "xnorm_done", "xtr_ready", "xtr_copied", "xproj_ready",
            "x2_ready", "x2T_ready", "x2T_high", "x2T_low", "x2T_copied",
            "wraw_free", "split_done", "up_ready", "gelu_done", "tanh_done", "hidden_done", "down_ready",
            "down_taken", "logits_ready", "gate_exp_in", "gate_exp", "xres_ready", "weighted_ready", "acc_done",
            "applied", "coef_ready", "coefT_ready", "coefT_copied", "corr_ready", "stored", "bgh_ready", "rows2_ready")}
        alone_loaded = [sem(f"alone_loaded{n}") for n in range(2)]
        stack_loaded = [sem(f"stack_loaded{n}") for n in range(4)]
        shift_loaded = [sem(f"shift_loaded{n}") for n in range(4)]
        w_loaded = [sem(f"w_loaded{n}") for n in range(2)]

        block = ctx.enter_context(nc.Block())

        def has(i, n):
            return not isinstance(i, int) or 0 <= n < STEPS

        def bodies(eng, body, first=2):
            for i in range(-2, first):
                body(i, i, 0)
            with eng.Fori(0, 3) as turn:
                for c in range(first, first + 4):
                    body(turn * 4 + c, c, turn)
            for i in range(first + 12, STEPS + 2):
                body(i, i, 0)

        def at_least(eng, semaphore, i, count):
            if isinstance(i, int) and count <= 0:
                return
            eng.wait_ge(semaphore, count)

        def turn_of(q, c, lag):
            return q + (c + lag) // 4

        @block.sync
        def _(sp):
            sp.dma_start(w_attn, A["w_attn"]).then_inc(S["loaded_x"], 16)
            sp.dma_start(xT[:, 0:TB], A["xT"][:, 0:TB]).then_inc(S["loaded_x"], 16)
            sp.dma_start(xT[:, TB:T], A["xT"][:, TB:T]).then_inc(S["loaded_x1"], 16)
            sp.wait_ge(S["pads_ready"], 6)
            sp.dma_start(ctx_pad[0:DE, :, P:P + KC], A["ctxT"]).then_inc(S["loaded_cross"], 16)
            sp.dma_start(wk, A["wk"]).then_inc(S["loaded_cross"], 16)

            rows = scratch.rearrange("(b p c) o t -> b o p c t", b=NB, c=COMBOS)
            sp.wait_ge(S["consts_ready"], 2)

            def write(b, o, first, step, n, source, done):
                sp.dma_start(rows[b, o][:, first:first + step * (n - 1) + 1:step, :],
                             source.unsqueeze(1).broadcast_to([P, n, TB])).then_inc(done, 16)

            for b in range(NB):
                for o, source in enumerate((zeros_b, ones_b)):
                    write(b, o, SHIFT_ROW, 1, SHIFT_ROWS, source, S["written0"])

            def write_parts(b):
                sp.wait_ge(S["parts_ready"], 4 * (b + 1))
                for o, table in enumerate((Q_ROWS, K_ROWS)):
                    for first, step, n, part in table:
                        write(b, o, first, step, n, parts[:, o, part, b * TB:(b + 1) * TB], S[f"written{b}"])

            own_rows = GH * HEAD_ROWS
            writes = 16 * (len(Q_ROWS) + len(K_ROWS))

            def load_stacks(i, c, lag):
                sp.dma_start(stacks[:, (c + lag) % 4, :, :],
                             scratch[bass.ds((i + lag) * own_rows, own_rows), :, :]
                             ).then_inc(stack_loaded[(c + lag) % 4], 16)

            def load_alone(i, c):
                n = (c + 1) % 2
                for h in range(GH):
                    own = slice(HEAD_ROWS * h, HEAD_ROWS * (h + 1))
                    sp.dma_start(k_alone[own, n, h, :],
                                 scratch[bass.ds((i + 1) * own_rows + HEAD_ROWS * h, HEAD_ROWS), 1, :]
                                 ).then_inc(alone_loaded[n], 16)

            write_parts(0)
            sp.dma_start(identb[:, :], A["identb"]).then_inc(S["loaded_const"], 16)
            sp.dma_start(maskb[:, :], A["maskb"]).then_inc(S["loaded_const"], 16)
            sp.dma_start(wqT[:, :, :], A["wqT"].rearrange("(a p) d -> p a d", p=P)).then_inc(S["loaded_cross"], 16)
            sp.wait_ge(S["written0"], writes + 16 * 2 * NB)

            def body(i, c, q):
                if isinstance(i, int) and i == -2:
                    load_stacks(i, c, 2)
                if isinstance(i, int) and i == -1:
                    write_parts(1)
                    sp.dma_start(wv[0:DE, :, 0:XD], A["wv"].rearrange("p (h d) -> p h d", h=XH)).then_inc(S["loaded_wv"], 16)
                if isinstance(i, int) and i == 0:
                    sp.wait_ge(S["written1"], writes)
                if has(i, i + 1):
                    at_least(sp, S["st_ready"], i, UNITS * i)
                    if isinstance(i, int) and i == -1:
                        sp.wait_ge(S["zeroed"], 1)
                    load_alone(i, c)
                if has(i, i + 3):
                    load_stacks(i, c, 3)
                if has(i, i + 1):
                    sp.wait_ge(S["rows_copied"], i + 2)
                    b = (c + 1) % 4
                    for part in range(SHIFT_ROWS):
                        sp.dma_start(stacks[SHIFT_ROW + part:P:HEAD_ROWS, b, 0, :].rearrange("p (i t) -> p i t", i=QT),
                                     max_rows[16 * part:16 * part + 16, (c + 1) % 2, :]).then_inc(shift_loaded[b], 16)

            bodies(sp, body, first=1)

            sp.wait_ge(S["st_ready"], UNITS * STEPS)
            sp.dma_start(indicator, A["indicator"]).then_inc(S["ind_loaded"], 16)

            def load_raw(e):
                sp.dma_start(w_raw[e % 2], A["Wig"][e]).then_inc(w_loaded[e % 2], 16)

            def load_rest(e):
                n = e % 2
                if e >= 2:
                    sp.wait_ge(S["down_ready"], 2 * (e - 1))
                sp.dma_start(wo_e[:, n, :, :], A["Wo_e"][e].rearrange("(k p) d -> p k d", p=P)).then_inc(S[f"wo_loaded{n}"], 16)
                if e >= 2:
                    sp.wait_ge(S["xres_ready"], 2 * (e - 1))
                    sp.wait_ge(S["weighted_ready"], e - 1)
                sp.dma_start(rows_e[:, n, :, :], A["rows_e"][e:e + 1].partition_broadcast(P)).then_inc(S[f"rows_loaded{n}"], 16)

            sp.wait_ge(S["v_staged"], QT * STEPS)
            load_raw(0)
            load_rest(0)
            load_rest(1)
            sp.wait_ge(S["xpv_ready"], NT * XOB)
            load_raw(1)
            for e in range(2, NE):
                sp.wait_ge(S["split_done"], 4 * (e - 1))
                load_raw(e)
                load_rest(e)
            sp.wait_ge(S["stored"], 16)

        @block.scalar
        def _(act):
            for b in range(NB):
                for o in range(2):
                    act.wait_ge(S["qk_ready"], 2 * b + o + 1)
                    nc.scalar.activation(parts[:, o, 0, b * TB:(b + 1) * TB], bank[2 * b + o][:, :], ACT.Copy,
                                         scale=[0.25, 1.0][o]).then_inc(S["high_ready"], 1)
            act.dma_start(rows_bc[:, :], A["rows_bc"].partition_broadcast(P)).then_inc(S["loaded_attn"], 16)
            act.dma_start(columns[:, :], A["columns"]).then_inc(S["loaded_attn"], 16)
            for b in range(NB):
                act.wait_ge(S["v_ready"], b + 1)
                nc.scalar.copy(v_all[:, b * NG:(b + 1) * NG, :, :].rearrange("p g j d -> p j g d"),
                               bank[4 + b][:, :].rearrange("p (j g d) -> p j g d", j=QT, g=NG)).then_inc(S["v_copied"], 1)
            act.dma_start(x_tok[:, :, :], A["x"].rearrange("(n p) d -> p n d", p=P)).then_inc(S["loaded_tok"], 16)
            act.dma_start(wo[:, :, :], A["wo"].rearrange("(k p) d -> p k d", p=P)).then_inc(S["loaded_tok"], 16)
            act.dma_start(gamma_beta[:, :], A["gamma_beta"]).then_inc(S["loaded_tok"], 16)
            act.wait_ge(S["lam_in"], 1)
            nc.scalar.activation(lam[:, 2:4], lam[:, 0:2], ACT.Exp).then_inc(S["lam_exp"], 1)
            for n in range(XH // 2):
                act.wait_ge(S["kt_ready"], n + 1)
                nc.scalar.copy(kT[:, n, :], bank[6 + n % 2][:, 0:NB * KC]).then_inc(S["kt_copied"], 1)
            for n in range(NB * XCH):
                b, c = divmod(n, XCH)
                to, w = fold_heads(0, b, c)
                act.wait_ge(S["fold_ready"], n + 1)
                nc.scalar.activation(to, bank[6 + n % 2][:, 0:w * KC].rearrange("p (h s) -> p h s", h=w), ACT.Copy,
                                     scale=0.125).then_inc(S["fold_high"], 1)

            def take_out(i, c):
                act.wait_ge(S["pv_done"], i - 1)
                if not has(i, i):
                    act.wait_ge(S["otr_done"], i - 3)
                nc.scalar.copy(out_t[c % 2][:, :], bank[6][:, :]).then_inc(S["ot_copied"], 1)

            def body(i, c, q):
                if has(i, i):
                    at_least(act, S["pv_done"], i, i - 1)
                    for u in range(UNITS):
                        act.wait_ge(S["st_ready"], UNITS * i + u + 1)
                        h, part = divmod(u, 3)
                        w = EXP_WIDTH[part]
                        nc.scalar.activation(pr[c % 2][:, h, TB * part:TB * part + w], bank[3 + part][:, 0:w],
                                             ACT.Exp).then_inc(S["exp_done"], 1)
                        if u == 1 and has(i, i - 2):
                            take_out(i, c)
                elif has(i, i - 2):
                    take_out(i, c)

            bodies(act, body)

            for n in range(NB * 7):
                b, g = divmod(n, 7)
                w = min(3, XT - 3 * g)
                act.wait_ge(S["vb_ready"], n + 1)
                nc.scalar.copy(vblock[:, b, 3 * g:3 * g + w, :],
                               bank[n % 2][:, 0:130 * w].rearrange("p (k c) -> p k c", k=w)).then_inc(S["vb_copied"], 1)
            for b in range(NB):
                act.wait_ge(S["attnT_ready"], b + 1)
                nc.scalar.copy(out_t[b][:, :], bank[2 + b][:, :]).then_inc(S["attnT_copied"], 1)
            for b in range(NB):
                act.wait_ge(S["x1T_ready"], b + 1)
                nc.scalar.copy(x1T[:, 0, b * TB:(b + 1) * TB], bank[6 + b][:, :]).then_inc(S["x1T_high"], 1)

            def copy_max_rows(n):
                act.wait_ge(S["xrows_ready"], n + 1)
                nc.scalar.copy(xneg_rows[:, n // QT, (n % QT) * P:(n % QT + 1) * P],
                               bank[6 + n % 2][0:32, 0:64].bitcast(BF16)).then_inc(S["xrows_copied"], 1)

            for b in range(NB):
                if b == 0:
                    for n in range(QT):
                        copy_max_rows(n)
                if b:
                    act.wait_ge(S["xpv_ready"], QT * XOB * b)
                for k in range(XT):
                    act.wait_ge(S["xst_ready"], XT * b + k + 1)
                    nc.scalar.activation(xprobs[:, k, :], bank[SCORE_RING[(XT * b + k) % 3]][:, :],
                                         ACT.Exp).then_inc(S["xexp_done"], 1)
                    for m in SECOND_MAX[k]:
                        if b == 0 and m % XCH == 2 and m // XCH % QT:
                            copy_max_rows(m // XCH - 1)
                if b == 0:
                    copy_max_rows(NT - 1)
                for t in range(QT):
                    n = QT * b + t
                    for half in range(2):
                        act.wait_ge(S["xtr_ready"], 2 * n + half + 1)
                        nc.scalar.copy(xattnT[:, n % 2, 4 * half:4 * half + 4, :],
                                       bank[6 + half][:, :].rearrange("p (k t) -> p k t", k=4)).then_inc(S["xtr_copied"], 1)
                act.wait_ge(S["x2T_ready"], b + 1)
                nc.scalar.copy(x2T[:, b * TB:(b + 1) * TB], bank[6 + b][:, :]).then_inc(S["x2T_copied"], 1)
                nc.scalar.copy(x2Tr[:, 0, b * TB:(b + 1) * TB], bank[6 + b][:, :]).then_inc(S["x2T_high"], 1)
            act.wait_ge(S["gate_exp_in"], 1)
            nc.scalar.activation(gatew[:, 1, :, :], gatew[:, 0, :, :], ACT.Exp).then_inc(S["gate_exp"], 1)

            act.wait_ge(S["bgh_ready"], 1)
            act.wait_ge(S["loaded_attn"], 32)

            def activations(e, half):
                for f in range(FT):
                    n = (2 * e + half) * FT + f
                    if n >= FT:
                        act.wait_ge(S["hidden_done"], n - FT + 1)
                    act.wait_ge(S["up_ready"], 2 * n + 1)
                    nc.scalar.activation(gelu[:, f, :], bank[2 * (f % 2)][:, :], ACT.Gelu,
                                         bias=bi[:, e, f:f + 1]).then_inc(S["gelu_done"], 1)
                    act.wait_ge(S["up_ready"], 2 * n + 2)
                    nc.scalar.activation(gate[:, f, :], bank[2 * (f % 2) + 1][:, :], ACT.Tanh,
                                         bias=bgh[:, e, f:f + 1], scale=0.5).then_inc(S["tanh_done"], 1)

            for e in range(NE):
                activations(e, 0)
                activations(e, 1)
            act.wait_ge(S["coefT_ready"], 1)
            nc.scalar.copy(coefT[0], bank[6][0:2 * NE, :]).then_inc(S["coefT_copied"], 1)
            nc.scalar.copy(coefT[1], bank[7][0:2 * NE, :]).then_inc(S["coefT_copied"], 1)
            act.wait_ge(S["acc_done"], 2 * NE + 1)
            act.dma_start(out.rearrange("(n p) d -> p n d", p=P), weighted).then_inc(S["stored"], 16)

        @block.gpsimd
        def _(pool):
            pads = [(ctx_pad[0:DE, :, :], 0.0), (wv[0:DE, :, XD:XD + 1], 0.0), (ctx_pad[DE:DE + 1, :, :], 0.0),
                    (wv[DE:DE + 1, :, :], 0.0), (ctx_pad[DE:DE + 1, :, P:P + KC], 1.0),
                    (wv[DE:DE + 1, :, XD:XD + 1], 1.0), (v_now[:, :, :, :, :], 0.0), (v_now[:, :, :, :, 8:9], 1.0)]
            for n, (region, value) in enumerate(pads):
                nc.gpsimd.memset(region, value).then_inc(S["pads_ready"], 1)
                pool.wait_ge(S["pads_ready"], n + 1)
            for n, (region, value) in enumerate(((ones_b, 1.0), (zeros_b, 0.0))):
                nc.gpsimd.memset(region, value).then_inc(S["consts_ready"], 1)
                pool.wait_ge(S["consts_ready"], n + 1)
            pool.wait_ge(S["v_copied"], NB)

            def body(i, c, q):
                if not has(i, i):
                    return
                at_least(pool, S["pv_done"], i, i - 1)
                for h in range(GH):
                    pool.wait_ge(S["exp_done"], UNITS * i + 3 * h + 1)
                    nc.gpsimd.tensor_copy(v_now[:, c % 2, h, :, 0:8],
                                          v_all[:, bass.ds(i, 1), h, :].rearrange("p s (h d) -> p (s h) d", h=2)
                                          ).then_inc(S["v_staged"], 1)
                    blocks = pr[c % 2][:, h, 0:TB].rearrange("p (j t) -> p j t", j=QT)
                    nc.gpsimd.affine_select(out=blocks, in_=blocks, compare_op=ALU.is_ge, fill=0.0, base=0,
                                            pattern=[[0, QT], [1, P]], channel_multiplier=-1).then_inc(S["masked"], 1)

            bodies(pool, body)

            def split(e):
                n = e % 2
                pool.wait_ge(w_loaded[n], 16 * (e // 2 + 1))
                if e >= 2:
                    pool.wait_ge(S["up_ready"], 4 * FT * (e - 1))
                for m in range(2):
                    nc.gpsimd.tensor_copy(w_split[n][:, 0, m, :], w_raw[n][:, m, :]).then_inc(S["split_done"], 1)
                pool.wait_ge(S["split_done"], 4 * e + 2)
                for m in range(2):
                    nc.gpsimd.tensor_tensor(w_split[n][:, 1, m, :], w_raw[n][:, m, :],
                                            w_split[n][:, 0, m, :].bitcast(F32), ALU.subtract).then_inc(S["split_done"], 1)

            def residual(e, half):
                n = 2 * e + half
                if half == 0:
                    pool.wait_ge(S[f"rows_loaded{e % 2}"], 16 * (e // 2 + 1))
                    nc.gpsimd.tensor_tensor(rows_e[:, e % 2, 1, :], rows_e[:, e % 2, 1, :], rows_e[:, e % 2, 1, :],
                                            ALU.add).then_inc(S["rows2_ready"], 1)
                    pool.wait_ge(S["rows2_ready"], e + 1)
                if n >= 2:
                    pool.wait_ge(S["down_taken"], n - 1)
                nc.gpsimd.tensor_tensor(xres[:, half, :].rearrange("p (n d) -> p n d", n=QT),
                                        x2d[:, half * QT:(half + 1) * QT, :],
                                        rows_e[:, e % 2, 1:2, :].broadcast_to([P, QT, D]),
                                        ALU.add).then_inc(S["xres_ready"], 1)

            def accumulate(e):
                pool.wait_ge(S["weighted_ready"], e + 1)
                for half in range(2):
                    own = slice(half * QT, (half + 1) * QT)
                    if e:
                        pool.wait_ge(S["acc_done"], 2 * e - 1 + half)
                    nc.gpsimd.tensor_tensor(acc[:, own, :], x2[:, own, :] if e == 0 else acc[:, own, :],
                                            weighted[:, own, :], ALU.add).then_inc(S["acc_done"], 1)

            split(0)
            pool.wait_ge(S["xst_ready"], NB * XT)
            pool.wait_ge(S["xpv_ready"], NT * XOB)
            pool.wait_ge(S["applied"], 1)
            residual(0, 0)
            residual(0, 1)
            split(1)
            for e in range(NE):
                if e:
                    if e + 1 < NE:
                        split(e + 1)
                    residual(e, 1)
                    accumulate(e - 1)
                if e + 1 < NE:
                    residual(e + 1, 0)
            accumulate(NE - 1)

        @block.vector
        def _(dve):
            count = [0]

            def link(ins):
                count[0] += 1
                ins.then_inc(S["dve_step"], 1)
                dve.wait_ge(S["dve_step"], count[0])

            def rsqrt(y, v, tmp):
                link(nc.vector.tensor_scalar(tmp.bitcast(I32), v.bitcast(I32), 1, None, ALU.logical_shift_right))
                link(nc.vector.tensor_scalar(y.bitcast(I32), tmp.bitcast(I32), -1.0, float(0x5F3759DF),
                                             ALU.mult, ALU.add))
                for _ in range(3):
                    link(nc.vector.tensor_tensor(tmp, y, y, ALU.mult))
                    link(nc.vector.scalar_tensor_tensor(out=tmp, in0=tmp, scalar=-0.5, in1=v, op0=ALU.mult, op1=ALU.mult))
                    link(nc.vector.scalar_tensor_tensor(out=y, in0=tmp, scalar=1.5, in1=y, op0=ALU.add, op1=ALU.mult))

            def statistics(src, tiles, mv, stats):
                for t in range(tiles):
                    ins = nc.vector.bn_stats(stats[:, t, :], src[:, t, :])
                    if t == tiles - 1:
                        link(ins)
                for t in range(tiles):
                    ins = nc.vector.bn_aggr(mv[:, t, :], stats[:, t, :])
                    if t == tiles - 1:
                        link(ins)

            def layer_norm(dst, src, tiles):
                stats = small[:, 0, 0:6 * tiles].rearrange("p (n c) -> p n c", c=6)
                mv = small[:, 1, 0:2 * tiles].rearrange("p (n c) -> p n c", c=2)
                v, y, tmp = small[:, 2, 0:tiles], small[:, 3, 0:tiles], small[:, 4, 0:tiles]
                statistics(src, tiles, mv, stats)
                link(nc.vector.tensor_scalar(v, mv[:, :, 1], LN_EPS, None, ALU.add))
                rsqrt(y, v, tmp)
                for t in range(tiles):
                    ins = nc.vector.tensor_scalar(dst[:, t, :], src[:, t, :], mv[:, t, 0:1], y[:, t:t + 1],
                                                  ALU.subtract, ALU.mult)
                return ins

            nc.vector.memset(x2_both[:, :], 0.0).then_inc(S["zeroed"], 1)
            for b in range(NB):
                for o in range(2):
                    own = slice(b * TB, (b + 1) * TB)
                    n = 2 * b + o
                    dve.wait_ge(S["high_ready"], n + 1)
                    link(nc.vector.scalar_tensor_tensor(out=rest[:, o, :], in0=bank[n][:, :], scalar=[0.25, 1.0][o],
                                                        in1=parts[:, o, 0, own], op0=ALU.mult, op1=ALU.subtract))
                    nc.vector.tensor_copy(parts[:, o, 1, own], rest[:, o, :]).then_inc(S["parts_ready"], 1)
                    dve.wait_ge(S["parts_ready"], 2 * n + 1)
                    nc.vector.tensor_tensor(parts[:, o, 2, own], rest[:, o, :], parts[:, o, 1, own],
                                            ALU.subtract).then_inc(S["parts_ready"], 1)
            dve.wait_ge(S["loaded_attn"], 32)
            lv = lambdas
            link(nc.vector.tensor_tensor(small[:, 0, 0:8].rearrange("p (a d) -> p a d", a=2), lv[:, :, 0, :],
                                         lv[:, :, 1, :], ALU.mult))
            nc.vector.tensor_reduce(lam[:, 0:2], small[:, 0, 0:8].rearrange("p (a d) -> p a d", a=2), AX.X,
                                    ALU.add).then_inc(S["lam_in"], 1)
            link(nc.vector.tensor_scalar(scaled_proj[:, :], w_proj, gamma_col, 1.0 - LAMBDA_INIT,
                                         ALU.mult, ALU.mult))
            dve.wait_ge(S["lam_exp"], 1)
            link(nc.vector.tensor_tensor(lam[:, 4:5], lam[:, 3:4], lam[:, 2:3], ALU.subtract))
            link(nc.vector.tensor_scalar(lam[:, 5:6], lam[:, 4:5], -LAMBDA_INIT, None, ALU.add))
            for n in range(NB * XCH):
                b, c = divmod(n, XCH)
                high, w = fold_heads(0, b, c)
                dve.wait_ge(S["fold_high"], n + 1)
                nc.vector.scalar_tensor_tensor(out=fold_heads(1, b, c)[0],
                                               in0=bank[6 + n % 2][:, 0:w * KC].rearrange("p (h s) -> p h s", h=w),
                                               scalar=0.125, in1=high.bitcast(F32), op0=ALU.mult,
                                               op1=ALU.subtract).then_inc(S["fold_low"], 1)
            nc.vector.memset(fold[:, :, :, XCOLS:XPAD].bitcast(F32), 0.0).then_inc(S["fold_low"], 1)

            def head_math(i, c, u):
                o = bank[7][:, :].rearrange("p (i g d) -> p i g d", i=QT, g=GH)
                val = head_val[:, c % 2, :, :, :]
                if u == 7:
                    dve.wait_ge(S["otr_done"], i - 1)
                    nc.vector.reciprocal(head_inv[:, :, :], o[:, :, :, 8]).then_inc(S["head_inv_done"], 1)
                if u == 8:
                    odd = head_inv[:, :, :].rearrange("p i (h two) -> p (i h) two", two=2)[:, :, 1:2]
                    dve.wait_ge(S["head_inv_done"], i - 1)
                    nc.vector.tensor_scalar(odd, odd, lam[:, 5:6], None, ALU.mult).then_inc(S["head_scaled"], 1)
                if u == 9:
                    dve.wait_ge(S["head_scaled"], i - 1)
                    nc.vector.tensor_tensor(val.rearrange("p i g d -> p (i g) d"),
                                            o[:, :, :, 0:8].rearrange("p i g d -> p (i g) d"),
                                            head_inv[:, :, :].rearrange("p i g -> p (i g)").unsqueeze(2)
                                            .broadcast_to([P, QT * GH, 8]), ALU.mult).then_inc(S["head_taken"], 1)
                if u == 10:
                    pair = val.rearrange("p i (h two) d -> p (i h) two d", two=2)
                    dve.wait_ge(S["head_taken"], i - 1)
                    nc.vector.tensor_tensor(
                        attn[:, bass.ds(i - 2, 1), :, :].rearrange("p s i (h d) -> p (s i h) d", h=2),
                        pair[:, :, 0, :], pair[:, :, 1, :], ALU.add).then_inc(S["head_done"], 1)

            def body(i, c, q):
                if has(i, i + 2):
                    at_least(dve, S["rows_ready"], i, i + 1)
                m = neg_max[:, c % 2, :, :]
                for u in range(UNITS):
                    h, part = divmod(u, 3)
                    if has(i, i + 2):
                        dve.wait_ge(S["max_ready"], UNITS * (i + 2) + u + 1)
                        for qt, col in MAX_PARTS[part]:
                            ins = nc.vector.tensor_reduce(m[:, h, qt:qt + 1], bank[part][:, col:col + (qt + 1) * P],
                                                          AX.X, ALU.max, negate=True)
                        ins.then_inc(S["max_taken"], 1)
                    if u == 2 and has(i, i + 1):
                        dve.wait_ge(S["rows_ready"], i + 2)
                        if has(i, i - 1):
                            dve.wait_ge(shift_loaded[(c - 1) % 4], 16 * SHIFT_ROWS * (turn_of(q, c, -1) + 1))
                        nc.vector.tensor_copy(max_rows[:, (c + 1) % 2, :],
                                              bank[7][0:32, 0:64].bitcast(BF16)).then_inc(S["rows_copied"], 1)
                    if has(i, i - 2):
                        head_math(i, c, u)
                if has(i, i + 2):
                    dve.wait_ge(S["max_taken"], UNITS * (i + 3))
                    nc.vector.tensor_copy(neg_maxb[:, c % 2, 0, :, :], m).then_inc(S["neg_high"], 1)
                    dve.wait_ge(S["neg_high"], i + 3)
                    nc.vector.tensor_tensor(neg_maxb[:, c % 2, 1, :, :], m, neg_maxb[:, c % 2, 0, :, :],
                                            ALU.subtract).then_inc(S["neg_low"], 1)

            bodies(dve, body)

            dve.wait_ge(S["head_done"], STEPS)
            heads = STEPS * QT * 2
            ms, v, y, tmp = (small[:, n, 0:heads] for n in (1, 2, 3, 4))
            flat = wqT[:, :, :].rearrange("p a b -> p (a b)")
            link(nc.vector.tensor_tensor(squares, flat, flat, ALU.mult))
            link(nc.vector.tensor_reduce(ms, squares.rearrange("p (n d) -> p n d", d=8), AX.X, ALU.add))
            link(nc.vector.tensor_scalar(v, ms, 0.125, RMS_EPS, ALU.mult, ALU.add))
            rsqrt(y, v, tmp)
            roots = y.rearrange("p (s i h) -> p s i h", s=STEPS, i=QT)
            for b in range(NB):
                for t in range(QT):
                    ins = nc.vector.tensor_tensor(
                        attn_rms[:, b * QT + t, :].rearrange("p (g h d) -> p g h d", g=NG, h=2),
                        attn[:, b * NG:(b + 1) * NG, t, :].rearrange("p g (h d) -> p g h d", h=2),
                        roots[:, b * NG:(b + 1) * NG, t, :].unsqueeze(3).broadcast_to([P, NG, 2, 8]), ALU.mult)
                ins.then_inc(S["attn_ready"], 1)
            dve.wait_ge(S["loaded_tok"], 48)

            def first_norm(b):
                own = slice(b * QT, (b + 1) * QT)
                dve.wait_ge(S["proj_ready"], b + 1)
                link(nc.vector.tensor_tensor(x1[:, own, :], bank[4 + b][:, :].rearrange("p (n d) -> p n d", n=QT),
                                             x_tok[:, own, :], ALU.add))
                layer_norm(x1[:, own, :], x1[:, own, :], QT).then_inc(S["x1_ready"], 1)

            def low_part(b):
                dve.wait_ge(S["x1T_high"], b + 1)
                nc.vector.tensor_tensor(x1T[:, 1, b * TB:(b + 1) * TB], bank[6 + b][:, :],
                                        x1T[:, 0, b * TB:(b + 1) * TB].bitcast(F32),
                                        ALU.subtract).then_inc(S["x1T_low"], 1)

            first_norm(0)
            first_norm(1)
            low_part(0)
            low_part(1)

            for n in range(NT):
                if n >= 2:
                    dve.wait_ge(S["xrows_ready"], n - 1)
                for c in range(XCH):
                    w = min(HPC, XH - HPC * c)
                    m = XCH * n + c
                    dve.wait_ge(S["xmax_ready"], m + 1)
                    nc.vector.tensor_reduce(xneg[:, n % 2, HPC * c:HPC * c + w],
                                            bank[MAX_RING[m % 3]][:, 0:w * KC].rearrange("p (h s) -> p h s", s=KC),
                                            AX.X, ALU.max, negate=True).then_inc(S["xmax_taken"], 1)
                dve.wait_ge(S["xmax_taken"], XCH * (n + 1))
                link(nc.vector.tensor_copy(xnegb[:, n % 2, 0, :], xneg[:, n % 2, :]))
                nc.vector.tensor_tensor(xnegb[:, n % 2, 1, :], xneg[:, n % 2, :], xnegb[:, n % 2, 0, :],
                                        ALU.subtract).then_inc(S["xneg_done"], 1)
            for t in range(NT):
                ins = nc.vector.tensor_tensor(x1[:, t, :], x1[:, t, :], bo_bc, ALU.add)
            link(ins)

            rec = xmax_free
            for b in range(NB):
                for t in range(QT):
                    n = QT * b + t
                    if n >= 2:
                        dve.wait_ge(S["xtr_ready"], 2 * (n - 1))
                    for c in range(XOB):
                        w = min(HPO, XH - HPO * c)
                        own = slice(HPO * c, HPO * c + w)
                        dve.wait_ge(S["xpv_ready"], XOB * n + c + 1)
                        o = bank[3 + c][:, 0:65 * w].rearrange("p (h d) -> p h d", h=w)
                        link(nc.vector.reciprocal(rec[:, n % 2, own], o[:, :, 64]))
                        nc.vector.tensor_tensor(xattn[:, n % 2, :].rearrange("p (h d) -> p h d", h=XH)[:, own, :],
                                                o[:, :, 0:64],
                                                rec[:, n % 2, own].unsqueeze(2).broadcast_to([P, w, 64]),
                                                ALU.mult).then_inc(S["xnorm_done"], 1)
                own = slice(b * QT, (b + 1) * QT)
                dve.wait_ge(S["xproj_ready"], QT * (b + 1))
                link(nc.vector.tensor_tensor(x2[:, own, :], bank[b][:, :].rearrange("p (n d) -> p n d", n=QT),
                                             x1[:, own, :], ALU.add))
                layer_norm(x2[:, own, :], x2[:, own, :], QT).then_inc(S["x2_ready"], 1)
                dve.wait_ge(S["x2T_high"], b + 1)
                nc.vector.tensor_tensor(x2Tr[:, 1, b * TB:(b + 1) * TB], bank[6 + b][:, :],
                                        x2Tr[:, 0, b * TB:(b + 1) * TB].bitcast(F32),
                                        ALU.subtract).then_inc(S["x2T_low"], 1)
            dve.wait_ge(S["xtr_ready"], 2 * NT)
            dve.wait_ge(S["x2_ready"], NB)
            nc.vector.tensor_scalar(x2d, x2, 2.0, None, ALU.mult).then_inc(S["applied"], 1)
            nc.vector.tensor_scalar(bgh[:, :, :], bg, 0.5, None, ALU.mult).then_inc(S["bgh_ready"], 1)

            G = [gatew[:, s, :, :] for s in range(8)]
            row = small[:, 5, :].rearrange("p (s n) -> p s n", s=NT * XH // NT)

            def over(v):
                return v.unsqueeze(2).broadcast_to([P, NT, NE])

            dve.wait_ge(S["logits_ready"], 1)
            link(nc.vector.tensor_tensor(G[2], bank[5][:, 0:NT * NE].rearrange("p (n e) -> p n e", n=NT),
                                         br_bc.unsqueeze(1).broadcast_to([P, NT, NE]), ALU.add))
            link(nc.vector.tensor_reduce(row[:, 0, :], G[2], AX.X, ALU.max))
            nc.vector.tensor_tensor(G[0], G[2], over(row[:, 0, :]), ALU.subtract).then_inc(S["gate_exp_in"], 1)
            dve.wait_ge(S["gate_exp"], 1)

            def pick(probabilities, at, chosen, tmp):
                link(nc.vector.tensor_reduce(row[:, at, :], probabilities, AX.X, ALU.max))
                link(nc.vector.tensor_tensor(tmp, probabilities, over(row[:, at, :]), ALU.is_equal))
                link(nc.vector.tensor_tensor(tmp, tmp, ranks.unsqueeze(1).broadcast_to([P, NT, NE]), ALU.mult))
                link(nc.vector.tensor_reduce(row[:, 5, :], tmp, AX.X, ALU.max))
                link(nc.vector.tensor_tensor(chosen, tmp, over(row[:, 5, :]), ALU.is_equal))

            def top_two():
                link(nc.vector.tensor_reduce(row[:, 1, :], G[1], AX.X, ALU.add))
                link(nc.vector.reciprocal(row[:, 2, :], row[:, 1, :]))
                link(nc.vector.tensor_tensor(G[2], G[1], over(row[:, 2, :]), ALU.mult))

                pick(G[2], 3, G[3], G[4])
                link(nc.vector.scalar_tensor_tensor(out=G[5], in0=G[3], scalar=-2.0, in1=G[2], op0=ALU.mult, op1=ALU.add))
                pick(G[5], 4, G[6], G[4])
                link(nc.vector.tensor_tensor(row[:, 6, :], row[:, 3, :], row[:, 4, :], ALU.add))
                link(nc.vector.reciprocal(row[:, 7, :], row[:, 6, :]))
                link(nc.vector.tensor_tensor(G[3], G[3], G[6], ALU.add))
                link(nc.vector.tensor_tensor(G[3], G[3], G[2], ALU.mult))
                link(nc.vector.tensor_tensor(coef[:, :, NE:2 * NE], G[3], over(row[:, 7, :]), ALU.mult))

            stats = small[:, 0, 0:6 * NT].rearrange("p (n c) -> p n c", c=6)
            mv = small[:, 1, 0:2 * NT].rearrange("p (n c) -> p n c", c=2)
            v, y, tmp = small[:, 2, 0:NT], small[:, 3, 0:NT], small[:, 4, 0:NT]

            def gated(e, half, f):
                n = (2 * e + half) * FT + f
                if f == 0 and e:
                    dve.wait_ge(S["down_ready"], 2 * e - 1 + half)
                dve.wait_ge(S["tanh_done"], n + 1)
                nc.vector.scalar_tensor_tensor(out=hidden[half][:, f, :], in0=gate[:, f, :], scalar=1.0,
                                               in1=gelu[:, f, :], op0=ALU.add, op1=ALU.mult).then_inc(S["hidden_done"], 1)

            def take(e, half):
                n = 2 * e + half
                own = slice(half * QT, (half + 1) * QT)
                r = res[e % 2]
                dve.wait_ge(S["down_ready"], n + 1)
                dve.wait_ge(S["xres_ready"], n + 1)
                nc.vector.tensor_tensor(r[:, own, :], bank[4 + half][:, :].rearrange("p (n d) -> p n d", n=QT),
                                        xres[:, half, :].rearrange("p (n d) -> p n d", n=QT),
                                        ALU.add).then_inc(S["down_taken"], 1)
                dve.wait_ge(S["down_taken"], n + 1)
                statistics(r[:, own, :], QT, mv[:, own, :], stats[:, own, :])

            def root():
                link(nc.vector.tensor_scalar(v, mv[:, :, 1], 4 * EXPERT_EPS, None, ALU.add))
                rsqrt(y, v, tmp)

            def apply(e):
                link(nc.vector.tensor_tensor(row[:, 0, :], y, coef[:, :, NE + e], ALU.mult))
                link(nc.vector.scalar_tensor_tensor(out=coef[:, :, e], in0=mv[:, :, 0], scalar=-1.0, in1=row[:, 0, :],
                                                    op0=ALU.mult, op1=ALU.mult))
                if e:
                    dve.wait_ge(S["acc_done"], 2 * e)
                for t in range(NT):
                    ins = nc.vector.scalar_tensor_tensor(out=weighted[:, t, :], in0=res[e % 2][:, t, :],
                                                         scalar=row[:, 0, t:t + 1], in1=rows_e[:, e % 2, 0, :],
                                                         op0=ALU.mult, op1=ALU.mult)
                ins.then_inc(S["weighted_ready"], 1)

            for e in range(NE):
                gated(e, 0, 0)
                gated(e, 0, 1)
                if e == 0:
                    top_two()
                if e:
                    take(e - 1, 1)
                gated(e, 0, 2)
                gated(e, 0, 3)
                if e:
                    root()
                gated(e, 1, 0)
                if e:
                    apply(e - 1)
                gated(e, 1, 1)
                gated(e, 1, 2)
                take(e, 0)
                gated(e, 1, 3)
            take(NE - 1, 1)
            root()
            apply(NE - 1)
            dve.wait_ge(S["weighted_ready"], NE)
            dve.wait_ge(S["dve_step"], count[0])
            nc.vector.tensor_copy(small[:, 5, 120:121], coef[:, 0, 0:1]).then_inc(S["coef_ready"], 1)
            dve.wait_ge(S["corr_ready"], 1)
            dve.wait_ge(S["acc_done"], 2 * NE)
            for half in range(2):
                own = slice(half * QT, (half + 1) * QT)
                link(nc.vector.tensor_tensor(weighted[:, own, :], bank[4 + half][:, :].rearrange("p (n d) -> p n d", n=QT),
                                             acc[:, own, :], ALU.add))
            layer_norm(weighted, weighted, NT).then_inc(S["acc_done"], 1)


        @block.tensor
        def _(pe):
            pe.wait_ge(S["loaded_x"], 32)
            for b in range(NB):
                if b:
                    pe.wait_ge(S["loaded_x1"], 16)
                for o in range(2):
                    nc.tensor.matmul(bank[2 * b + o][:, :], w_attn[:, o * D:(o + 1) * D], xT[:, b * TB:(b + 1) * TB],
                                     start=True, stop=True).then_inc(S["qk_ready"], 1)
            for b in range(NB):
                for j in range(QT):
                    n = b * QT + j
                    ins = nc.tensor.matmul(bank[4 + b][:, j * D:(j + 1) * D], xT[:, n * P:(n + 1) * P],
                                           w_attn[:, 2 * D:3 * D], start=True, stop=True)
                ins.then_inc(S["v_ready"], 1)
            pe.wait_ge(S["loaded_cross"], 16 * 3)
            for n in range(XH // 2):
                if n >= 2:
                    pe.wait_ge(S["kt_copied"], n - 1)
                nc.tensor.matmul(bank[6 + n % 2][:, 0:NB * KC], wk[:, n * P:(n + 1) * P],
                                 ctx_pad[0:DE, :, P:P + KC], start=True, stop=True).then_inc(S["kt_ready"], 1)
            pe.wait_ge(S["kt_copied"], XH // 2)
            for n in range(NB * XCH):
                b, c = divmod(n, XCH)
                if n >= 2:
                    pe.wait_ge(S["fold_low"], n - 1)
                for m, h in enumerate(range(XH)[FOLD_HEADS[c]]):
                    at = (h % 2) * XD
                    ins = nc.tensor.matmul(bank[6 + n % 2][:, m * KC:(m + 1) * KC],
                                           wqT[at:at + XD, h // 2, :], kT[at:at + XD, h // 2, b * KC:(b + 1) * KC],
                                           start=True, stop=True)
                ins.then_inc(S["fold_ready"], 1)
            pe.wait_ge(S["loaded_const"], 16 * 2)
            pe.wait_ge(S["loaded_attn"], 32)
            pe.wait_ge(S["parts_ready"], 8)
            pe.wait_ge(S["v_copied"], NB)
            pe.wait_ge(S["fold_low"], NB * XCH)
            pe.wait_ge(S["pads_ready"], 8)

            def max_unit(i, c, q, u):
                b = (c + 2) % 4
                if u == 0:
                    pe.wait_ge(stack_loaded[b], 16 * (turn_of(q, c, 2) + 1))
                h, part = divmod(u, 3)
                own = slice(HEAD_ROWS * h, HEAD_ROWS * (h + 1))
                at_least(pe, S["max_taken"], i, UNITS * (i + 2) + u - 2)
                for n, (qt, col) in enumerate(MAX_PARTS[part]):
                    nc.tensor.matmul(bank[part][:, col:col + (qt + 1) * P], stacks[own, b, 0, qt * P:(qt + 1) * P],
                                     stacks[own, b, 1, 0:(qt + 1) * P], start=(n == 0), stop=False,
                                     skip_group_check=True)
                for qt, col in MAX_PARTS[part]:
                    ins = nc.tensor.matmul(bank[part][:, col + qt * P:col + (qt + 1) * P], identb[:, :], maskb[:, :],
                                           start=False, stop=True, skip_group_check=True)
                ins.then_inc(S["max_ready"], 1)

            def score_unit(i, c, q, u):
                b = c % 4
                if u == 0:
                    pe.wait_ge(shift_loaded[b], 16 * SHIFT_ROWS * (turn_of(q, c, 0) + 1))
                if u == 0:
                    pe.wait_ge(alone_loaded[c % 2], 16 * GH * (2 * q + c // 2 + 1))
                h, part = divmod(u, 3)
                at_least(pe, S["exp_done"], i, UNITS * i + u - 2)
                for n, (j, t, k, col) in enumerate(EXP_PARTS[part]):
                    ins = nc.tensor.matmul(bank[3 + part][:, col:col + k * P], k_alone[:, c % 2, h, j * P:(j + 1) * P],
                                           stacks[:, b, 0, t * P:(t + k) * P], start=(n == 0), stop=True,
                                           skip_group_check=True)
                ins.then_inc(S["st_ready"], 1)

            def value_block(i, c, n):
                j, t, k, col = VALUE_BLOCKS[n]
                p = (c - 1) % 2
                if n == 0:
                    pe.wait_ge(S["masked"], GH * i)
                    pe.wait_ge(S["exp_done"], UNITS * i)
                    pe.wait_ge(S["v_staged"], QT * i)
                    at_least(pe, S["ot_copied"], i, i - 1)
                for h in range(GH):
                    ins = nc.tensor.matmul(bank[6][32 * h:32 * h + 32, t * P:(t + k) * P], v_now[:, p, j, h // 2, :],
                                           pr[p][:, h, col:col + k * P], start=(n == 0),
                                           stop=(n == len(VALUE_BLOCKS) - 1),
                                           skip_group_check=True)
                if n == len(VALUE_BLOCKS) - 1:
                    ins.then_inc(S["pv_done"], 1)

            def body(i, c, q):
                for u in range(UNITS):
                    if has(i, i + 2):
                        max_unit(i, c, q, u)
                    if u == 1 and has(i, i + 1):
                        pe.wait_ge(S["neg_low"], i + 2)
                        nc.tensor.transpose(bank[7][0:32, 0:64].bitcast(BF16),
                                            neg_maxb[:, (c + 1) % 2, :, :, :].rearrange("p a h i -> p (a h i)"),
                                            identb[:, :]).then_inc(S["rows_ready"], 1)
                    if has(i, i):
                        score_unit(i, c, q, u)
                    if has(i, i - 1) and u in VALUE_AT:
                        value_block(i, c, VALUE_AT.index(u))
                    if u == 6 and has(i, i - 2):
                        pe.wait_ge(S["ot_copied"], i - 1)
                        if has(i, i + 1):
                            pe.wait_ge(S["rows_copied"], i + 2)
                        else:
                            pe.wait_ge(S["head_taken"], i - 2)
                        for t in range(QT):
                            ins = nc.tensor.transpose(bank[7][:, t * P:(t + 1) * P], out_t[c % 2][:, t * P:(t + 1) * P],
                                                      ident)
                        ins.then_inc(S["otr_done"], 1)

            bodies(pe, body)

            pe.wait_ge(S["loaded_wv"], 16)
            for n in range(NB * 7):
                b, g = divmod(n, 7)
                if n >= 2:
                    pe.wait_ge(S["vb_copied"], n - 1)
                to = bank[n % 2]
                for m, k in enumerate(range(3 * g, min(3 * g + 3, XT))):
                    for s in range(2):
                        h = segments(k)[0] + s
                        at = max(P + k * P - KC * h, 0)
                        h = min(h, XH - 1)
                        ins = nc.tensor.matmul(to[:, 130 * m + 65 * s:130 * m + 65 * s + 65],
                                               ctx_pad[:, b, at:at + P],
                                               wv[:, h, :], start=True, stop=True)
                ins.then_inc(S["vb_ready"], 1)
            for b in range(NB):
                pe.wait_ge(S["attn_ready"], b + 1)
                for t in range(QT):
                    ins = nc.tensor.transpose(bank[2 + b][:, t * P:(t + 1) * P], attn_rms[:, b * QT + t, :], ident)
                ins.then_inc(S["attnT_ready"], 1)
                pe.wait_ge(S["attnT_copied"], b + 1)
                for t in range(QT):
                    ins = nc.tensor.matmul(bank[4 + b][:, t * D:(t + 1) * D], out_t[b][:, t * P:(t + 1) * P],
                                           scaled_proj[:, :], start=True, stop=True)
                ins.then_inc(S["proj_ready"], 1)
            for b in range(NB):
                pe.wait_ge(S["x1_ready"], b + 1)
                for t in range(QT):
                    ins = nc.tensor.transpose(bank[6 + b][:, t * P:(t + 1) * P], x1[:, b * QT + t, :], ident)
                ins.then_inc(S["x1T_ready"], 1)

            pe.wait_ge(S["vb_copied"], NB * 7)
            pe.wait_ge(S["x1T_high"], NB)

            def max_tile_rows(n):
                pe.wait_ge(S["xneg_done"], n + 1)
                if n < 2:
                    pe.wait_ge(S["x1T_low"], NB)
                else:
                    pe.wait_ge(S["xrows_copied"], n - 1)
                nc.tensor.transpose(bank[6 + n % 2][0:32, 0:64].bitcast(BF16),
                                    xnegb[:, n % 2, :, :].rearrange("p a h -> p (a h)"),
                                    identb[:, :]).then_inc(S["xrows_ready"], 1)

            def max_chunk(m):
                n, c = divmod(m, XCH)
                w = min(HPC, XH - HPC * c) * KC
                if m >= 3:
                    pe.wait_ge(S["xmax_taken"], m - 2)
                nc.tensor.matmul(bank[MAX_RING[m % 3]][:, 0:w], x1T[:, 0, n * P:(n + 1) * P],
                                 fold[:, 0, n // QT, HPC * KC * c:HPC * KC * c + w],
                                 start=True, stop=True).then_inc(S["xmax_ready"], 1)
                if c == 2 and n % QT:
                    max_tile_rows(n - 1)

            for m in range(QT * XCH):
                max_chunk(m)
            pe.wait_ge(S["ind_loaded"], 16)

            def cross_transposes(n):
                if n == 0:
                    pe.wait_ge(S["xrows_copied"], NT)
                for half in range(2):
                    pe.wait_ge(S["xnorm_done"], XOB * (n + 1))
                    if n:
                        pe.wait_ge(S["xtr_copied"], 2 * n - 1 + half)
                    if n == QT:
                        pe.wait_ge(S["x2T_low"], 1)
                    for k in range(4):
                        ins = nc.tensor.transpose(bank[6 + half][:, k * P:(k + 1) * P],
                                                  xattn[:, n % 2, (4 * half + k) * P:(4 * half + k + 1) * P], ident)
                    ins.then_inc(S["xtr_ready"], 1)

            def cross_projection(n):
                pe.wait_ge(S["xtr_copied"], 2 * n + 2)
                to = bank[n // QT]
                for k in range(XH // 2):
                    ins = nc.tensor.matmul(to[:, (n % QT) * D:(n % QT + 1) * D], xattnT[:, n % 2, k, :], wo[:, k, :],
                                           start=(k == 0), stop=(k == XH // 2 - 1))
                ins.then_inc(S["xproj_ready"], 1)

            for b in range(NB):
                if b == 0:
                    max_tile_rows(QT - 1)
                    max_chunk(QT * XCH)
                for k in range(XT):
                    m = XT * b + k
                    if k == 0:
                        pe.wait_ge(S["xrows_copied"], QT * (b + 1))
                        pe.wait_ge(S["x1T_low"], b + 1)
                        if b:
                            pe.wait_ge(S["xnorm_done"], QT * XOB * b)
                    if m >= 3:
                        pe.wait_ge(S["xexp_done"], m - 2)
                    to = bank[SCORE_RING[m % 3]][:, :]
                    cols = slice(k * P, (k + 1) * P)
                    tok = slice(b * TB, (b + 1) * TB)
                    nc.tensor.matmul(to, fold[:, 0, b, cols], x1T[:, 0, tok], start=True, stop=False)
                    nc.tensor.matmul(to, fold[:, 0, b, cols], x1T[:, 1, tok], start=False, stop=False)
                    nc.tensor.matmul(to, fold[:, 1, b, cols], x1T[:, 0, tok], start=False, stop=False)
                    nc.tensor.matmul(to, indicator[:, cols], xneg_rows[:, b, :], start=False,
                                     stop=True).then_inc(S["xst_ready"], 1)
                    if b == 0:
                        for m in SECOND_MAX[k]:
                            max_chunk(m)
                if b == 0:
                    max_tile_rows(NT - 1)
                    pe.wait_ge(S["xmax_taken"], NT * XCH)
                pe.wait_ge(S["xexp_done"], XT * (b + 1))
                for t in range(QT):
                    n = QT * b + t
                    started, done = [], [max(k for k in range(XT) for h in segments(k) if h // HPO == c)
                                         for c in range(XOB)]
                    for k in range(XT):
                        for first, heads, c in OUTPUT_RUNS[k]:
                            if c not in started and n:
                                pe.wait_ge(S["xnorm_done"], XOB * (n - 1) + c + 1)
                            at = 65 * (segments(k)[first] % HPO)
                            ins = nc.tensor.matmul(bank[3 + c][:, at:at + 65 * heads],
                                                   xprobs[:, k, t * P:(t + 1) * P],
                                                   vblock[:, b, k, 65 * first:65 * (first + heads)],
                                                   start=c not in started, stop=k == done[c], skip_group_check=True)
                            started.append(c)
                            if k == done[c]:
                                ins.then_inc(S["xpv_ready"], 1)
                    if t:
                        cross_projection(n - 1)
                    cross_transposes(n)
                cross_projection(QT * b + QT - 1)
                pe.wait_ge(S["x2_ready"], b + 1)
                for t in range(QT):
                    ins = nc.tensor.transpose(bank[6 + b][:, t * P:(t + 1) * P], x2[:, QT * b + t, :], ident)
                ins.then_inc(S["x2T_ready"], 1)

            pe.wait_ge(S["x2T_copied"], NB)
            pe.wait_ge(S["xnorm_done"], NT * XOB)
            for n in range(NT):
                ins = nc.tensor.matmul(bank[5][:, n * NE:(n + 1) * NE], x2T[:, n * P:(n + 1) * P], wr,
                                       start=True, stop=True)
            ins.then_inc(S["logits_ready"], 1)
            pe.wait_ge(S["x2T_low"], NB)

            def up(e, half):
                tok = slice(half * TB, (half + 1) * TB)
                if half == 0:
                    pe.wait_ge(S["split_done"], 4 * (e + 1))
                for f in range(FT):
                    cols = slice(f * P, (f + 1) * P)
                    n = (2 * e + half) * FT + f
                    for m in range(2):
                        to = bank[2 * (f % 2) + m][:, :]
                        if n >= 2:
                            pe.wait_ge([S["gelu_done"], S["tanh_done"]][m], n - 1)
                        w = w_split[e % 2]
                        nc.tensor.matmul(to, w[:, 0, m, cols], x2Tr[:, 0, tok], start=True, stop=False)
                        nc.tensor.matmul(to, w[:, 0, m, cols], x2Tr[:, 1, tok], start=False, stop=False)
                        nc.tensor.matmul(to, w[:, 1, m, cols], x2Tr[:, 0, tok], start=False,
                                         stop=True).then_inc(S["up_ready"], 1)

            def down(e, half):
                n = 2 * e + half
                if n >= 2:
                    pe.wait_ge(S["down_taken"], n - 1)
                else:
                    pe.wait_ge(S["gate_exp_in"], 1)
                pe.wait_ge(S[f"wo_loaded{e % 2}"], 16 * (e // 2 + 1))
                pe.wait_ge(S["hidden_done"], FT * (n + 1))
                for t in range(QT):
                    for f in range(FT):
                        ins = nc.tensor.matmul(bank[4 + half][:, t * D:(t + 1) * D], hidden[half][:, f, t * P:(t + 1) * P],
                                               wo_e[:, e % 2, f, :], start=(f == 0), stop=(f == FT - 1))
                ins.then_inc(S["down_ready"], 1)

            for e in range(NE):
                up(e, 0)
                if e:
                    down(e - 1, 1)
                up(e, 1)
                down(e, 0)
            down(NE - 1, 1)
            pe.wait_ge(S["coef_ready"], 1)
            for n in range(NT):
                ins = nc.tensor.transpose(bank[6 + n // QT][0:2 * NE, (n % QT) * P:(n % QT + 1) * P], coef[:, n, :],
                                          ident)
            ins.then_inc(S["coefT_ready"], 1)
            pe.wait_ge(S["coefT_copied"], 2)
            pe.wait_ge(S["down_taken"], 2 * NE)
            for n in range(NT):
                ins = nc.tensor.matmul(bank[4 + n // QT][:, (n % QT) * D:(n % QT + 1) * D], coefT[n // QT][:, (n % QT) * P:(n % QT + 1) * P],
                                       gamma_beta[:, :], start=True, stop=True)
            ins.then_inc(S["corr_ready"], 1)


def kernel(**inputs):
    import concourse.bacc as bacc
    from concourse.bass_utils import run_bass_kernel_spmd
    import ml_dtypes

    a = {k: np.asarray(v) for k, v in inputs.items()}
    pre, xa, ff = "L0_attn_", "L0_xattn_", "L0_ffn_"
    x = a["x"].reshape(T, D)
    row = np.arange(XPAD)
    head = np.arange(XH)[:, None]
    hot = ((row // KC == head) & (row < XCOLS))
    layout = {
        "x": x, "xT": x.T,
        "columns": np.concatenate([
            np.eye(P, dtype=np.float32), a[pre + "w_proj"],
            *(a[ff + n].reshape(NE, FT, P).transpose(2, 0, 1).reshape(P, NE * FT) for n in ("bi", "bg")),
            a[ff + "Wr"], np.tile(a[pre + "gamma"], D // (2 * HD))[:, None]], axis=1),
        "rows_bc": np.concatenate([a[pre + "lambda_" + n] for n in ("q1", "k1", "q2", "k2")] + [
            a[ff + "br"], np.arange(NE, 0, -1, dtype=np.float32), a[xa + "bo"]])[None],
        "ctxT": a["ctx_768"].transpose(2, 0, 1),
        "w_attn": a[pre + "w_attn"],
        "wk": a[xa + "Wk"], "wv": a[xa + "Wv"], "wqT": a[xa + "Wq"].T, "wo": a[xa + "Wo"],
        "Wig": np.stack([a[ff + "Wi"], a[ff + "Wg"]], axis=2), "Wo_e": a[ff + "Wo"],
        "rows_e": np.stack([a[ff + "gamma"], a[ff + "bo"]], axis=1),
        "gamma_beta": np.concatenate([a[ff + "gamma"], a[ff + "beta"]]),
        "identb": np.eye(P).astype(ml_dtypes.bfloat16),
        "maskb": np.triu(np.full((P, P), -3e38), 1).astype(ml_dtypes.bfloat16),
        "indicator": np.concatenate([hot, hot]).astype(ml_dtypes.bfloat16),
    }
    nc = bacc.Bacc("TRN2", target_bir_lowering=False, num_devices=1)
    arrays, aps = {}, {}
    for name, v in layout.items():
        v = np.ascontiguousarray(v)
        arrays[f"in_{name}"] = v
        aps[name] = nc.dram_tensor(f"in_{name}", v.shape, mybir.dt.from_np(v.dtype), kind="ExternalInput").ap()
    out = nc.dram_tensor("out_x", [T, D], F32, kind="ExternalOutput").ap()
    decoder_layer(nc, aps, out)
    r = run_bass_kernel_spmd(nc, [arrays], core_ids=[0])
    return r.results[0]["out_x"].reshape(NB, TB, D)
```

```python
from contextlib import ExitStack

import numpy as np

import concourse.bass as bass
from concourse import mybir

F32 = mybir.dt.float32
F32R = mybir.dt.float32r
BF16 = mybir.dt.bfloat16
I32 = mybir.dt.int32
ALU = mybir.AluOpType
ACT = mybir.ActivationFunctionType
AX = mybir.AxisListType

P = 128
NB, TB, D = 2, 512, 128
T = NB * TB
QT, NT = TB // P, T // P
HD = 4
SH = D // HD
GH = 4
NG = SH // GH
STEPS = NB * NG
COMBOS = 8
Q_ROWS = [(0, 1, 3, 0), (3, 1, 2, 1), (5, 1, 1, 2)]
K_ROWS = [(0, 3, 2, 0), (5, 1, 1, 0), (1, 3, 2, 1), (2, 1, 1, 2)]
SHIFT_ROW, SHIFT_ROWS = 6, 2
HEAD_ROWS = HD * COMBOS
LAMBDA_INIT = 0.2
RMS_EPS, LN_EPS, EXPERT_EPS = 1e-5, 1e-5, 1e-12
XH, XD, KC, DE = 16, 64, 154, 96
XCOLS = XH * KC
XT = -(-XCOLS // P)
XPAD = XT * P
HPC = 3
XCH = -(-XH // HPC)
FOLD_RING = [6, 7, 5, 4]
FOLD_HEADS = [slice(HPC * c, min(HPC * (c + 1), XH)) for c in range(XCH)]
HPO = 7
XOB = -(-XH // HPO)
MAX_RING, SCORE_RING = [[3, 4, 2], [1, 2]], [2, 3, 4]
NORM_BANK = [2, 5]
VALUE_MAX = [3, 6, 9, 12, 15, 18]
TURN_AT, PROJ_AT, X1T_AT = 4, 6, 15
X2T_AT = 14
XTR_AT, XPROJ_AT = 6, 13
QT_CHUNKS = QT * XCH
V_GROUPS = -(-XT // 3)
NE, F = 8, 512
FT = F // P

MAX_PARTS = [[(3, 0)], [(2, 0), (0, 3 * P)], [(1, 0)]]
EXP_PARTS = [[(j, j, 1, j * P) for j in range(QT)], [(0, 1, 3, 0), (2, 3, 1, 3 * P)], [(1, 2, 2, 0)]]
EXP_WIDTH = [TB, TB, TB // 2]
UNITS = 3 * GH
HEAD_COLS = sum(EXP_WIDTH)
FOLD_AT = {u: NB * XCH - UNITS // 2 + u // 2 for u in range(1, UNITS, 2)}
V_AT = [{2: 0, 5: 1, 8: 2}, {5: 3, 7: 4, 9: 5}]
MAX_UNIT = 4
MAX_EARLY = UNITS - MAX_UNIT
V_BESIDE_MAX = {MAX_EARLY + 1 + 2 * n: 6 + n for n in range(NB * V_GROUPS - 6)}
VALUE_BLOCKS = sorted((j, t, k, TB * part + col) for part, blocks in enumerate(EXP_PARTS) for j, t, k, col in blocks)
VALUE_AT = [3, 4, 6, 7, 8, 10, 11]
ROWS_AT, OUT_AT = 3, 7


def segments(k):
    return [h for h in range(XH) if h * KC < (k + 1) * P and (h + 1) * KC > k * P]


OUTPUT_RUNS = []
for _k in range(XT):
    _banks = [h // HPO for h in segments(_k)]
    OUTPUT_RUNS.append([(_banks.index(c), _banks.count(c), c) for c in sorted(set(_banks))])
OUTPUT_LAST = [max(k for k in range(XT) if c in [h // HPO for h in segments(k)]) for c in range(XOB)]


def decoder_layer(nc, A, out):
    ctx = ExitStack()
    with ctx:
        def sb(name, shape, dt=F32):
            return ctx.enter_context(nc.sbuf_tensor(name, shape, dt))

        def sem(name):
            return ctx.enter_context(nc.semaphore(name))

        def cut(region, start, *dims):
            n = int(np.prod(dims))
            v = region[:, start:start + n]
            if len(dims) == 1:
                return v
            names = "abcd"[:len(dims)]
            sizes = {a: d for a, d in zip(names, dims)}
            return v.rearrange(f"p ({' '.join(names)}) -> p {' '.join(names)}", **sizes)

        columns = sb("columns", [P, 2 * P + 2 * NE * FT + NE + 1])
        ident = cut(columns, 0, P)
        w_proj = cut(columns, P, D)
        bi = cut(columns, 2 * P, NE, FT)
        bg = cut(columns, 2 * P + NE * FT, NE, FT)
        wr = cut(columns, 2 * P + 2 * NE * FT, NE)
        gamma_col = cut(columns, 2 * P + 2 * NE * FT + NE, 1)
        rows_bc = sb("rows_bc", [P, 4 * HD + 2 * NE + D])
        lambdas = cut(rows_bc, 0, 2, 2, HD)
        br_bc = cut(rows_bc, 4 * HD, NE)
        ranks = cut(rows_bc, 4 * HD + NE, NE)
        bo_bc = cut(rows_bc, 4 * HD + 2 * NE, D)
        identb = sb("identb", [P, P], BF16)
        maskb = sb("maskb", [P, P], BF16)
        x_tok = sb("x_tok", [P, NT, D])
        scaled_proj = sb("scaled_proj", [P, D])
        lam = sb("lam", [P, 8])
        small = sb("small", [P, 6, NT * XH])

        early = sb("early", [P, 5504])
        xT = cut(early, 0, T)
        parts = cut(early, T, 3 * T).bitcast(BF16).rearrange("p (o i t) -> p o i t", o=2, i=3)
        rest = cut(early, 4 * T, 2, TB)
        w_attn = cut(early, 5 * T, 3 * D)
        vblock = cut(early, 0, NB, XT, 130)
        w_raw1 = cut(early, 0, 2, F)
        xres = cut(early, 1024, 2, TB)
        weighted = cut(early, 2048, NT, D)
        acc = cut(early, 3072, NT, D)

        stacks = sb("stacks", [P, 4, 2, TB], BF16)
        indicator = stacks[0:32, :, :, :].rearrange("p a b c -> p (a b c)")[:, 0:XPAD]
        probs = sb("probs", [P, 10240])
        pr = [cut(probs, 5120 * n, GH, HEAD_COLS) for n in range(2)]
        zeros_b = cut(probs, 0, TB // 2).bitcast(BF16)
        kT = cut(probs, 5120, XH, NB * KC)
        xprobs = cut(probs, 0, XT, TB)
        hidden = [cut(probs, 2048 * n, FT, TB) for n in range(2)]
        gelu = cut(probs, 4096, FT, TB)
        gate = cut(probs, 6144, FT, TB)
        res = [cut(probs, 8192 + 1024 * n, NT, D) for n in range(2)]

        v_now = sb("v_now", [P, 2, QT, 2, 32])
        v_all = sb("v_all", [P, STEPS, QT, 16])
        w_raw0 = v_all[:, :, :, :].rearrange("p a b c -> p (a b c)").rearrange("p (a b) -> p a b", a=2)
        x2_both = sb("x2_both", [P, 2 * T])
        head_inv = sb("head_inv", [P, QT, GH])
        head_val = sb("head_val", [P, 2, QT, GH, 8])
        k_alone = x2_both[:, :].bitcast(BF16).rearrange("p (n g t) -> p n g t", n=2, g=GH)
        x2 = cut(x2_both, 0, NT, D)
        x2T = cut(x2_both, 1024, T)
        out_t = [sb(f"out_t{n}", [P, TB]) for n in range(2)]
        neg_max = sb("neg_max", [P, 2, GH, QT])
        neg_maxb = sb("neg_maxb", [P, 2, 2, GH, QT], BF16)
        max_rows = sb("max_rows", [32, 2, P], BF16)
        wqT = sb("wqT", [P, XH // 2, D])
        attn = wqT[:, :, :].rearrange("p a b -> p (a b)").rearrange("p (s i c) -> p s i c", s=STEPS, i=QT)
        outputs = sb("outputs", [P, XH * P + 2 * P])
        xattn = outputs[:, 0:2048].rearrange("p (n c) -> p n c", n=2)
        x2d = outputs[:, 0:NT * D].rearrange("p (n d) -> p n d", n=NT)
        turned = [outputs[:, T + TB * b:T + TB * (b + 1)] for b in range(NB)]
        attn_rms = outputs[:, 0:T].rearrange("p (n c) -> p n c", n=NT)
        ctx_pad = sb("ctx_pad", [DE + 1, NB, 2 * P + KC])
        wkv = sb("wkv", [P, XH * XD + XH * (XD + 1)])
        wk = wkv[0:DE, 0:XH * XD]
        wv = wkv[0:DE + 1, XH * XD:].rearrange("p (h d) -> p h d", h=XH)
        xattnT = wkv[:, 0:2048].rearrange("p (n k t) -> p n k t", n=2, k=XH // 2)
        wo = sb("wo", [P, XH // 2, D])
        x1 = sb("x1", [P, NT, D])
        ones_b = x1[:, 0:2, :].rearrange("p a b -> p (a b)").bitcast(BF16)
        fold = sb("fold", [P, 2, NB, XPAD], F32R)

        def fold_heads(part, b, c):
            v = fold[:, part, b, 0:XCOLS].rearrange("p (h s) -> p h s", h=XH)[:, FOLD_HEADS[c], :]
            return v, v.shape[1]

        x1T = sb("x1T", [P, 2, T], F32R)
        x2Tr = sb("x2Tr", [P, 2, T], F32R)
        w_split0 = sb("w_split0", [P, 2, 2, F], F32R)
        w_split1 = fold[:, 0, 0, 0:2048].rearrange("p (s m f) -> p s m f", s=2, m=2)
        w_raw, w_split = [w_raw0, w_raw1], [w_split0[:, :, :, :], w_split1]
        wo_e = sb("wo_e", [P, 2, FT, D])
        rows_e = sb("rows_e", [P, 2, 2, D])
        bgh = sb("bgh", [P, NE, FT])
        gamma_beta = sb("gamma_beta", [2 * NE, D])
        gatew = sb("gatew", [P, 8, NT, NE])
        coef = sb("coef", [P, NT, 2 * NE])
        coefT = [out_t[n][0:2 * NE, :] for n in range(2)]
        xneg = sb("xneg", [P, QT, XH])
        xnegb = sb("xnegb", [P, QT, 2, XH], BF16)
        xneg_rows = sb("xneg_rows", [32, NB, TB], BF16)
        rec = small[:, 5, 0:2 * XH].rearrange("p (n h) -> p n h", n=2)

        bank = [ctx.enter_context(nc.psum_tensor(f"bank{n}", [P, TB], F32)) for n in range(8)]
        scratch = nc.dram_tensor("scratch", [NB * D * COMBOS, 2, TB], BF16, kind="Internal").ap()

        S = {n: sem(n) for n in (
            "loaded_x", "loaded_x1", "loaded_cross", "loaded_wq", "loaded_wv", "loaded_const", "loaded_attn",
            "loaded_tok", "ind_loaded", "wo_loaded0", "wo_loaded1", "rows_loaded0", "rows_loaded1",
            "pads_ready", "consts_ready", "zeroed", "written0", "written1",
            "xproj_taken", "final_ready", "head_inv_done", "head_scaled", "head_done", "qk_ready", "v_ready",
            "v_copied", "high_ready", "parts_ready", "kt_ready", "kt_copied", "fold_ready", "fold_high",
            "fold_low", "max_ready", "max_taken", "neg_high", "neg_low", "rows_ready", "rows_copied",
            "st_ready", "exp_done", "masked", "v_staged", "pv_done", "ot_copied", "otr_done", "head_taken",
            "vb_ready", "vb_copied", "attn_ready", "attnT_ready", "attnT_copied", "proj_ready", "x1_ready",
            "x1T_ready", "x1T_high", "x1T_low", "dve_step", "lam_exp", "lam_in", "xmax_ready", "xmax_taken",
            "xneg_done", "xrows_ready", "xrows_copied", "xst_ready", "xexp_done", "xpv_ready", "xnorm_done",
            "xtr_ready", "xtr_copied", "xproj_ready", "x2_ready", "x2T_ready", "x2T_high", "x2T_low",
            "x2T_copied", "split_done", "up_ready", "gelu_done", "tanh_done", "hidden_done", "down_ready",
            "down_taken", "logits_ready", "gate_exp_in", "gate_exp", "xres_ready", "weighted_ready", "acc_done",
            "applied", "coef_ready", "coefT_ready", "coefT_copied", "corr_ready", "stored", "bgh_ready",
            "rows2_ready")}
        alone_loaded = [sem(f"alone_loaded{n}") for n in range(2)]
        stack_loaded = [sem(f"stack_loaded{n}") for n in range(4)]
        shift_loaded = [sem(f"shift_loaded{n}") for n in range(4)]
        w_loaded = [sem(f"w_loaded{n}") for n in range(2)]

        block = ctx.enter_context(nc.Block())

        def has(i, n):
            return not isinstance(i, int) or 0 <= n < STEPS

        def bodies(eng, body, first=2):
            for i in range(-2, first):
                body(i, i, 0)
            with eng.Fori(0, 3) as turn:
                for c in range(first, first + 4):
                    body(turn * 4 + c, c, turn)
            for i in range(first + 12, STEPS + 2):
                body(i, i, 0)

        def at_least(eng, semaphore, i, count):
            if isinstance(i, int) and count <= 0:
                return
            eng.wait_ge(semaphore, count)

        def turn_of(q, c, lag):
            return q + (c + lag) // 4

        @block.sync
        def _(sp):
            sp.dma_start(w_attn, A["w_attn"]).then_inc(S["loaded_x"], 16)
            sp.dma_start(xT[:, 0:TB], A["xT"][:, 0:TB]).then_inc(S["loaded_x"], 16)
            sp.dma_start(xT[:, TB:T], A["xT"][:, TB:T]).then_inc(S["loaded_x1"], 16)
            sp.dma_start(ctx_pad[0:DE, :, P:P + KC], A["ctxT"]).then_inc(S["loaded_cross"], 16)
            sp.dma_start(wk, A["wk"]).then_inc(S["loaded_cross"], 16)

            rows = scratch.rearrange("(b p c) o t -> b o p c t", b=NB, c=COMBOS)
            sp.wait_ge(S["consts_ready"], 2)

            def write(b, o, first, step, n, source, done):
                sp.dma_start(rows[b, o][:, first:first + step * (n - 1) + 1:step, :],
                             source.unsqueeze(1).broadcast_to([P, n, TB])).then_inc(done, 16)

            for b in range(NB):
                for o, source in enumerate((zeros_b, ones_b)):
                    write(b, o, SHIFT_ROW, 1, SHIFT_ROWS, source, S["written0"])

            sp.dma_start(wqT[:, :, :], A["wqT"].rearrange("(a p) d -> p a d", p=P)).then_inc(S["loaded_wq"], 16)

            def write_parts(b):
                sp.wait_ge(S["parts_ready"], 4 * (b + 1))
                for o, table in enumerate((Q_ROWS, K_ROWS)):
                    for first, step, n, part in table:
                        write(b, o, first, step, n, parts[:, o, part, b * TB:(b + 1) * TB], S[f"written{b}"])

            own_rows = GH * HEAD_ROWS
            writes = 16 * (len(Q_ROWS) + len(K_ROWS))

            def load_stacks(i, c, lag):
                sp.dma_start(stacks[:, (c + lag) % 4, :, :],
                             scratch[bass.ds((i + lag) * own_rows, own_rows), :, :]
                             ).then_inc(stack_loaded[(c + lag) % 4], 16)

            def load_alone(i, c):
                n = (c + 1) % 2
                for h in range(GH):
                    own = slice(HEAD_ROWS * h, HEAD_ROWS * (h + 1))
                    sp.dma_start(k_alone[own, n, h, :],
                                 scratch[bass.ds((i + 1) * own_rows + HEAD_ROWS * h, HEAD_ROWS), 1, :]
                                 ).then_inc(alone_loaded[n], 16)

            write_parts(0)
            sp.dma_start(identb[:, :], A["identb"]).then_inc(S["loaded_const"], 16)
            sp.dma_start(maskb[:, :], A["maskb"]).then_inc(S["loaded_const"], 16)
            sp.wait_ge(S["written0"], writes + 16 * 2 * NB)

            def body(i, c, q):
                if isinstance(i, int) and i == -2:
                    load_stacks(i, c, 2)
                if isinstance(i, int) and i == -1:
                    write_parts(1)
                    sp.dma_start(wv[0:DE, :, 0:XD],
                                 A["wv"].rearrange("p (h d) -> p h d", h=XH)).then_inc(S["loaded_wv"], 16)
                if isinstance(i, int) and i == 0:
                    sp.wait_ge(S["written1"], writes)
                if has(i, i + 1):
                    at_least(sp, S["st_ready"], i, UNITS * i)
                    if isinstance(i, int) and i == -1:
                        sp.wait_ge(S["zeroed"], 2)
                    load_alone(i, c)
                if has(i, i + 3):
                    load_stacks(i, c, 3)
                if has(i, i + 1):
                    sp.wait_ge(S["rows_copied"], i + 2)
                    b = (c + 1) % 4
                    for part in range(SHIFT_ROWS):
                        sp.dma_start(stacks[SHIFT_ROW + part:P:HEAD_ROWS, b, 0, :].rearrange("p (i t) -> p i t", i=QT),
                                     max_rows[16 * part:16 * part + 16, (c + 1) % 2, :]).then_inc(shift_loaded[b], 16)

            bodies(sp, body, first=1)

            sp.wait_ge(S["st_ready"], UNITS * STEPS)
            sp.dma_start(indicator, A["indicator"]).then_inc(S["ind_loaded"], 16)

            def load_raw(e):
                sp.dma_start(w_raw[e % 2], A["Wig"][e]).then_inc(w_loaded[e % 2], 16)

            def load_rest(e):
                n = e % 2
                if e >= 2:
                    sp.wait_ge(S["down_ready"], 2 * (e - 1))
                sp.dma_start(wo_e[:, n, :, :],
                             A["Wo_e"][e].rearrange("(k p) d -> p k d", p=P)).then_inc(S[f"wo_loaded{n}"], 16)
                if e >= 2:
                    sp.wait_ge(S["xres_ready"], 2 * (e - 1))
                    sp.wait_ge(S["weighted_ready"], e - 1)
                sp.dma_start(rows_e[:, n, :, :],
                             A["rows_e"][e:e + 1].partition_broadcast(P)).then_inc(S[f"rows_loaded{n}"], 16)

            sp.wait_ge(S["v_staged"], QT * STEPS)
            load_raw(0)
            load_rest(0)
            load_rest(1)
            sp.wait_ge(S["xpv_ready"], NT * XOB)
            load_raw(1)
            for e in range(2, NE):
                sp.wait_ge(S["split_done"], 4 * (e - 1))
                load_raw(e)
                load_rest(e)
            sp.wait_ge(S["stored"], 16 * 2)

        @block.scalar
        def _(act):
            for b in range(NB):
                for o in range(2):
                    act.wait_ge(S["qk_ready"], 2 * b + o + 1)
                    nc.scalar.activation(parts[:, o, 0, b * TB:(b + 1) * TB], bank[2 * b + o][:, :], ACT.Copy,
                                         scale=[0.25, 1.0][o]).then_inc(S["high_ready"], 1)
            act.dma_start(rows_bc[:, :], A["rows_bc"].partition_broadcast(P)).then_inc(S["loaded_attn"], 16)
            act.dma_start(columns[:, :], A["columns"]).then_inc(S["loaded_attn"], 16)
            for b in range(NB):
                act.wait_ge(S["v_ready"], b + 1)
                nc.scalar.copy(v_all[:, b * NG:(b + 1) * NG, :, :].rearrange("p g j d -> p j g d"),
                               bank[4 + b][:, :].rearrange("p (j g d) -> p j g d", j=QT, g=NG)).then_inc(S["v_copied"], 1)
            act.dma_start(x_tok[:, :, :], A["x"].rearrange("(n p) d -> p n d", p=P)).then_inc(S["loaded_tok"], 16)
            act.dma_start(wo[:, :, :], A["wo"].rearrange("(k p) d -> p k d", p=P)).then_inc(S["loaded_tok"], 16)
            act.dma_start(gamma_beta[:, :], A["gamma_beta"]).then_inc(S["loaded_tok"], 16)
            for n in range(XH // 2):
                act.wait_ge(S["kt_ready"], n + 1)
                if n == 0:
                    act.wait_ge(S["zeroed"], 1)
                for half in range(2):
                    own = slice(XD * half, XD * (half + 1))
                    nc.scalar.copy(kT[own, 2 * n + half, :], bank[FOLD_RING[n % 4]][own, 0:NB * KC]).then_inc(S["kt_copied"], 1)
            act.wait_ge(S["lam_in"], 1)
            nc.scalar.activation(lam[:, 2:4], lam[:, 0:2], ACT.Exp).then_inc(S["lam_exp"], 1)
            for n in range(NB * XCH):
                b, c = divmod(n, XCH)
                to, w = fold_heads(0, b, c)
                act.wait_ge(S["fold_ready"], n + 1)
                nc.scalar.activation(to, bank[FOLD_RING[n % 4]][:, 0:w * KC].rearrange("p (h s) -> p h s", h=w), ACT.Copy,
                                     scale=0.125).then_inc(S["fold_high"], 1)

            def copy_cross_v(n):
                b, g = divmod(n, V_GROUPS)
                w = min(3, XT - 3 * g)
                act.wait_ge(S["vb_ready"], n + 1)
                nc.scalar.copy(vblock[:, b, 3 * g:3 * g + w, :],
                               bank[n % 2][:, 0:130 * w].rearrange("p (k c) -> p k c", k=w)).then_inc(S["vb_copied"], 1)

            def copy_turned(b):
                act.wait_ge(S["attnT_ready"], b + 1)
                nc.scalar.copy(turned[b], bank[NORM_BANK[b]][:, :]).then_inc(S["attnT_copied"], 1)

            def copy_x1T(b):
                act.wait_ge(S["x1T_ready"], b + 1)
                nc.scalar.copy(x1T[:, 0, b * TB:(b + 1) * TB], bank[NORM_BANK[b]][:, :]).then_inc(S["x1T_high"], 1)

            def beside(i, u):
                if isinstance(i, int) and i >= STEPS - 2:
                    n = V_AT[i - STEPS + 2].get(u)
                    if n is not None:
                        copy_cross_v(n)
                    if (i, u) == (STEPS - 1, 1):
                        copy_turned(0)

            def take_out(i, c):
                act.wait_ge(S["pv_done"], i - 1)
                if not has(i, i):
                    act.wait_ge(S["otr_done"], i - 3)
                nc.scalar.copy(out_t[c % 2][:, :], bank[6][:, :]).then_inc(S["ot_copied"], 1)

            def body(i, c, q):
                if has(i, i):
                    at_least(act, S["pv_done"], i, i - 1)
                    for u in range(UNITS):
                        act.wait_ge(S["st_ready"], UNITS * i + u + 1)
                        h, part = divmod(u, 3)
                        w = EXP_WIDTH[part]
                        nc.scalar.activation(pr[c % 2][:, h, TB * part:TB * part + w], bank[3 + part][:, 0:w],
                                             ACT.Exp).then_inc(S["exp_done"], 1)
                        if u == 1 and has(i, i - 2):
                            take_out(i, c)
                        beside(i, u)
                elif has(i, i - 2):
                    take_out(i, c)
                    if i == STEPS:
                        copy_x1T(0)

            bodies(act, body)

            def copy_max_rows(b):
                act.wait_ge(S["xrows_ready"], b + 1)
                nc.scalar.copy(xneg_rows[:, b, :], bank[7][0:32, 0:TB // 2].bitcast(BF16)).then_inc(S["xrows_copied"], 1)

            def copy_x2T(b):
                act.wait_ge(S["x2T_ready"], b + 1)
                nc.scalar.copy(x2T[:, b * TB:(b + 1) * TB], bank[6 + b][:, :]).then_inc(S["x2T_copied"], 1)
                nc.scalar.copy(x2Tr[:, 0, b * TB:(b + 1) * TB], bank[6 + b][:, :]).then_inc(S["x2T_high"], 1)

            for n in V_BESIDE_MAX.values():
                copy_cross_v(n)
            for b in range(NB):
                copy_max_rows(b)
                if b:
                    act.wait_ge(S["xpv_ready"], QT * XOB * b)
                for k in range(XT):
                    act.wait_ge(S["xst_ready"], XT * b + k + 1)
                    nc.scalar.activation(xprobs[:, k, :], bank[SCORE_RING[(XT * b + k) % 3]][:, :],
                                         ACT.Exp).then_inc(S["xexp_done"], 1)
                    if b == 0 and k == TURN_AT:
                        copy_turned(1)
                    if b == 0 and k == X1T_AT:
                        copy_x1T(1)
                    if b == 1 and k == X2T_AT:
                        copy_x2T(0)
                for t in range(QT):
                    n = QT * b + t
                    for half in range(2):
                        act.wait_ge(S["xtr_ready"], 2 * n + half + 1)
                        nc.scalar.copy(xattnT[:, n % 2, 4 * half:4 * half + 4, :],
                                       bank[6 + half][:, :].rearrange("p (k t) -> p k t", k=4)).then_inc(S["xtr_copied"], 1)
            act.wait_ge(S["bgh_ready"], 1)
            act.wait_ge(S["loaded_attn"], 32)
            act.wait_ge(S["xpv_ready"], NT * XOB)

            def activations(e, half):
                for f in range(FT):
                    n = (2 * e + half) * FT + f
                    if n >= FT:
                        act.wait_ge(S["hidden_done"], n - FT + 1)
                    act.wait_ge(S["up_ready"], 2 * n + 1)
                    nc.scalar.activation(gelu[:, f, :], bank[2 * (f % 2)][:, :], ACT.Gelu,
                                         bias=bi[:, e, f:f + 1]).then_inc(S["gelu_done"], 1)
                    act.wait_ge(S["up_ready"], 2 * n + 2)
                    nc.scalar.activation(gate[:, f, :], bank[2 * (f % 2) + 1][:, :], ACT.Tanh,
                                         bias=bgh[:, e, f:f + 1], scale=0.5).then_inc(S["tanh_done"], 1)

            for e in range(NE):
                activations(e, 0)
                if e == 0:
                    copy_x2T(1)
                    act.wait_ge(S["gate_exp_in"], 1)
                    nc.scalar.activation(gatew[:, 1, :, :], gatew[:, 0, :, :], ACT.Exp).then_inc(S["gate_exp"], 1)
                activations(e, 1)
            for half in range(2):
                act.wait_ge(S["coefT_ready"], half + 1)
                nc.scalar.copy(coefT[half], bank[6 + half][0:2 * NE, :]).then_inc(S["coefT_copied"], 1)
            to = out.rearrange("(n p) d -> p n d", p=P)
            for half in range(2):
                own = slice(half * QT, (half + 1) * QT)
                act.wait_ge(S["final_ready"], half + 1)
                act.dma_start(to[:, own, :], weighted[:, own, :]).then_inc(S["stored"], 16)

        @block.gpsimd
        def _(pool):
            pads = [(ctx_pad[0:DE, :, 0:P], 0.0), (ctx_pad[0:DE, :, P + KC:], 0.0),
                    (wv[0:DE, :, XD:XD + 1], 0.0), (ctx_pad[DE:DE + 1, :, :], 0.0), (wv[DE:DE + 1, :, :], 0.0), (ctx_pad[DE:DE + 1, :, P:P + KC], 1.0),
                    (wv[DE:DE + 1, :, XD:XD + 1], 1.0), (v_now[:, :, :, :, :], 0.0), (v_now[:, :, :, :, 8:9], 1.0)]
            for n, (region, value) in enumerate(pads):
                nc.gpsimd.memset(region, value).then_inc(S["pads_ready"], 1)
                pool.wait_ge(S["pads_ready"], n + 1)
            for n, (region, value) in enumerate(((ones_b, 1.0), (zeros_b, 0.0))):
                nc.gpsimd.memset(region, value).then_inc(S["consts_ready"], 1)
                pool.wait_ge(S["consts_ready"], n + 1)
            pool.wait_ge(S["v_copied"], NB)

            def body(i, c, q):
                if not has(i, i):
                    return
                at_least(pool, S["pv_done"], i, i - 1)
                for h in range(GH):
                    pool.wait_ge(S["exp_done"], UNITS * i + 3 * h + 1)
                    nc.gpsimd.tensor_copy(v_now[:, c % 2, h, :, 0:8],
                                          v_all[:, bass.ds(i, 1), h, :].rearrange("p s (h d) -> p (s h) d", h=2)
                                          ).then_inc(S["v_staged"], 1)
                    blocks = pr[c % 2][:, h, 0:TB].rearrange("p (j t) -> p j t", j=QT)
                    nc.gpsimd.affine_select(out=blocks, in_=blocks, compare_op=ALU.is_ge, fill=0.0, base=0,
                                            pattern=[[0, QT], [1, P]], channel_multiplier=-1).then_inc(S["masked"], 1)

            bodies(pool, body)

            def split(e):
                n = e % 2
                pool.wait_ge(w_loaded[n], 16 * (e // 2 + 1))
                if e >= 2:
                    pool.wait_ge(S["up_ready"], 4 * FT * (e - 1))
                for m in range(2):
                    nc.gpsimd.tensor_copy(w_split[n][:, 0, m, :], w_raw[n][:, m, :]).then_inc(S["split_done"], 1)
                pool.wait_ge(S["split_done"], 4 * e + 2)
                for m in range(2):
                    nc.gpsimd.tensor_tensor(w_split[n][:, 1, m, :], w_raw[n][:, m, :],
                                            w_split[n][:, 0, m, :].bitcast(F32), ALU.subtract).then_inc(S["split_done"], 1)

            def residual(e, half):
                n = 2 * e + half
                if half == 0:
                    pool.wait_ge(S[f"rows_loaded{e % 2}"], 16 * (e // 2 + 1))
                    nc.gpsimd.tensor_tensor(rows_e[:, e % 2, 1, :], rows_e[:, e % 2, 1, :], rows_e[:, e % 2, 1, :],
                                            ALU.add).then_inc(S["rows2_ready"], 1)
                    pool.wait_ge(S["rows2_ready"], e + 1)
                if n >= 2:
                    pool.wait_ge(S["down_taken"], n - 1)
                nc.gpsimd.tensor_tensor(xres[:, half, :].rearrange("p (n d) -> p n d", n=QT),
                                        x2d[:, half * QT:(half + 1) * QT, :],
                                        rows_e[:, e % 2, 1:2, :].broadcast_to([P, QT, D]),
                                        ALU.add).then_inc(S["xres_ready"], 1)

            def accumulate(e):
                pool.wait_ge(S["weighted_ready"], e + 1)
                for half in range(2):
                    own = slice(half * QT, (half + 1) * QT)
                    if e:
                        pool.wait_ge(S["acc_done"], 2 * e - 1 + half)
                    nc.gpsimd.tensor_tensor(acc[:, own, :], x2[:, own, :] if e == 0 else acc[:, own, :],
                                            weighted[:, own, :], ALU.add).then_inc(S["acc_done"], 1)

            split(0)
            pool.wait_ge(S["xst_ready"], NB * XT)
            pool.wait_ge(S["xpv_ready"], NT * XOB)
            split(1)
            pool.wait_ge(S["applied"], 1)
            residual(0, 0)
            residual(0, 1)
            for e in range(NE):
                if e:
                    if e + 1 < NE:
                        split(e + 1)
                    residual(e, 1)
                    accumulate(e - 1)
                if e + 1 < NE:
                    residual(e + 1, 0)
        @block.vector
        def _(dve):
            count = [0]

            def link(ins):
                count[0] += 1
                ins.then_inc(S["dve_step"], 1)
                dve.wait_ge(S["dve_step"], count[0])

            def rsqrt(y, v, tmp):
                link(nc.vector.tensor_scalar(tmp.bitcast(I32), v.bitcast(I32), 1, None, ALU.logical_shift_right))
                link(nc.vector.tensor_scalar(y.bitcast(I32), tmp.bitcast(I32), -1.0, float(0x5F3759DF),
                                             ALU.mult, ALU.add))
                for _ in range(3):
                    link(nc.vector.tensor_tensor(tmp, y, y, ALU.mult))
                    link(nc.vector.scalar_tensor_tensor(out=tmp, in0=tmp, scalar=-0.5, in1=v, op0=ALU.mult, op1=ALU.mult))
                    link(nc.vector.scalar_tensor_tensor(out=y, in0=tmp, scalar=1.5, in1=y, op0=ALU.add, op1=ALU.mult))

            def statistics(src, tiles, mv, stats):
                for t in range(tiles):
                    ins = nc.vector.bn_stats(stats[:, t, :], src[:, t, :])
                    if t == tiles - 1:
                        link(ins)
                for t in range(tiles):
                    ins = nc.vector.bn_aggr(mv[:, t, :], stats[:, t, :])
                    if t == tiles - 1:
                        link(ins)

            def layer_norm(dst, src, tiles):
                stats = small[:, 0, 0:6 * tiles].rearrange("p (n c) -> p n c", c=6)
                mv = small[:, 1, 0:2 * tiles].rearrange("p (n c) -> p n c", c=2)
                v, y, tmp = small[:, 2, 0:tiles], small[:, 3, 0:tiles], small[:, 4, 0:tiles]
                statistics(src, tiles, mv, stats)
                link(nc.vector.tensor_scalar(v, mv[:, :, 1], LN_EPS, None, ALU.add))
                rsqrt(y, v, tmp)
                for t in range(tiles):
                    ins = nc.vector.tensor_scalar(dst[:, t, :], src[:, t, :], mv[:, t, 0:1], y[:, t:t + 1],
                                                  ALU.subtract, ALU.mult)
                return ins

            nc.vector.memset(kT, 0.0).then_inc(S["zeroed"], 1)
            for b in range(NB):
                for o in range(2):
                    own = slice(b * TB, (b + 1) * TB)
                    n = 2 * b + o
                    dve.wait_ge(S["high_ready"], n + 1)
                    link(nc.vector.scalar_tensor_tensor(out=rest[:, o, :], in0=bank[n][:, :], scalar=[0.25, 1.0][o],
                                                        in1=parts[:, o, 0, own], op0=ALU.mult, op1=ALU.subtract))
                    nc.vector.tensor_copy(parts[:, o, 1, own], rest[:, o, :]).then_inc(S["parts_ready"], 1)
                    dve.wait_ge(S["parts_ready"], 2 * n + 1)
                    nc.vector.tensor_tensor(parts[:, o, 2, own], rest[:, o, :], parts[:, o, 1, own],
                                            ALU.subtract).then_inc(S["parts_ready"], 1)
            dve.wait_ge(S["loaded_attn"], 32)
            nc.vector.tensor_scalar(bgh[:, :, :], bg, 0.5, None, ALU.mult).then_inc(S["bgh_ready"], 1)
            lv = lambdas
            link(nc.vector.tensor_tensor(small[:, 0, 0:8].rearrange("p (a d) -> p a d", a=2), lv[:, :, 0, :],
                                         lv[:, :, 1, :], ALU.mult))
            nc.vector.tensor_reduce(lam[:, 0:2], small[:, 0, 0:8].rearrange("p (a d) -> p a d", a=2), AX.X,
                                    ALU.add).then_inc(S["lam_in"], 1)
            link(nc.vector.tensor_scalar(scaled_proj[:, :], w_proj, gamma_col, 1.0 - LAMBDA_INIT,
                                         ALU.mult, ALU.mult))
            nc.vector.memset(x2_both[:, :], 0.0).then_inc(S["zeroed"], 1)
            dve.wait_ge(S["lam_exp"], 1)
            link(nc.vector.tensor_tensor(lam[:, 4:5], lam[:, 3:4], lam[:, 2:3], ALU.subtract))
            link(nc.vector.tensor_scalar(lam[:, 5:6], lam[:, 4:5], -LAMBDA_INIT, None, ALU.add))

            def fold_low(n):
                b, c = divmod(n, XCH)
                high, w = fold_heads(0, b, c)
                dve.wait_ge(S["fold_high"], n + 1)
                nc.vector.scalar_tensor_tensor(out=fold_heads(1, b, c)[0],
                                               in0=bank[FOLD_RING[n % 4]][:, 0:w * KC].rearrange("p (h s) -> p h s", h=w),
                                               scalar=0.125, in1=high.bitcast(F32), op0=ALU.mult,
                                               op1=ALU.subtract).then_inc(S["fold_low"], 1)

            link(nc.vector.memset(fold[:, :, :, XCOLS:XPAD].bitcast(F32), 0.0))
            for n in range(NB * XCH - len(FOLD_AT)):
                fold_low(n)

            def head_math(i, c, u):
                o = bank[7][:, :].rearrange("p (i g d) -> p i g d", i=QT, g=GH)
                val = head_val[:, c % 2, :, :, :]
                if u == OUT_AT + 1:
                    dve.wait_ge(S["otr_done"], i - 1)
                    nc.vector.reciprocal(head_inv[:, :, :], o[:, :, :, 8]).then_inc(S["head_inv_done"], 1)
                if u == OUT_AT + 2:
                    odd = head_inv[:, :, :].rearrange("p i (h two) -> p (i h) two", two=2)[:, :, 1:2]
                    dve.wait_ge(S["head_inv_done"], i - 1)
                    nc.vector.tensor_scalar(odd, odd, lam[:, 5:6], None, ALU.mult).then_inc(S["head_scaled"], 1)
                if u == OUT_AT + 3:
                    dve.wait_ge(S["head_scaled"], i - 1)
                    nc.vector.tensor_tensor(val.rearrange("p i g d -> p (i g) d"),
                                            o[:, :, :, 0:8].rearrange("p i g d -> p (i g) d"),
                                            head_inv[:, :, :].rearrange("p i g -> p (i g)").unsqueeze(2)
                                            .broadcast_to([P, QT * GH, 8]), ALU.mult).then_inc(S["head_taken"], 1)
                if u == OUT_AT + 4:
                    pair = val.rearrange("p i (h two) d -> p (i h) two d", two=2)
                    dve.wait_ge(S["head_taken"], i - 1)
                    nc.vector.tensor_tensor(
                        attn[:, bass.ds(i - 2, 1), :, :].rearrange("p s i (h d) -> p (s i h) d", h=2),
                        pair[:, :, 0, :], pair[:, :, 1, :], ALU.add).then_inc(S["head_done"], 1)

            def body(i, c, q):
                if has(i, i + 2):
                    at_least(dve, S["rows_ready"], i, i + 1)
                m = neg_max[:, c % 2, :, :]
                for u in range(UNITS):
                    h, part = divmod(u, 3)
                    if has(i, i + 2):
                        dve.wait_ge(S["max_ready"], UNITS * (i + 2) + u + 1)
                        for qt, col in MAX_PARTS[part]:
                            ins = nc.vector.tensor_reduce(m[:, h, qt:qt + 1], bank[part][:, col:col + (qt + 1) * P],
                                                          AX.X, ALU.max, negate=True)
                        ins.then_inc(S["max_taken"], 1)
                    if u == ROWS_AT + 1 and has(i, i + 1):
                        dve.wait_ge(S["rows_ready"], i + 2)
                        if has(i, i - 1):
                            dve.wait_ge(shift_loaded[(c - 1) % 4], 16 * SHIFT_ROWS * (turn_of(q, c, -1) + 1))
                        nc.vector.tensor_copy(max_rows[:, (c + 1) % 2, :],
                                              bank[7][0:32, 0:64].bitcast(BF16)).then_inc(S["rows_copied"], 1)
                    if isinstance(i, int) and i == -2 and u in FOLD_AT:
                        fold_low(FOLD_AT[u])
                    if isinstance(i, int):
                        if (i, u) == (STEPS - 2, 3):
                            head_rms(0)
                        if (i, u) == (STEPS - 1, 3):
                            first_norm(0)
                        if (i, u) == (STEPS, 2):
                            low_part(0)
                        if i == STEPS and u >= MAX_UNIT:
                            take_maximum(u - MAX_UNIT)
                    if has(i, i - 2):
                        head_math(i, c, u)
                if has(i, i + 2):
                    dve.wait_ge(S["max_taken"], UNITS * (i + 3))
                    nc.vector.tensor_copy(neg_maxb[:, c % 2, 0, :, :], m).then_inc(S["neg_high"], 1)
                    dve.wait_ge(S["neg_high"], i + 3)
                    nc.vector.tensor_tensor(neg_maxb[:, c % 2, 1, :, :], m, neg_maxb[:, c % 2, 0, :, :],
                                            ALU.subtract).then_inc(S["neg_low"], 1)

            def head_rms(b):
                dve.wait_ge(S["head_done"], NG * (b + 1))
                heads = NG * QT * 2
                own = slice(b * NG, (b + 1) * NG)
                ms, v, y, tmp = (small[:, n, 0:heads] for n in (1, 2, 3, 4))
                flat = wqT[:, :, :].rearrange("p a b -> p (a b)")[:, b * TB:(b + 1) * TB]
                link(nc.vector.tensor_tensor(turned[b], flat, flat, ALU.mult))
                link(nc.vector.tensor_reduce(ms, turned[b].rearrange("p (n d) -> p n d", d=8), AX.X, ALU.add))
                link(nc.vector.tensor_scalar(v, ms, 0.125, RMS_EPS, ALU.mult, ALU.add))
                rsqrt(y, v, tmp)
                roots = y.rearrange("p (s i h) -> p s i h", s=NG, i=QT)
                for t in range(QT):
                    ins = nc.vector.tensor_tensor(
                        attn_rms[:, b * QT + t, :].rearrange("p (g h d) -> p g h d", g=NG, h=2),
                        attn[:, own, t, :].rearrange("p g (h d) -> p g h d", h=2),
                        roots[:, :, t, :].unsqueeze(3).broadcast_to([P, NG, 2, 8]), ALU.mult)
                ins.then_inc(S["attn_ready"], 1)

            def first_norm(b):
                own = slice(b * QT, (b + 1) * QT)
                if b == 0:
                    dve.wait_ge(S["loaded_tok"], 48)
                dve.wait_ge(S["proj_ready"], b + 1)
                link(nc.vector.tensor_tensor(x1[:, own, :], bank[NORM_BANK[b]][:, :].rearrange("p (n d) -> p n d", n=QT),
                                             x_tok[:, own, :], ALU.add))
                layer_norm(x1[:, own, :], x1[:, own, :], QT).then_inc(S["x1_ready"], 1)

            def low_part(b):
                dve.wait_ge(S["x1T_high"], b + 1)
                nc.vector.tensor_tensor(x1T[:, 1, b * TB:(b + 1) * TB], bank[NORM_BANK[b]][:, :],
                                        x1T[:, 0, b * TB:(b + 1) * TB].bitcast(F32),
                                        ALU.subtract).then_inc(S["x1T_low"], 1)

            def take_maximum(m):
                n, c = divmod(m, XCH)
                t = n % QT
                w = min(HPC, XH - HPC * c)
                ring = MAX_RING[n // QT]
                if m == QT * XCH:
                    dve.wait_ge(S["xrows_ready"], 1)
                dve.wait_ge(S["xmax_ready"], m + 1)
                nc.vector.tensor_reduce(xneg[:, t, HPC * c:HPC * c + w],
                                        bank[ring[m % QT_CHUNKS % len(ring)]][:, 0:w * KC].rearrange("p (h s) -> p h s", s=KC),
                                        AX.X, ALU.max, negate=True).then_inc(S["xmax_taken"], 1)
                if c == XCH - 1:
                    dve.wait_ge(S["xmax_taken"], m + 1)
                    link(nc.vector.tensor_copy(xnegb[:, t, 0, :], xneg[:, t, :]))
                    nc.vector.tensor_tensor(xnegb[:, t, 1, :], xneg[:, t, :], xnegb[:, t, 0, :],
                                            ALU.subtract).then_inc(S["xneg_done"], 1)

            bodies(dve, body)

            for m in range(MAX_EARLY, QT_CHUNKS):
                take_maximum(m)
            head_rms(1)
            first_norm(1)
            dve.wait_ge(S["x1T_ready"], NB)
            for t in range(NT):
                ins = nc.vector.tensor_tensor(x1[:, t, :], x1[:, t, :], bo_bc, ALU.add)
            link(ins)
            low_part(1)

            for b in range(NB):
                for t in range(QT):
                    n = QT * b + t
                    if n >= 2:
                        dve.wait_ge(S["xtr_ready"], 2 * (n - 1))
                    for k in range(XT):
                        if k in OUTPUT_LAST:
                            c = OUTPUT_LAST.index(k)
                            w = min(HPO, XH - HPO * c)
                            own = slice(HPO * c, HPO * c + w)
                            dve.wait_ge(S["xpv_ready"], XOB * n + c + 1)
                            o = bank[3 + c][:, 0:65 * w].rearrange("p (h d) -> p h d", h=w)
                            link(nc.vector.reciprocal(rec[:, n % 2, own], o[:, :, 64]))
                            nc.vector.tensor_tensor(xattn[:, n % 2, :].rearrange("p (h d) -> p h d", h=XH)[:, own, :],
                                                    o[:, :, 0:64],
                                                    rec[:, n % 2, own].unsqueeze(2).broadcast_to([P, w, 64]),
                                                    ALU.mult).then_inc(S["xnorm_done"], 1)
                        if b == 0 and k in VALUE_MAX:
                            take_maximum(QT_CHUNKS + XCH * t + VALUE_MAX.index(k))
                own = slice(b * QT, (b + 1) * QT)
                dve.wait_ge(S["xproj_ready"], QT * (b + 1))
                nc.vector.tensor_tensor(x2[:, own, :], bank[b][:, :].rearrange("p (n d) -> p n d", n=QT),
                                        x1[:, own, :], ALU.add).then_inc(S["xproj_taken"], 1)
                dve.wait_ge(S["xproj_taken"], b + 1)
                layer_norm(x2[:, own, :], x2[:, own, :], QT).then_inc(S["x2_ready"], 1)
                dve.wait_ge(S["x2T_high"], b + 1)
                nc.vector.tensor_tensor(x2Tr[:, 1, b * TB:(b + 1) * TB], bank[6 + b][:, :],
                                        x2Tr[:, 0, b * TB:(b + 1) * TB].bitcast(F32),
                                        ALU.subtract).then_inc(S["x2T_low"], 1)
            G = [gatew[:, s, :, :] for s in range(8)]
            row = small[:, 5, :].rearrange("p (s n) -> p s n", s=NT * XH // NT)

            def over(v):
                return v.unsqueeze(2).broadcast_to([P, NT, NE])

            dve.wait_ge(S["logits_ready"], 1)
            link(nc.vector.tensor_tensor(G[2], bank[5][:, 0:NT * NE].rearrange("p (n e) -> p n e", n=NT),
                                         br_bc.unsqueeze(1).broadcast_to([P, NT, NE]), ALU.add))
            link(nc.vector.tensor_reduce(row[:, 0, :], G[2], AX.X, ALU.max))
            nc.vector.tensor_tensor(G[0], G[2], over(row[:, 0, :]), ALU.subtract).then_inc(S["gate_exp_in"], 1)

            def pick(probabilities, at, chosen, tmp):
                link(nc.vector.tensor_reduce(row[:, at, :], probabilities, AX.X, ALU.max))
                link(nc.vector.tensor_tensor(tmp, probabilities, over(row[:, at, :]), ALU.is_equal))
                link(nc.vector.tensor_tensor(tmp, tmp, ranks.unsqueeze(1).broadcast_to([P, NT, NE]), ALU.mult))
                link(nc.vector.tensor_reduce(row[:, 5, :], tmp, AX.X, ALU.max))
                link(nc.vector.tensor_tensor(chosen, tmp, over(row[:, 5, :]), ALU.is_equal))

            def top_two():
                link(nc.vector.tensor_reduce(row[:, 1, :], G[1], AX.X, ALU.add))
                link(nc.vector.reciprocal(row[:, 2, :], row[:, 1, :]))
                link(nc.vector.tensor_tensor(G[2], G[1], over(row[:, 2, :]), ALU.mult))

                pick(G[2], 3, G[3], G[4])
                link(nc.vector.scalar_tensor_tensor(out=G[5], in0=G[3], scalar=-2.0, in1=G[2], op0=ALU.mult, op1=ALU.add))
                pick(G[5], 4, G[6], G[4])
                link(nc.vector.tensor_tensor(row[:, 6, :], row[:, 3, :], row[:, 4, :], ALU.add))
                link(nc.vector.reciprocal(row[:, 7, :], row[:, 6, :]))
                link(nc.vector.tensor_tensor(G[3], G[3], G[6], ALU.add))
                link(nc.vector.tensor_tensor(G[3], G[3], G[2], ALU.mult))
                link(nc.vector.tensor_tensor(coef[:, :, NE:2 * NE], G[3], over(row[:, 7, :]), ALU.mult))

            stats = small[:, 0, 0:6 * NT].rearrange("p (n c) -> p n c", c=6)
            mv = small[:, 1, 0:2 * NT].rearrange("p (n c) -> p n c", c=2)
            v, y, tmp = small[:, 2, 0:NT], small[:, 3, 0:NT], small[:, 4, 0:NT]

            def gated(e, half, f):
                n = (2 * e + half) * FT + f
                if f == 0 and e:
                    dve.wait_ge(S["down_ready"], 2 * e - 1 + half)
                dve.wait_ge(S["tanh_done"], n + 1)
                nc.vector.scalar_tensor_tensor(out=hidden[half][:, f, :], in0=gate[:, f, :], scalar=1.0,
                                               in1=gelu[:, f, :], op0=ALU.add, op1=ALU.mult).then_inc(S["hidden_done"], 1)

            def take(e, half):
                n = 2 * e + half
                own = slice(half * QT, (half + 1) * QT)
                r = res[e % 2]
                dve.wait_ge(S["down_ready"], n + 1)
                dve.wait_ge(S["xres_ready"], n + 1)
                nc.vector.tensor_tensor(r[:, own, :], bank[4 + half][:, :].rearrange("p (n d) -> p n d", n=QT),
                                        xres[:, half, :].rearrange("p (n d) -> p n d", n=QT),
                                        ALU.add).then_inc(S["down_taken"], 1)
                dve.wait_ge(S["down_taken"], n + 1)
                statistics(r[:, own, :], QT, mv[:, own, :], stats[:, own, :])

            def root(own):
                link(nc.vector.tensor_scalar(v[:, own], mv[:, own, 1], 4 * EXPERT_EPS, None, ALU.add))
                rsqrt(y[:, own], v[:, own], tmp[:, own])

            def apply(e, own, done):
                link(nc.vector.tensor_tensor(row[:, 0, own], y[:, own], coef[:, own, NE + e], ALU.mult))
                nc.vector.scalar_tensor_tensor(out=coef[:, own, e], in0=mv[:, own, 0], scalar=-1.0, in1=row[:, 0, own],
                                               op0=ALU.mult, op1=ALU.mult).then_inc(S["coef_ready"], 1)
                if e:
                    dve.wait_ge(S["acc_done"], 2 * e)
                for t in range(own.start, own.stop):
                    ins = nc.vector.scalar_tensor_tensor(out=weighted[:, t, :], in0=res[e % 2][:, t, :],
                                                         scalar=row[:, 0, t:t + 1], in1=rows_e[:, e % 2, 0, :],
                                                         op0=ALU.mult, op1=ALU.mult)
                done(ins)

            def count_weighted(ins):
                ins.then_inc(S["weighted_ready"], 1)

            every = slice(0, NT)
            for f in range(FT):
                gated(0, 0, f)
            dve.wait_ge(S["xtr_ready"], 2 * NT)
            nc.vector.tensor_scalar(x2d, x2, 2.0, None, ALU.mult).then_inc(S["applied"], 1)
            dve.wait_ge(S["gate_exp"], 1)
            for e in range(NE):
                if e:
                    gated(e, 0, 0)
                    gated(e, 0, 1)
                    take(e - 1, 1)
                    gated(e, 0, 2)
                    gated(e, 0, 3)
                    root(every)
                gated(e, 1, 0)
                if e:
                    apply(e - 1, every, count_weighted)
                gated(e, 1, 1)
                if e == 0:
                    top_two()
                gated(e, 1, 2)
                if e < NE - 1:
                    take(e, 0)
                gated(e, 1, 3)
            halves = [slice(0, QT), slice(QT, NT)]
            e = NE - 1
            take(e, 0)
            for half, own in enumerate(halves):
                root(own)
                apply(e, own, link)
                link(nc.vector.tensor_tensor(weighted[:, own, :], weighted[:, own, :], acc[:, own, :], ALU.add))
                if half == 0:
                    take(e, 1)
            for half, own in enumerate(halves):
                dve.wait_ge(S["corr_ready"], half + 1)
                link(nc.vector.tensor_tensor(weighted[:, own, :], weighted[:, own, :],
                                             bank[4 + half][:, :].rearrange("p (n d) -> p n d", n=QT), ALU.add))
                layer_norm(weighted[:, own, :], weighted[:, own, :], QT).then_inc(S["final_ready"], 1)

        @block.tensor
        def _(pe):
            pe.wait_ge(S["loaded_x"], 32)
            for b in range(NB):
                if b:
                    pe.wait_ge(S["loaded_x1"], 16)
                for o in range(2):
                    nc.tensor.matmul(bank[2 * b + o][:, :], w_attn[:, o * D:(o + 1) * D], xT[:, b * TB:(b + 1) * TB],
                                     start=True, stop=True).then_inc(S["qk_ready"], 1)
            for b in range(NB):
                for j in range(QT):
                    n = b * QT + j
                    ins = nc.tensor.matmul(bank[4 + b][:, j * D:(j + 1) * D], xT[:, n * P:(n + 1) * P],
                                           w_attn[:, 2 * D:3 * D], start=True, stop=True)
                ins.then_inc(S["v_ready"], 1)
            pe.wait_ge(S["loaded_cross"], 16 * 2)
            for n in range(XH // 2):
                if n >= 4:
                    pe.wait_ge(S["kt_copied"], 2 * (n - 3))
                elif n == 2:
                    pe.wait_ge(S["v_copied"], NB)
                nc.tensor.matmul(bank[FOLD_RING[n % 4]][:, 0:NB * KC], wk[:, n * P:(n + 1) * P],
                                 ctx_pad[0:DE, :, P:P + KC], start=True, stop=True).then_inc(S["kt_ready"], 1)
            pe.wait_ge(S["kt_copied"], XH)
            pe.wait_ge(S["loaded_wq"], 16)

            def fold_chunk(n):
                b, c = divmod(n, XCH)
                if n >= 4:
                    pe.wait_ge(S["fold_low"], n - 3)
                for m, h in enumerate(range(XH)[FOLD_HEADS[c]]):
                    ins = nc.tensor.matmul(bank[FOLD_RING[n % 4]][:, m * KC:(m + 1) * KC],
                                           wqT[:, h // 2, :], kT[:, h, b * KC:(b + 1) * KC],
                                           start=True, stop=True)
                ins.then_inc(S["fold_ready"], 1)

            for n in range(NB * XCH - len(FOLD_AT)):
                fold_chunk(n)
            pe.wait_ge(S["loaded_const"], 16 * 2)
            pe.wait_ge(S["loaded_attn"], 32)
            pe.wait_ge(S["parts_ready"], 8)
            pe.wait_ge(S["v_copied"], NB)
            pe.wait_ge(S["pads_ready"], 9)

            def max_unit(i, c, q, u):
                b = (c + 2) % 4
                if u == 0:
                    pe.wait_ge(stack_loaded[b], 16 * (turn_of(q, c, 2) + 1))
                h, part = divmod(u, 3)
                own = slice(HEAD_ROWS * h, HEAD_ROWS * (h + 1))
                at_least(pe, S["max_taken"], i, UNITS * (i + 2) + u - 2)
                for n, (qt, col) in enumerate(MAX_PARTS[part]):
                    nc.tensor.matmul(bank[part][:, col:col + (qt + 1) * P], stacks[own, b, 0, qt * P:(qt + 1) * P],
                                     stacks[own, b, 1, 0:(qt + 1) * P], start=(n == 0), stop=False,
                                     skip_group_check=True)
                for qt, col in MAX_PARTS[part]:
                    ins = nc.tensor.matmul(bank[part][:, col + qt * P:col + (qt + 1) * P], identb[:, :], maskb[:, :],
                                           start=False, stop=True, skip_group_check=True)
                ins.then_inc(S["max_ready"], 1)

            def score_unit(i, c, q, u):
                b = c % 4
                if u == 0:
                    pe.wait_ge(shift_loaded[b], 16 * SHIFT_ROWS * (turn_of(q, c, 0) + 1))
                if u == 0 and isinstance(i, int) and i == 0:
                    pe.wait_ge(S["fold_low"], NB * XCH)
                if u == 0:
                    pe.wait_ge(alone_loaded[c % 2], 16 * GH * (2 * q + c // 2 + 1))
                h, part = divmod(u, 3)
                at_least(pe, S["exp_done"], i, UNITS * i + u - 2)
                for n, (j, t, k, col) in enumerate(EXP_PARTS[part]):
                    ins = nc.tensor.matmul(bank[3 + part][:, col:col + k * P], k_alone[:, c % 2, h, j * P:(j + 1) * P],
                                           stacks[:, b, 0, t * P:(t + k) * P], start=(n == 0), stop=True,
                                           skip_group_check=True)
                ins.then_inc(S["st_ready"], 1)

            def value_block(i, c, n):
                j, t, k, col = VALUE_BLOCKS[n]
                p = (c - 1) % 2
                if n == 0:
                    pe.wait_ge(S["masked"], GH * i)
                    pe.wait_ge(S["exp_done"], UNITS * i)
                    pe.wait_ge(S["v_staged"], QT * i)
                    at_least(pe, S["ot_copied"], i, i - 1)
                for h in range(GH):
                    ins = nc.tensor.matmul(bank[6][32 * h:32 * h + 32, t * P:(t + k) * P], v_now[:, p, j, h // 2, :],
                                           pr[p][:, h, col:col + k * P], start=(n == 0),
                                           stop=(n == len(VALUE_BLOCKS) - 1),
                                           skip_group_check=True)
                if n == len(VALUE_BLOCKS) - 1:
                    ins.then_inc(S["pv_done"], 1)

            def body(i, c, q):
                for u in range(UNITS):
                    if has(i, i + 2):
                        max_unit(i, c, q, u)
                    if u == ROWS_AT and has(i, i + 1):
                        pe.wait_ge(S["neg_low"], i + 2)
                        if isinstance(i, int) and i == -1:
                            pe.wait_ge(S["fold_low"], NB * XCH)
                        nc.tensor.transpose(bank[7][0:32, 0:64].bitcast(BF16),
                                            neg_maxb[:, (c + 1) % 2, :, :, :].rearrange("p a h i -> p (a h i)"),
                                            identb[:, :]).then_inc(S["rows_ready"], 1)
                    if has(i, i):
                        score_unit(i, c, q, u)
                    if has(i, i - 1) and u in VALUE_AT:
                        value_block(i, c, VALUE_AT.index(u))
                    beside(i, u)
                    if u == OUT_AT and has(i, i - 2):
                        pe.wait_ge(S["ot_copied"], i - 1)
                        if has(i, i + 1):
                            pe.wait_ge(S["rows_copied"], i + 2)
                        else:
                            pe.wait_ge(S["head_taken"], i - 2)
                        for t in range(QT):
                            ins = nc.tensor.transpose(bank[7][:, t * P:(t + 1) * P], out_t[c % 2][:, t * P:(t + 1) * P],
                                                      ident)
                        ins.then_inc(S["otr_done"], 1)

            def cross_value_group(n):
                b, g = divmod(n, V_GROUPS)
                if n == 0:
                    pe.wait_ge(S["loaded_wv"], 16)
                    pe.wait_ge(S["max_taken"], UNITS * STEPS)
                if n >= 2:
                    pe.wait_ge(S["vb_copied"], n - 1)
                to = bank[n % 2]
                for m, k in enumerate(range(3 * g, min(3 * g + 3, XT))):
                    for s in range(2):
                        h = segments(k)[0] + s
                        at = max(P + k * P - KC * h, 0)
                        h = min(h, XH - 1)
                        ins = nc.tensor.matmul(to[:, 130 * m + 65 * s:130 * m + 65 * s + 65],
                                               ctx_pad[:, b, at:at + P],
                                               wv[:, h, :], start=True, stop=True)
                ins.then_inc(S["vb_ready"], 1)

            def turn_outputs(b):
                pe.wait_ge(S["attn_ready"], b + 1)
                if b:
                    pe.wait_ge(S["exp_done"], UNITS * STEPS)
                for t in range(QT):
                    ins = nc.tensor.transpose(bank[NORM_BANK[b]][:, t * P:(t + 1) * P], attn_rms[:, b * QT + t, :], ident)
                ins.then_inc(S["attnT_ready"], 1)

            def project(b):
                pe.wait_ge(S["attnT_copied"], b + 1)
                for t in range(QT):
                    ins = nc.tensor.matmul(bank[NORM_BANK[b]][:, t * D:(t + 1) * D], turned[b][:, t * P:(t + 1) * P],
                                           scaled_proj[:, :], start=True, stop=True)
                ins.then_inc(S["proj_ready"], 1)

            def turn_x1(b):
                pe.wait_ge(S["x1_ready"], b + 1)
                for t in range(QT):
                    ins = nc.tensor.transpose(bank[NORM_BANK[b]][:, t * P:(t + 1) * P], x1[:, b * QT + t, :], ident)
                ins.then_inc(S["x1T_ready"], 1)

            def max_chunk(m):
                n, c = divmod(m, XCH)
                w = min(HPC, XH - HPC * c) * KC
                ring = MAX_RING[n // QT]
                if m % QT_CHUNKS >= len(ring):
                    pe.wait_ge(S["xmax_taken"], m - len(ring) + 1)
                elif m == QT_CHUNKS:
                    pe.wait_ge(S["xmax_taken"], m)
                elif m == 0:
                    pe.wait_ge(S["exp_done"], UNITS * STEPS)
                    pe.wait_ge(S["x1T_low"], 1)
                nc.tensor.matmul(bank[ring[m % QT_CHUNKS % len(ring)]][:, 0:w], x1T[:, 0, n * P:(n + 1) * P],
                                 fold[:, 0, n // QT, HPC * KC * c:HPC * KC * c + w],
                                 start=True, stop=True).then_inc(S["xmax_ready"], 1)

            def beside(i, u):
                if not isinstance(i, int):
                    return
                if i == -2 and u in FOLD_AT:
                    fold_chunk(FOLD_AT[u])
                if i == STEPS - 1 and u == 1:
                    turn_outputs(0)
                if i == STEPS - 1 and u == 3:
                    project(0)
                if i in (STEPS - 2, STEPS - 1) and u in V_AT[i - STEPS + 2]:
                    cross_value_group(V_AT[i - STEPS + 2][u])
                if i == STEPS and u == 1:
                    turn_x1(0)
                if i == STEPS and u >= MAX_UNIT:
                    max_chunk(u - MAX_UNIT)

            bodies(pe, body)


            def max_rows_of(b):
                pe.wait_ge(S["xneg_done"], QT * (b + 1))
                if b == 0:
                    pe.wait_ge(S["head_taken"], STEPS)
                else:
                    pe.wait_ge(S["xtr_copied"], 2 * QT)
                for t in range(QT):
                    ins = nc.tensor.transpose(bank[7][0:32, t * P // 2:(t + 1) * P // 2].bitcast(BF16),
                                              xnegb[:, t, :, :].rearrange("p a h -> p (a h)"), identb[:, :])
                ins.then_inc(S["xrows_ready"], 1)

            for m in range(MAX_EARLY, QT_CHUNKS):
                max_chunk(m)
                if m in V_BESIDE_MAX:
                    cross_value_group(V_BESIDE_MAX[m])
            max_rows_of(0)
            pe.wait_ge(S["ind_loaded"], 16)

            def cross_transposes(n):
                if n % QT == 0:
                    pe.wait_ge(S["xrows_copied"], n // QT + 1)
                for half in range(2):
                    pe.wait_ge(S["xnorm_done"], XOB * (n + 1))
                    if n:
                        pe.wait_ge(S["xtr_copied"], 2 * n - 1 + half)
                    if n == QT:
                        pe.wait_ge(S["x2T_low"], 1)
                    for k in range(4):
                        ins = nc.tensor.transpose(bank[6 + half][:, k * P:(k + 1) * P],
                                                  xattn[:, n % 2, (4 * half + k) * P:(4 * half + k + 1) * P], ident)
                    ins.then_inc(S["xtr_ready"], 1)

            def cross_projection(n):
                pe.wait_ge(S["xtr_copied"], 2 * n + 2)
                to = bank[n // QT]
                for k in range(XH // 2):
                    ins = nc.tensor.matmul(to[:, (n % QT) * D:(n % QT + 1) * D], xattnT[:, n % 2, k, :], wo[:, k, :],
                                           start=(k == 0), stop=(k == XH // 2 - 1))
                ins.then_inc(S["xproj_ready"], 1)

            def turn_x2(b):
                pe.wait_ge(S["x2_ready"], b + 1)
                for t in range(QT):
                    ins = nc.tensor.transpose(bank[6 + b][:, t * P:(t + 1) * P], x2[:, QT * b + t, :], ident)
                ins.then_inc(S["x2T_ready"], 1)

            for b in range(NB):
                for k in range(XT):
                    m = XT * b + k
                    if k == 0:
                        pe.wait_ge(S["xrows_copied"], b + 1)
                        pe.wait_ge(S["x1T_low"], b + 1)
                        if b:
                            pe.wait_ge(S["xnorm_done"], QT * XOB * b)
                        else:
                            pe.wait_ge(S["exp_done"], UNITS * STEPS)
                    if m >= 3:
                        pe.wait_ge(S["xexp_done"], m - 2)
                    to = bank[SCORE_RING[m % 3]][:, :]
                    cols = slice(k * P, (k + 1) * P)
                    tok = slice(b * TB, (b + 1) * TB)
                    nc.tensor.matmul(to, fold[:, 0, b, cols], x1T[:, 0, tok], start=True, stop=False)
                    nc.tensor.matmul(to, fold[:, 0, b, cols], x1T[:, 1, tok], start=False, stop=False)
                    nc.tensor.matmul(to, fold[:, 1, b, cols], x1T[:, 0, tok], start=False, stop=False)
                    nc.tensor.matmul(to, indicator[:, cols], xneg_rows[:, b, :], start=False,
                                     stop=True).then_inc(S["xst_ready"], 1)
                    if b == 0 and k == TURN_AT:
                        turn_outputs(1)
                    if b == 0 and k == PROJ_AT:
                        project(1)
                    if b == 0 and k == X1T_AT:
                        turn_x1(1)
                    if b == 1 and k == X2T_AT:
                        turn_x2(0)
                if b == 0:
                    pe.wait_ge(S["vb_copied"], NB * V_GROUPS)
                    pe.wait_ge(S["x1T_low"], NB)
                pe.wait_ge(S["xexp_done"], XT * (b + 1))
                for t in range(QT):
                    n = QT * b + t
                    started, done = [], OUTPUT_LAST
                    for k in range(XT):
                        for first, heads, c in OUTPUT_RUNS[k]:
                            if c not in started and n:
                                pe.wait_ge(S["xnorm_done"], XOB * (n - 1) + c + 1)
                            at = 65 * (segments(k)[first] % HPO)
                            ins = nc.tensor.matmul(bank[3 + c][:, at:at + 65 * heads],
                                                   xprobs[:, k, t * P:(t + 1) * P],
                                                   vblock[:, b, k, 65 * first:65 * (first + heads)],
                                                   start=c not in started, stop=k == done[c], skip_group_check=True)
                            started.append(c)
                            if k == done[c]:
                                ins.then_inc(S["xpv_ready"], 1)
                        if b == 0 and k in VALUE_MAX:
                            max_chunk(QT_CHUNKS + XCH * t + VALUE_MAX.index(k))
                        if t and k == XTR_AT:
                            cross_transposes(n - 1)
                        if t and k == XPROJ_AT:
                            cross_projection(n - 1)
                cross_transposes(QT * b + QT - 1)
                cross_projection(QT * b + QT - 1)
                if b == 0:
                    max_rows_of(1)
            def up(e, half):
                tok = slice(half * TB, (half + 1) * TB)
                if half == 0:
                    pe.wait_ge(S["split_done"], 4 * (e + 1))
                for f in range(FT):
                    cols = slice(f * P, (f + 1) * P)
                    n = (2 * e + half) * FT + f
                    for m in range(2):
                        to = bank[2 * (f % 2) + m][:, :]
                        if n >= 2:
                            pe.wait_ge([S["gelu_done"], S["tanh_done"]][m], n - 1)
                        elif n == 0:
                            pe.wait_ge(S["xproj_taken"], m + 1)
                        w = w_split[e % 2]
                        nc.tensor.matmul(to, w[:, 0, m, cols], x2Tr[:, 0, tok], start=True, stop=False)
                        nc.tensor.matmul(to, w[:, 0, m, cols], x2Tr[:, 1, tok], start=False, stop=False)
                        nc.tensor.matmul(to, w[:, 1, m, cols], x2Tr[:, 0, tok], start=False,
                                         stop=True).then_inc(S["up_ready"], 1)

            def down(e, half):
                n = 2 * e + half
                if n >= 2:
                    pe.wait_ge(S["down_taken"], n - 1)
                else:
                    pe.wait_ge(S["gate_exp_in"], 1)
                pe.wait_ge(S[f"wo_loaded{e % 2}"], 16 * (e // 2 + 1))
                pe.wait_ge(S["hidden_done"], FT * (n + 1))
                for t in range(QT):
                    for f in range(FT):
                        ins = nc.tensor.matmul(bank[4 + half][:, t * D:(t + 1) * D], hidden[half][:, f, t * P:(t + 1) * P],
                                               wo_e[:, e % 2, f, :], start=(f == 0), stop=(f == FT - 1))
                ins.then_inc(S["down_ready"], 1)

            pe.wait_ge(S["xnorm_done"], NT * XOB)
            pe.wait_ge(S["x2T_low"], 1)
            for e in range(NE):
                up(e, 0)
                if e:
                    down(e - 1, 1)
                else:
                    turn_x2(1)
                    pe.wait_ge(S["x2T_copied"], NB)
                    pe.wait_ge(S["xnorm_done"], NT * XOB)
                    for n in range(NT):
                        ins = nc.tensor.matmul(bank[5][:, n * NE:(n + 1) * NE], x2T[:, n * P:(n + 1) * P], wr,
                                               start=True, stop=True)
                    ins.then_inc(S["logits_ready"], 1)
                    pe.wait_ge(S["x2T_low"], NB)
                up(e, 1)
                down(e, 0)
            down(NE - 1, 1)
            for half in range(2):
                pe.wait_ge(S["coef_ready"], NE + half)
                for t in range(QT):
                    ins = nc.tensor.transpose(bank[6 + half][0:2 * NE, t * P:(t + 1) * P], coef[:, half * QT + t, :], ident)
                ins.then_inc(S["coefT_ready"], 1)
                pe.wait_ge(S["coefT_copied"], half + 1)
                pe.wait_ge(S["down_taken"], 2 * NE - 1 + half)
                for t in range(QT):
                    ins = nc.tensor.matmul(bank[4 + half][:, t * D:(t + 1) * D], coefT[half][:, t * P:(t + 1) * P],
                                           gamma_beta[:, :], start=True, stop=True)
                ins.then_inc(S["corr_ready"], 1)


def kernel(**inputs):
    import concourse.bacc as bacc
    from concourse.bass_utils import run_bass_kernel_spmd
    import ml_dtypes

    a = {k: np.asarray(v) for k, v in inputs.items()}
    pre, xa, ff = "L0_attn_", "L0_xattn_", "L0_ffn_"
    x = a["x"].reshape(T, D)
    row = np.arange(XPAD)
    head = np.arange(XH)[:, None]
    hot = ((row // KC == head) & (row < XCOLS))
    layout = {
        "x": x, "xT": x.T,
        "columns": np.concatenate([
            np.eye(P, dtype=np.float32), a[pre + "w_proj"],
            *(a[ff + n].reshape(NE, FT, P).transpose(2, 0, 1).reshape(P, NE * FT) for n in ("bi", "bg")),
            a[ff + "Wr"], np.tile(a[pre + "gamma"], D // (2 * HD))[:, None]], axis=1),
        "rows_bc": np.concatenate([a[pre + "lambda_" + n] for n in ("q1", "k1", "q2", "k2")] + [
            a[ff + "br"], np.arange(NE, 0, -1, dtype=np.float32), a[xa + "bo"]])[None],
        "ctxT": a["ctx_768"].transpose(2, 0, 1),
        "w_attn": a[pre + "w_attn"],
        "wk": a[xa + "Wk"], "wv": a[xa + "Wv"], "wqT": a[xa + "Wq"].T, "wo": a[xa + "Wo"],
        "Wig": np.stack([a[ff + "Wi"], a[ff + "Wg"]], axis=2), "Wo_e": a[ff + "Wo"],
        "rows_e": np.stack([a[ff + "gamma"], a[ff + "bo"]], axis=1),
        "gamma_beta": np.concatenate([a[ff + "gamma"], a[ff + "beta"]]),
        "identb": np.eye(P).astype(ml_dtypes.bfloat16),
        "maskb": np.triu(np.full((P, P), -3e38), 1).astype(ml_dtypes.bfloat16),
        "indicator": np.concatenate([hot, hot]).astype(ml_dtypes.bfloat16),
    }
    nc = bacc.Bacc("TRN2", target_bir_lowering=False, num_devices=1)
    arrays, aps = {}, {}
    for name, v in layout.items():
        v = np.ascontiguousarray(v)
        arrays[f"in_{name}"] = v
        aps[name] = nc.dram_tensor(f"in_{name}", v.shape, mybir.dt.from_np(v.dtype), kind="ExternalInput").ap()
    out = nc.dram_tensor("out_x", [T, D], F32, kind="ExternalOutput").ap()
    decoder_layer(nc, aps, out)
    r = run_bass_kernel_spmd(nc, [arrays], core_ids=[0])
    return r.results[0]["out_x"].reshape(NB, TB, D)
```
